# Optimizing a Trainium2 kernel written in Bass

```python
import numpy as np
import jax
import jax.numpy as jnp

def _softmax(x, axis=-1):
    return jax.nn.softmax(x, axis=axis)

def _gelu(x):
    return jax.nn.gelu(x, approximate=True)

def _silu(x):
    return jax.nn.silu(x)

def _sigmoid(x):
    return jax.nn.sigmoid(x)

def _layernorm(x, axis=-1, eps=1e-05):
    m = jnp.mean(x, axis=axis, keepdims=True)
    v = jnp.var(x, axis=axis, keepdims=True)
    return (x - m) / jnp.sqrt(v + eps)

def _scatter_add(tgt, idx, src, axis=0):
    return tgt.at[idx].add(src)

def _segment_sum(src, seg, n):
    return jax.ops.segment_sum(src, seg, n)
kernel_name = 'mk_flamingo_gated_d4_seqx_r8_903d22'

def setup_inputs(seed: int=0):
    np.random.seed(seed)
    _w = jnp.asarray

    def _rec_inputs():
        import jax
        import jax.numpy as jnp
        _rk = jax.random.key(seed)
        x = 7.22e-05 + 1 * jax.random.normal(jax.random.fold_in(_rk, 1), (32, 128, 128), jnp.float32)
        _lenS = 128 - jax.random.randint(jax.random.fold_in(_rk, 7), (32,), 0, max(1, 128 // 4) + 1, jnp.int32)
        _lenS2 = 128 - jax.random.randint(jax.random.fold_in(_rk, 8), (32,), 0, max(1, 128 // 4) + 1, jnp.int32)
        itok_S_0_31 = jax.random.randint(jax.random.fold_in(_rk, 11), (128,), 0, 32, jnp.int32)
        _ctx_1024P = jax.random.normal(jax.random.fold_in(_rk, 12), (32, 16, 128), jnp.float32)
        _ctx_1024c = jax.random.dirichlet(jax.random.fold_in(_rk, 512), 0.3 * jnp.ones((16,), jnp.float32), (32, 128))
        _ctx_1024t = jnp.einsum('bsk,bkd->bsd', _ctx_1024c, _ctx_1024P)
        _ctx_1024t = _ctx_1024t * jax.lax.rsqrt(jnp.mean(jnp.square(_ctx_1024t)) + 1e-12) * 0.953939
        ctx_1024 = 0.000121155 + 1.00018 * (_ctx_1024t + 0.3 * jax.random.normal(jax.random.fold_in(_rk, 612), (32, 128, 128), jnp.float32))
        _validS = jnp.arange(128)[None, :] < _lenS[:, None]
        _validS2 = jnp.arange(128)[None, :] < _lenS2[:, None]
        _causal = jnp.tril(jnp.ones((128, 128), dtype=bool))
        mask_1x1xSxS2_ik0 = jnp.where(jnp.broadcast_to(_validS2[0:1, None, None, :], (1, 1, 128, 128)), 0, 1).astype(jnp.int32)
        _g = jax.random.normal(jax.random.fold_in(_rk, 9001), (2, 4), jnp.float32)
        _g = jnp.sign(_g) * jnp.maximum(jnp.abs(_g), 1.0) + (_g == 0) * 1.0
        g_xattn = _g[0]
        g_ffn = _g[1]
        return (x, itok_S_0_31, ctx_1024, mask_1x1xSxS2_ik0, g_xattn, g_ffn)
    x, itok_S_0_31, ctx_1024, mask_1x1xSxS2_ik0, g_xattn, g_ffn = _rec_inputs()

    def _L0_xattn_setup():
        import jax, jax.numpy as jnp
        import numpy as np
        NUM_LAYERS = 32
        IN_SIZE = 128
        OUT_SIZE = 128
        B, S = (32, 32)
        key = jax.random.key(seed)
        k1, k2, k3 = jax.random.split(key, 3)
        x = jax.random.normal(k1, (B, S, IN_SIZE), dtype=jnp.float32)
        layer_idx = jax.random.randint(k2, (S,), 0, NUM_LAYERS, dtype=jnp.int32)
        weight = jax.random.normal(k3, (NUM_LAYERS, OUT_SIZE, IN_SIZE), dtype=jnp.float32)
        return {'x': x, 'layer_idx': layer_idx, 'weight': weight}
    _L0_xattn_all = _L0_xattn_setup()
    _L0_xattn_in = {k: v for k, v in _L0_xattn_all.items() if k in ()}
    del _L0_xattn_all

    def _L0_ffn_setup():
        import jax, jax.numpy as jnp
        import numpy as np
        T, Z, D_DIM = (8, 256, 128)
        N_EXP, P_SLOT, H = (64, 32, 128)
        LN_EPS = 1e-05
        key = jax.random.key(seed)
        k = jax.random.split(key, 5)
        s = 0.02
        return {'x': jax.random.normal(k[0], (T, Z, D_DIM), dtype=jnp.float32), 'phi_w': jax.random.normal(k[1], (N_EXP * P_SLOT, D_DIM), dtype=jnp.float32) * s, 'phi_b': jax.random.normal(k[2], (N_EXP * P_SLOT,), dtype=jnp.float32) * s, 'expert_w': jax.random.normal(k[3], (N_EXP, D_DIM, H), dtype=jnp.float32) * s, 'expert_b': jax.random.normal(k[4], (N_EXP, H), dtype=jnp.float32) * s}
    _L0_ffn_all = _L0_ffn_setup()
    _L0_ffn_in = {k: v for k, v in _L0_ffn_all.items() if k in ('phi_w', 'phi_b', 'expert_w', 'expert_b')}
    del _L0_ffn_all

    def _L1_xattn_setup():
        import jax, jax.numpy as jnp
        import numpy as np
        import math
        B, S, D, H = (4, 256, 128, 16)
        HD = D // H

        def _rope_tables(seq_len, dim, base=10000.0):
            half = dim // 2
            inv_freq = 1.0 / base ** (jnp.arange(half, dtype=jnp.float32) / half)
            angles = jnp.arange(seq_len, dtype=jnp.float32)[:, None] * inv_freq[None, :]
            return (jnp.cos(angles), jnp.sin(angles))

        def _apply_rope(x, cos, sin):
            half = x.shape[-1] // 2
            x1, x2 = (x[..., :half], x[..., half:])
            c = cos[None, None, :, :]
            s = sin[None, None, :, :]
            return jnp.concatenate([x1 * c - x2 * s, x1 * s + x2 * c], axis=-1)
        key = jax.random.key(seed)
        ks = jax.random.split(key, 7)
        sc = 1.0 / math.sqrt(D)
        return {'Q': jax.random.normal(ks[0], (B, S, D), jnp.float32), 'K': jax.random.normal(ks[1], (B, S, D), jnp.float32), 'V': jax.random.normal(ks[2], (B, S, D), jnp.float32), 'Wq': jax.random.normal(ks[3], (D, D), jnp.float32) * sc, 'bq': jnp.zeros((D,), jnp.float32), 'Wk': jax.random.normal(ks[4], (D, D), jnp.float32) * sc, 'bk': jnp.zeros((D,), jnp.float32), 'Wv': jax.random.normal(ks[5], (D, D), jnp.float32) * sc, 'bv': jnp.zeros((D,), jnp.float32), 'Wo': jax.random.normal(ks[6], (D, D), jnp.float32) * sc, 'bo': jnp.zeros((D,), jnp.float32)}
    _L1_xattn_all = _L1_xattn_setup()
    _L1_xattn_in = {k: v for k, v in _L1_xattn_all.items() if k in ('Wq', 'bq', 'Wk', 'bk', 'Wv', 'bv', 'Wo', 'bo')}
    del _L1_xattn_all

    def _L1_ffn_setup():
        import jax, jax.numpy as jnp
        import numpy as np
        TOP_K = 2
        key = jax.random.key(seed)
        ks = jax.random.split(key, 8)
        B, S, D = (2, 256, 128)
        N_r, N_s = (16, 2)
        u = jax.random.normal(ks[0], (B, S, D), dtype=jnp.float32)
        centroids = jax.random.normal(ks[1], (N_r, D), dtype=jnp.float32)
        expert_biases = jnp.zeros((N_r,), dtype=jnp.float32)
        Wr = jax.random.normal(ks[2], (N_r, D, D), dtype=jnp.float32) * (1.0 / np.sqrt(D))
        br = jax.random.normal(ks[3], (N_r, D), dtype=jnp.float32) * 0.01
        Ws = jax.random.normal(ks[4], (N_s, D, D), dtype=jnp.float32) * (1.0 / np.sqrt(D))
        bs = jax.random.normal(ks[5], (N_s, D), dtype=jnp.float32) * 0.01
        return {'u': u, 'centroids': centroids, 'expert_biases': expert_biases, 'Wr': Wr, 'br': br, 'Ws': Ws, 'bs': bs}
    _L1_ffn_all = _L1_ffn_setup()
    _L1_ffn_in = {k: v for k, v in _L1_ffn_all.items() if k in ('centroids', 'expert_biases', 'Wr', 'br', 'Ws', 'bs')}
    del _L1_ffn_all

    def _L2_xattn_setup():
        import jax, jax.numpy as jnp
        import numpy as np
        HEADS_COUNT = 16
        HIDDEN_SIZE = 128
        SCALE = float(np.sqrt(HIDDEN_SIZE // HEADS_COUNT))
        B, S, D = (4, 512, 128)
        key = jax.random.key(seed)
        kq, kk, kv = jax.random.split(key, 3)
        query = jax.random.normal(kq, (B, S, D), dtype=jnp.float32)
        key_t = jax.random.normal(kk, (B, S, D), dtype=jnp.float32)
        value = jax.random.normal(kv, (B, S, D), dtype=jnp.float32)
        return {'query': query, 'key': key_t, 'value': value}
    _L2_xattn_all = _L2_xattn_setup()
    _L2_xattn_in = {k: v for k, v in _L2_xattn_all.items() if k in ()}
    del _L2_xattn_all

    def _L2_ffn_setup():
        import jax, jax.numpy as jnp
        import numpy as np
        NUM_EXPERTS = 8
        EXPERT_CAPACITY = 2.0
        key = jax.random.key(seed)
        k1, k2, k3, k4 = jax.random.split(key, 4)
        B, T, C, H, E = (4, 512, 128, 512, NUM_EXPERTS)
        x = jax.random.normal(k1, (B, T, C), jnp.float32)
        gate_w = jax.random.normal(k2, (C, E), jnp.float32) * 0.02
        w1 = jax.random.normal(k3, (E, C, H), jnp.float32) * 0.02
        w2 = jax.random.normal(k4, (E, H, C), jnp.float32) * 0.02
        return {'x': x, 'gate_w': gate_w, 'w1': w1, 'w2': w2}
    _L2_ffn_all = _L2_ffn_setup()
    _L2_ffn_in = {k: v for k, v in _L2_ffn_all.items() if k in ('gate_w', 'w1', 'w2')}
    del _L2_ffn_all

    def _L3_xattn_setup():
        import jax, jax.numpy as jnp
        import numpy as np
        D_MODEL = 128
        H = 16
        D_K = D_MODEL // H
        key = jax.random.key(seed)
        ks = jax.random.split(key, 12)
        B, S = (4, 256)
        q = jax.random.normal(ks[0], (B, S, D_MODEL), jnp.float32)
        k = jax.random.normal(ks[1], (B, S, D_MODEL), jnp.float32)
        v = jax.random.normal(ks[2], (B, S, D_MODEL), jnp.float32)
        mask = jnp.tril(jnp.ones((S, S), jnp.int32))[None, None]
        scale = 1.0 / np.sqrt(D_MODEL)
        Wq = jax.random.normal(ks[3], (D_MODEL, D_MODEL), jnp.float32) * scale
        bq = jax.random.normal(ks[4], (D_MODEL,), jnp.float32) * 0.02
        Wk = jax.random.normal(ks[5], (D_MODEL, D_MODEL), jnp.float32) * scale
        bk = jax.random.normal(ks[6], (D_MODEL,), jnp.float32) * 0.02
        Wv = jax.random.normal(ks[7], (D_MODEL, D_MODEL), jnp.float32) * scale
        bv = jax.random.normal(ks[8], (D_MODEL,), jnp.float32) * 0.02
        Wo = jax.random.normal(ks[9], (D_MODEL, D_MODEL), jnp.float32) * scale
        bo = jax.random.normal(ks[10], (D_MODEL,), jnp.float32) * 0.02
        return {'q': q, 'k': k, 'v': v, 'mask': mask, 'Wq': Wq, 'bq': bq, 'Wk': Wk, 'bk': bk, 'Wv': Wv, 'bv': bv, 'Wo': Wo, 'bo': bo}
    _L3_xattn_all = _L3_xattn_setup()
    _L3_xattn_in = {k: v for k, v in _L3_xattn_all.items() if k in ('Wq', 'bq', 'Wk', 'bk', 'Wv', 'bv', 'Wo', 'bo')}
    del _L3_xattn_all

    def _L3_ffn_setup():
        import jax, jax.numpy as jnp
        import numpy as np
        from jax import lax
        D = 128
        E = 8
        F = 512
        TOP_K = 2
        key = jax.random.key(seed)
        ks = jax.random.split(key, 8)
        s = 0.02
        return {'x': jax.random.normal(ks[0], (4, 256, D), dtype=jnp.float32), 'gate_w': jax.random.normal(ks[1], (D, E), dtype=jnp.float32) * s, 'gate_b': jnp.zeros((E,), dtype=jnp.float32), 'w1': jax.random.normal(ks[2], (E, D, F), dtype=jnp.float32) * s, 'b1': jnp.zeros((E, F), dtype=jnp.float32), 'w2': jax.random.normal(ks[3], (E, F, D), dtype=jnp.float32) * s, 'b2': jnp.zeros((E, D), dtype=jnp.float32)}
    _L3_ffn_all = _L3_ffn_setup()
    _L3_ffn_in = {k: v for k, v in _L3_ffn_all.items() if k in ('gate_w', 'gate_b', 'w1', 'b1', 'w2', 'b2')}
    del _L3_ffn_all
    return {'x': x, 'itok_S_0_31': itok_S_0_31, 'ctx_1024': ctx_1024, 'mask_1x1xSxS2_ik0': mask_1x1xSxS2_ik0, 'g_xattn': g_xattn, 'g_ffn': g_ffn, 'L0_ffn_phi_w': _L0_ffn_in['phi_w'], 'L0_ffn_phi_b': _L0_ffn_in['phi_b'], 'L0_ffn_expert_w': _L0_ffn_in['expert_w'], 'L0_ffn_expert_b': _L0_ffn_in['expert_b'], 'L1_xattn_Wq': _L1_xattn_in['Wq'], 'L1_xattn_bq': _L1_xattn_in['bq'], 'L1_xattn_Wk': _L1_xattn_in['Wk'], 'L1_xattn_bk': _L1_xattn_in['bk'], 'L1_xattn_Wv': _L1_xattn_in['Wv'], 'L1_xattn_bv': _L1_xattn_in['bv'], 'L1_xattn_Wo': _L1_xattn_in['Wo'], 'L1_xattn_bo': _L1_xattn_in['bo'], 'L1_ffn_centroids': _L1_ffn_in['centroids'], 'L1_ffn_expert_biases': _L1_ffn_in['expert_biases'], 'L1_ffn_Wr': _L1_ffn_in['Wr'], 'L1_ffn_br': _L1_ffn_in['br'], 'L1_ffn_Ws': _L1_ffn_in['Ws'], 'L1_ffn_bs': _L1_ffn_in['bs'], 'L2_ffn_gate_w': _L2_ffn_in['gate_w'], 'L2_ffn_w1': _L2_ffn_in['w1'], 'L2_ffn_w2': _L2_ffn_in['w2'], 'L3_xattn_Wq': _L3_xattn_in['Wq'], 'L3_xattn_bq': _L3_xattn_in['bq'], 'L3_xattn_Wk': _L3_xattn_in['Wk'], 'L3_xattn_bk': _L3_xattn_in['bk'], 'L3_xattn_Wv': _L3_xattn_in['Wv'], 'L3_xattn_bv': _L3_xattn_in['bv'], 'L3_xattn_Wo': _L3_xattn_in['Wo'], 'L3_xattn_bo': _L3_xattn_in['bo'], 'L3_ffn_gate_w': _L3_ffn_in['gate_w'], 'L3_ffn_gate_b': _L3_ffn_in['gate_b'], 'L3_ffn_w1': _L3_ffn_in['w1'], 'L3_ffn_b1': _L3_ffn_in['b1'], 'L3_ffn_w2': _L3_ffn_in['w2'], 'L3_ffn_b2': _L3_ffn_in['b2']}

def reference(x, itok_S_0_31, ctx_1024, mask_1x1xSxS2_ik0, g_xattn, g_ffn, L0_ffn_phi_w, L0_ffn_phi_b, L0_ffn_expert_w, L0_ffn_expert_b, L1_xattn_Wq, L1_xattn_bq, L1_xattn_Wk, L1_xattn_bk, L1_xattn_Wv, L1_xattn_bv, L1_xattn_Wo, L1_xattn_bo, L1_ffn_centroids, L1_ffn_expert_biases, L1_ffn_Wr, L1_ffn_br, L1_ffn_Ws, L1_ffn_bs, L2_ffn_gate_w, L2_ffn_w1, L2_ffn_w2, L3_xattn_Wq, L3_xattn_bq, L3_xattn_Wk, L3_xattn_bk, L3_xattn_Wv, L3_xattn_bv, L3_xattn_Wo, L3_xattn_bo, L3_ffn_gate_w, L3_ffn_gate_b, L3_ffn_w1, L3_ffn_b1, L3_ffn_w2, L3_ffn_b2):
    import jax
    import jax.numpy as jnp

    def _L0_xattn_ref(x, layer_idx, weight):
        import jax, jax.numpy as jnp
        import numpy as np
        NUM_LAYERS = 32
        IN_SIZE = 128
        OUT_SIZE = 128
        B, S = (32, 32)
        w = weight[layer_idx]
        return jnp.einsum('bsd,sod->bso', x, w)

    def _L0_ffn_ref(x, phi_w, phi_b, expert_w, expert_b):
        import jax, jax.numpy as jnp
        import numpy as np
        T, Z, D_DIM = (8, 256, 128)
        N_EXP, P_SLOT, H = (64, 32, 128)
        LN_EPS = 1e-05
        t, z, d = x.shape
        n = expert_w.shape[0]
        p = phi_w.shape[0] // n
        logits = (jnp.einsum('tzd,ed->tze', x, phi_w) + phi_b).reshape(t, z, n, p)
        D = jax.nn.softmax(logits, axis=3)
        C = jax.nn.softmax(logits, axis=2)
        X_tilde = jnp.einsum('tznp,tzd->npd', D, x)
        X_tilde = jnp.clip(X_tilde, -33000.0, 65000.0)
        mu = jnp.mean(X_tilde, axis=-1, keepdims=True)
        var = jnp.mean(jnp.square(X_tilde - mu), axis=-1, keepdims=True)
        X_tilde = (X_tilde - mu) * jax.lax.rsqrt(var + LN_EPS)
        X_tilde = jnp.tanh(X_tilde)
        Y_tilde = jnp.einsum('npd,ndH->npH', X_tilde, expert_w) + expert_b[:, None, :]
        Y = jnp.einsum('tznp,npH->tzH', C, Y_tilde)
        return Y

    def _L1_xattn_ref(Q, K, V, Wq, bq, Wk, bk, Wv, bv, Wo, bo):
        import jax, jax.numpy as jnp
        import numpy as np
        import math
        B, S, D, H = (4, 256, 128, 16)
        HD = D // H

        def _rope_tables(seq_len, dim, base=10000.0):
            half = dim // 2
            inv_freq = 1.0 / base ** (jnp.arange(half, dtype=jnp.float32) / half)
            angles = jnp.arange(seq_len, dtype=jnp.float32)[:, None] * inv_freq[None, :]
            return (jnp.cos(angles), jnp.sin(angles))

        def _apply_rope(x, cos, sin):
            half = x.shape[-1] // 2
            x1, x2 = (x[..., :half], x[..., half:])
            c = cos[None, None, :, :]
            s = sin[None, None, :, :]
            return jnp.concatenate([x1 * c - x2 * s, x1 * s + x2 * c], axis=-1)
        bs, n, _ = Q.shape
        q = (Q @ Wq.T + bq).reshape(bs, n, H, HD).transpose(0, 2, 1, 3)
        k = (K @ Wk.T + bk).reshape(bs, n, H, HD).transpose(0, 2, 1, 3)
        v = (V @ Wv.T + bv).reshape(bs, n, H, HD).transpose(0, 2, 1, 3)
        cos, sin = _rope_tables(n, HD)
        q = _apply_rope(q, cos, sin)
        k = _apply_rope(k, cos, sin)
        scores = jnp.einsum('bhqd,bhkd->bhqk', q, k) / math.sqrt(HD)
        causal = jnp.tril(jnp.ones((n, n), dtype=bool))
        scores = jnp.where(causal[None, None], scores, -jnp.inf)
        probs = jax.nn.softmax(scores, axis=-1)
        out = jnp.einsum('bhqk,bhkd->bhqd', probs, v)
        out = out.transpose(0, 2, 1, 3).reshape(bs, n, D)
        return out @ Wo.T + bo

    def _L1_ffn_ref(u, centroids, expert_biases, Wr, br, Ws, bs):
        import jax, jax.numpy as jnp
        import numpy as np
        TOP_K = 2
        N_r = centroids.shape[0]
        N_s = Ws.shape[0]
        raw_scores = jnp.einsum('bsd,ed->bse', u, centroids)
        s = jax.nn.softmax(raw_scores + expert_biases, axis=-1)
        topk_vals, topk_idx = jax.lax.top_k(s, TOP_K)
        g_topk = jnp.sum(jax.nn.one_hot(topk_idx, N_r, dtype=s.dtype) * topk_vals[..., None], axis=-2)
        xe = jnp.einsum('bsd,eod->bseo', u, Wr) + br
        routed = jnp.einsum('bse,bseo->bso', g_topk, xe)
        shared = (jnp.einsum('bsd,eod->bso', u, Ws) + jnp.sum(bs, axis=0)) / N_s
        return u + routed + shared

    def _L2_xattn_ref(query, key, value):
        import jax, jax.numpy as jnp
        import numpy as np
        HEADS_COUNT = 16
        HIDDEN_SIZE = 128
        SCALE = float(np.sqrt(HIDDEN_SIZE // HEADS_COUNT))
        B, S, D = (4, 512, 128)
        qk = jnp.einsum('bqd,bkd->bqk', query, key)
        scaled_qk = qk * SCALE
        attn = jax.nn.softmax(scaled_qk, axis=-1)
        out = jnp.einsum('bqk,bkd->bqd', attn, value)
        return out

    def _L2_ffn_ref(x, gate_w, w1, w2):
        import jax, jax.numpy as jnp
        import numpy as np
        NUM_EXPERTS = 8
        EXPERT_CAPACITY = 2.0
        B, T, C = x.shape
        E = gate_w.shape[1]
        cap = int(EXPERT_CAPACITY * T / E)
        scores = jnp.einsum('BTC,CE->BTE', x, gate_w)
        probs = jax.nn.softmax(scores, axis=-1)
        probs_et = jnp.transpose(probs, (0, 2, 1))
        top_p, top_idx = jax.lax.top_k(probs_et, cap)
        xin = jnp.take_along_axis(x[:, None, :, :], top_idx[..., None], axis=2)
        h = jax.nn.gelu(jnp.einsum('BElC,ECH->BElH', xin, w1), approximate=False)
        y = jnp.einsum('BElH,EHC->BElC', h, w2)
        y = y * top_p[..., None]
        b_idx = jnp.arange(B)[:, None, None]
        out = jnp.zeros((B, T, C), x.dtype).at[b_idx, top_idx].add(y)
        return out

    def _L3_xattn_ref(q, k, v, mask, Wq, bq, Wk, bk, Wv, bv, Wo, bo):
        import jax, jax.numpy as jnp
        import numpy as np
        D_MODEL = 128
        H = 16
        D_K = D_MODEL // H
        B, S, _ = q.shape
        query = q @ Wq.T + bq
        key = k @ Wk.T + bk
        value = v @ Wv.T + bv

        def split_heads(x):
            return x.reshape(B, S, H, D_K).transpose(0, 2, 1, 3)
        query, key, value = (split_heads(query), split_heads(key), split_heads(value))
        scores = jnp.einsum('bhqd,bhkd->bhqk', query, key) / np.sqrt(D_K)
        scores = jnp.where(mask == 0, jnp.float32(-1000000000.0), scores)
        attn = jax.nn.softmax(scores, axis=-1)
        x = jnp.einsum('bhqk,bhkd->bhqd', attn, value)
        x = x.transpose(0, 2, 1, 3).reshape(B, S, D_MODEL)
        return x @ Wo.T + bo

    def _L3_ffn_ref(x, gate_w, gate_b, w1, b1, w2, b2):
        import jax, jax.numpy as jnp
        import numpy as np
        from jax import lax
        D = 128
        E = 8
        F = 512
        TOP_K = 2
        B, S, _ = x.shape
        flat = x.reshape(-1, D)
        T = flat.shape[0]
        logits = flat @ gate_w + gate_b
        topv, topi = lax.top_k(logits, TOP_K)
        topw = jax.nn.softmax(topv.astype(jnp.float32), axis=-1).astype(x.dtype)
        routing = jnp.zeros_like(logits).at[jnp.arange(T)[:, None], topi].set(topw)

        def body(acc, params):
            W1e, b1e, W2e, b2e, we = params
            h = jax.nn.gelu(flat @ W1e + b1e, approximate=False)
            out = h @ W2e + b2e
            return (acc + out * we[:, None], None)
        init = jnp.zeros_like(flat)
        final, _ = lax.scan(body, init, (w1, b1, w2, b2, routing.T))
        return final.reshape(B, S, D)
    x = x + jnp.tanh(g_xattn[0]) * _L0_xattn_ref(_layernorm(x, axis=-1), itok_S_0_31, ctx_1024)
    x = x + jnp.tanh(g_ffn[0]) * _L0_ffn_ref(_layernorm(x, axis=-1), L0_ffn_phi_w, L0_ffn_phi_b, L0_ffn_expert_w, L0_ffn_expert_b)
    x = x + jnp.tanh(g_xattn[1]) * _L1_xattn_ref(_layernorm(x, axis=-1), ctx_1024, ctx_1024, L1_xattn_Wq, L1_xattn_bq, L1_xattn_Wk, L1_xattn_bk, L1_xattn_Wv, L1_xattn_bv, L1_xattn_Wo, L1_xattn_bo)
    x = x + jnp.tanh(g_ffn[1]) * _L1_ffn_ref(_layernorm(x, axis=-1), L1_ffn_centroids, L1_ffn_expert_biases, L1_ffn_Wr, L1_ffn_br, L1_ffn_Ws, L1_ffn_bs)
    x = x + jnp.tanh(g_xattn[2]) * _L2_xattn_ref(_layernorm(x, axis=-1), ctx_1024, ctx_1024)
    x = x + jnp.tanh(g_ffn[2]) * _L2_ffn_ref(_layernorm(x, axis=-1), L2_ffn_gate_w, L2_ffn_w1, L2_ffn_w2)
    x = x + jnp.tanh(g_xattn[3]) * _L3_xattn_ref(_layernorm(x, axis=-1), ctx_1024, ctx_1024, mask_1x1xSxS2_ik0, L3_xattn_Wq, L3_xattn_bq, L3_xattn_Wk, L3_xattn_bk, L3_xattn_Wv, L3_xattn_bv, L3_xattn_Wo, L3_xattn_bo)
    x = x + jnp.tanh(g_ffn[3]) * _L3_ffn_ref(_layernorm(x, axis=-1), L3_ffn_gate_w, L3_ffn_gate_b, L3_ffn_w1, L3_ffn_b1, L3_ffn_w2, L3_ffn_b2)
    return x

_drawn_inputs = setup_inputs


def setup_inputs(seed=0):
    import zlib

    import numpy as np

    out = dict(_drawn_inputs(seed))
    spreads = {'L1_xattn_bq': (0.0, 0.8),
     'L1_xattn_bk': (0.0, 0.8),
     'L1_xattn_bv': (0.0, 0.766),
     'L1_xattn_bo': (0.0, 0.654),
     'L1_ffn_expert_biases': (0.0, 0.8),
     'L3_ffn_gate_b': (0.0, 0.8),
     'L3_ffn_b1': (0.0, 0.8),
     'L3_ffn_b2': (0.0, 0.8)}
    factors = {'g_ffn': 8.0,
     'L0_ffn_phi_w': 8.0,
     'L0_ffn_phi_b': 8.0,
     'L0_ffn_expert_b': 7.018,
     'L1_ffn_br': 8.0,
     'L1_ffn_bs': 8.0,
     'L2_ffn_gate_w': 8.0,
     'L2_ffn_w1': 8.0,
     'L2_ffn_w2': 8.0,
     'L3_xattn_bv': 8.0,
     'L3_xattn_bo': 8.0,
     'L3_ffn_gate_w': 8.0,
     'L3_ffn_w1': 8.0,
     'L3_ffn_w2': 8.0}
    for name, (base, spread) in spreads.items():
        noise = np.random.default_rng([zlib.crc32(name.encode()), seed]).standard_normal(out[name].shape)
        drawn = base * np.exp(spread * noise) if base else spread * noise
        out[name] = jnp.asarray(drawn.astype(out[name].dtype))
    for name, factor in factors.items():
        out[name] = (out[name] * factor).astype(out[name].dtype)
    return out
```

```python
import numpy as np
from contextlib import ExitStack

import concourse.bass as bass
from concourse import mybir

F32 = mybir.dt.float32
F32R = mybir.dt.float32r
BF16 = mybir.dt.bfloat16
I32 = mybir.dt.int32
ALU = mybir.AluOpType
ACT = mybir.ActivationFunctionType
AX = mybir.AxisListType

B, S, D = 32, 128, 128
GB = 4
NG = B // GB
GD = GB * D
EPS = 1e-5
NL, NP = 64, 32
NE_L0 = NL * NP
H, HD = 16, 8
NR = 16
NX, FF = 8, 512
FC = FF // 128
CAP = 32
TOPK = 2
NEG = -(2.0 ** 100)


class Steps:

    def __init__(self, eng, sem):
        self.eng, self.sem, self.base, self.k = eng, sem, 0, 0

    def link(self, ins):
        ins.then_inc(self.sem, 1)
        self.k += 1
        self.eng.wait_ge(self.sem, self.base + self.k)

    def loop(self, n, i, per):
        self.start = self.base + self.k
        self.per, self.n = per, n
        self.base, self.k = i * per + self.start, 0

    def end(self):
        assert self.k == self.per, (self.k, self.per)
        self.base, self.k = self.start + self.n * self.per, 0


class Stage:

    def __init__(self, nc, name):
        self.nc, self.name, self.ctx, self.sems = nc, name, ExitStack(), []

    def __enter__(self):
        return self

    def __exit__(self, *a):
        self.ctx.__exit__(*a)
        if a[0] is None:
            self.nc.clear_and_free_semaphores(self.sems)
            self.nc.all_engine_barrier()

    def sb(self, name, shape, dt=F32):
        return self.ctx.enter_context(self.nc.sbuf_tensor(f"{self.name}_{name}", shape, dt))

    def bank(self, name, dt=F32):
        return self.ctx.enter_context(self.nc.psum_tensor(f"{self.name}_{name}", [128, 512], dt))

    def sem(self, name):
        self.sems.append(self.nc.alloc_semaphore(f"{self.name}_{name}"))
        return self.sems[-1]

    def block(self):
        return self.ctx.enter_context(self.nc.Block())


class Front:

    def __init__(self, st, p):
        self.st, self.p = st, p
        self.xn = [st.sb(f"xn{u}", [128, GB, D]) for u in range(2)]
        self.xnT = [st.sb(f"xnT{u}", [128, GD]) for u in range(2)]
        self.ps = st.bank("frontT")
        self.xn_ready = st.sem("xn_ready")
        self.xn_used = st.sem("xn_used")
        self.xnT_ps = st.sem("xnT_ps")
        self.xnT_ready = st.sem("xnT_ready")
        self.xnT_used = st.sem("xnT_used")

    def vector(self, eng, n, u):
        nc, p = self.st.nc, self.p
        eng.wait_ge(self.xn_used, n + 1)
        for j in range(GB):
            b = n * GB + j
            ins = nc.vector.tensor_scalar(self.xn[u][:, j, :], p.X[:, bass.ds(b, 1), :].rearrange("p a d -> p (a d)"),
                                          p.mean[:, bass.ds(b, 1)], p.rstd[:, bass.ds(b, 1)],
                                          ALU.subtract, ALU.mult)
        ins.then_inc(self.xn_ready, 1)

    def tensor(self, eng, n, u):
        nc = self.st.nc
        eng.wait_ge(self.xn_ready, n + 1)
        eng.wait_ge(self.xnT_ready, n + 1)
        for j in range(GB):
            ins = nc.tensor.transpose(self.ps[:, j * D:(j + 1) * D], self.xn[u][:, j, :], self.p.ident[:])
        ins.then_inc(self.xnT_ps, 1)

    def scalar(self, eng, n, u):
        nc = self.st.nc
        eng.wait_ge(self.xnT_ps, n + 1)
        eng.wait_ge(self.xnT_used, n + 1)
        nc.scalar.activation(self.xnT[u][:], self.ps[:], ACT.Copy).then_inc(self.xnT_ready, 1)


def stand(eng, waited):
    eng.sem_inc(waited, 1)


def credit(eng, *pairs):
    for sem, n in pairs:
        eng.sem_inc(sem, n)


class Tail:
    STEPS = 3

    def __init__(self, st, p):
        self.st, self.p = st, p
        self.stats = st.sb("bn", [128, GB, 6])
        self.mv = st.sb("mv", [128, 2, GB, 2])
        self.var_ready = st.sem("var_ready")
        self.rstd_done = st.sem("rstd_done")
        self.waited = st.sem("tail_waited")

    def vector(self, eng, n, u, steps, last):
        nc, p = self.st.nc, self.p
        steps.link(last)
        stand(eng, self.waited)
        for j in range(GB):
            ins = nc.vector.bn_stats(self.stats[:, j, :], p.X[:, bass.ds(n * GB + j, 1), :].rearrange("p a d -> p (a d)"))
        steps.link(ins)
        eng.wait_ge(self.rstd_done, n + 1)
        stand(eng, self.waited)
        for j in range(GB):
            ins = nc.vector.bn_aggr(self.mv[:, u, j, :], self.stats[:, j, :])
        steps.link(ins)
        stand(eng, self.waited)
        nc.vector.tensor_copy(p.mean[:, bass.ds(n * GB, GB)], self.mv[:, u, :, 0])
        nc.vector.tensor_scalar(self.mv[:, u, :, 1], self.mv[:, u, :, 1], EPS, None, ALU.add)\
            .then_inc(self.var_ready, 1)

    def gpsimd(self, eng, n, u):
        nc, p = self.st.nc, self.p
        eng.wait_ge(self.var_ready, n + 2)
        nc.gpsimd.tensor_tensor(p.rstd[:, bass.ds(n * GB, GB)], self.mv[:, u, :, 1], p.mhalf[:, 0:GB], ALU.pow)\
            .then_inc(self.rstd_done, 1)


def over_groups(eng, body, steps=None, per=0):
    with eng.Fori(0, NG // 2 - 1) as i:
        if steps:
            steps.loop(NG // 2 - 1, i, per)
        body(i * 2, 0, True)
        body(i * 2 + 1, 1, True)
        if steps:
            steps.end()
    body(NG - 2, 0, True)
    body(NG - 1, 1, False)


def xgroup(p, n):
    return p.X[:, bass.ds(n * GB, GB), :]


def stage_a(nc, p, d):
    RING, PB = 8, 16
    with Stage(nc, "A") as st:
        xn = [st.sb(f"xn{u}", [128, GB, D]) for u in range(2)]
        xnT = st.sb("xnT", [128, B, S])
        wring = st.sb("wring", [128, RING, D])
        yT = st.sb("yT", [128, B, S])
        stats = st.sb("stats", [128, B, 6])
        itok = st.sb("itok", [1, S], I32)
        graw = st.sb("graw", [128, 8])
        front = [st.bank(f"front{u}") for u in range(2)]
        pos = [st.bank(f"pos{u}") for u in range(2)]
        x_in = [st.sem(f"x_in{g}") for g in range(NG)]
        g_in, tok_in, const_in = st.sem("g_in"), st.sem("tok_in"), st.sem("const_in")
        mh_ready, var_ready, rstd_ready, v_step = st.sem("mh"), st.sem("var"), st.sem("rstd"), st.sem("v_step")
        xn_ready, xT_ps, xT_ready = st.sem("xn_ready"), st.sem("xT_ps"), st.sem("xT_ready")
        w_in = [st.sem(f"w_in{r}") for r in range(RING)]
        w_used, y_ps, y_out = st.sem("w_used"), st.sem("y_ps"), st.sem("y_out")
        yt_ps, x_new, gate_ready = st.sem("yt_ps"), st.sem("x_new"), st.sem("gate_ready")
        pool_done = st.sem("pool_done")
        block = st.block()

        @block.sync
        def _(sp):
            sp.dma_start(itok[:], d["itok"]).then_inc(tok_in, 16)
            for g in range(NG):
                sp.dma_start(p.X[:, g * GB:(g + 1) * GB, :], d["x"][:, g * GB:(g + 1) * GB, :]).then_inc(x_in[g], 16)
            sp.dma_start(p.ident[:], d["ident"]).then_inc(const_in, 16)
            sp.wait_ge(tok_in, 16)
            credit(sp, (w_used, RING))
            with sp.Fori(0, S // RING) as i:
                for r in range(RING):
                    s0 = i * RING
                    t = nc.values_load(itok[0:1, bass.ds(s0 + r, 1)], engines=[mybir.EngineType.SP],
                                       min_val=0, max_val=B - 1)
                    sp.wait_ge(w_used, s0 + r + 1)
                    sp.dma_start(wring[:, r, :], d["ctxT_rows"][bass.ds(t, 1), :, :].rearrange("a p o -> (a p) o"))\
                        .then_inc(w_in[r], 16)

        @block.gpsimd
        def _(g):
            for dst, src in ((graw[:, 0:4], d["g_xattn"]), (graw[:, 4:8], d["g_ffn"])):
                g.dma_start(dst, src.rearrange("(a n) -> a n", a=1).to_broadcast([128, 4])).then_inc(g_in, 16)
            nc.gpsimd.memset(p.mhalf[:], -0.5).then_inc(mh_ready, 1)
            g.wait_ge(mh_ready, 1)
            g.wait_ge(var_ready, 1)
            nc.gpsimd.tensor_tensor(p.rstd[:], stats[:, :, 1], p.mhalf[:], ALU.pow).then_inc(rstd_ready, 1)
            for n in range(NG):
                g.wait_ge(x_new, n + 1)
                nc.gpsimd.tensor_tensor(p.rstd[:, n * GB:(n + 1) * GB], stats[:, n * GB:(n + 1) * GB, 1],
                                        p.mhalf[:, 0:GB], ALU.pow).then_inc(pool_done, 1)

        @block.vector
        def _(v):
            steps = Steps(v, v_step)
            mv = stats
            for g in range(NG):
                v.wait_ge(x_in[g], 16)
                for b in range(g * GB, (g + 1) * GB):
                    ins = nc.vector.bn_stats(xnT[:, b, 0:6], p.X[:, b, :])
            steps.link(ins)
            for b in range(B):
                ins = nc.vector.bn_aggr(mv[:, b, 0:2], xnT[:, b, 0:6])
            steps.link(ins)
            nc.vector.tensor_copy(p.mean[:], mv[:, :, 0])
            steps.link(nc.vector.tensor_scalar(mv[:, :, 1], mv[:, :, 1], EPS, None, ALU.add))
            v.sem_inc(var_ready, 1)
            v.wait_ge(const_in, 16)
            nc.vector.tensor_copy(p.ident16[:], p.ident[:])
            v.wait_ge(rstd_ready, 1)
            for g in range(NG):
                if g >= 2:
                    v.wait_ge(xT_ps, g - 1)
                for j in range(GB):
                    b = g * GB + j
                    ins = nc.vector.tensor_scalar(xn[g % 2][:, j, :], p.X[:, b, :], p.mean[:, b:b + 1],
                                                  p.rstd[:, b:b + 1], ALU.subtract, ALU.mult)
                ins.then_inc(xn_ready, 1)
            v.wait_ge(gate_ready, 1)
            for g in range(NG):
                v.wait_ge(yt_ps, g + 1)
                xg = p.X[:, g * GB:(g + 1) * GB, :]
                steps.link(nc.vector.scalar_tensor_tensor(xg, front[g % 2][:].rearrange("p (a d) -> p a d", a=GB),
                                                          p.gate[:, 0:1], xg, ALU.mult, ALU.add))
                for j in range(GB):
                    ins = nc.vector.bn_stats(xn[0][:, j, 0:6], p.X[:, g * GB + j, :])
                steps.link(ins)
                for j in range(GB):
                    ins = nc.vector.bn_aggr(mv[:, g * GB + j, 0:2], xn[0][:, j, 0:6])
                steps.link(ins)
                nc.vector.tensor_copy(p.mean[:, g * GB:(g + 1) * GB], mv[:, g * GB:(g + 1) * GB, 0])
                steps.link(nc.vector.tensor_scalar(mv[:, g * GB:(g + 1) * GB, 1], mv[:, g * GB:(g + 1) * GB, 1],
                                                   EPS, None, ALU.add))
                v.sem_inc(x_new, 1)

        @block.scalar
        def _(a):
            a.wait_ge(g_in, 32)
            nc.scalar.activation(p.gate[:], graw[:], ACT.Tanh).then_inc(gate_ready, 1)
            for g in range(NG):
                a.wait_ge(xT_ps, g + 1)
                nc.scalar.activation(xnT[:, g * GB:(g + 1) * GB, :],
                                     front[g % 2][:].rearrange("p (a d) -> p a d", a=GB), ACT.Copy).then_inc(xT_ready, 1)
            with a.Fori(0, S // PB // 2) as i:
                for u in range(2):
                    k = i * 2 + u
                    a.wait_ge(y_ps, k + 1)
                    nc.scalar.activation(yT[:, :, bass.ds(k * PB, PB)],
                                         pos[u][:].rearrange("p (s b) -> p b s", s=PB), ACT.Copy).then_inc(y_out, 1)

        @block.tensor
        def _(t):
            t.wait_ge(const_in, 16)
            for g in range(NG):
                t.wait_ge(xn_ready, g + 1)
                if g >= 2:
                    t.wait_ge(xT_ready, g - 1)
                for j in range(GB):
                    ins = nc.tensor.transpose(front[g % 2][:, j * D:(j + 1) * D], xn[g % 2][:, j, :], p.ident[:])
                ins.then_inc(xT_ps, 1)
            t.wait_ge(xT_ready, NG)
            credit(t, (y_out, 2))
            with t.Fori(0, S // PB // 2) as i:
                for u in range(2):
                    k = i * 2 + u
                    t.wait_ge(y_out, k + 1)
                    for q in range(PB):
                        r = q % RING
                        t.wait_ge(w_in[r], k * (16 * PB // RING) + 16 * (q // RING) + 16)
                        ins = nc.tensor.matmul(pos[u][:, q * B:(q + 1) * B], wring[:, r, :],
                                               xnT[:, :, bass.ds(k * PB + q, 1)].rearrange("p b a -> p (b a)"),
                                               start=True, stop=True)
                        ins.then_inc(w_used, 1)
                    t.wait_ge(w_used, (k * PB) + PB + RING)
                    t.sem_inc(y_ps, 1)
            t.wait_ge(y_out, S // PB + 2)
            for g in range(NG):
                if g >= 2:
                    t.wait_ge(x_new, g - 1)
                for j in range(GB):
                    ins = nc.tensor.transpose(front[g % 2][:, j * D:(j + 1) * D], yT[:, g * GB + j, :], p.ident[:])
                ins.then_inc(yt_ps, 1)


class SoftUnit:
    RING, STEPS = 4, 4

    def __init__(self, st, size):
        self.st, self.size, self.ng = st, size, 512 // size
        self.banks = [st.bank(f"logits{i}") for i in range(2)]
        self.E = [st.sb(f"E{i}", [128, 512]) for i in range(self.RING)]
        self.m = st.sb("m", [128, 2, self.ng])
        self.r = st.sb("r", [128, 2, self.ng])
        self.logits_ready = st.sem("logits_ready")
        self.diff_done = st.sem("diff_done")
        self.exp_done = st.sem("exp_done")
        self.probs_ready = st.sem("probs_ready")
        self.probs_used = st.sem("probs_used")

    def bank(self, w):
        return self.banks[w % 2]

    def tensor_logits(self, eng, k, w, xT, phiT, q, p):
        nc = self.st.nc
        eng.wait_ge(self.diff_done, k + 1)
        nc.tensor.matmul(self.bank(w)[:], xT, phiT[:, q * 512:(q + 1) * 512], start=True, stop=False)
        nc.tensor.matmul(self.bank(w)[:], p.ones16[:], p.bias3[:, q * 512:(q + 1) * 512], start=False, stop=True)\
            .then_inc(self.logits_ready, 1)

    def vector_diff(self, eng, k, w, steps):
        nc = self.st.nc
        lg = self.bank(w)[:].rearrange("p (n q) -> p n q", q=self.size)
        e = self.E[w % self.RING][:].rearrange("p (n q) -> p n q", q=self.size)
        eng.wait_ge(self.logits_ready, k + 1)
        steps.link(nc.vector.tensor_reduce(self.m[:, w % 2, :], lg, AX.X, ALU.max))
        eng.wait_ge(self.probs_used, k + 1)
        nc.vector.tensor_tensor(e, lg, self.m[:, w % 2, :].unsqueeze(2).to_broadcast([128, self.ng, self.size]),
                                ALU.subtract).then_inc(self.diff_done, 1)

    def scalar_exp(self, eng, k, w):
        e = self.E[w % self.RING][:]
        eng.wait_ge(self.diff_done, k + 3)
        self.st.nc.scalar.activation(e, e, ACT.Exp).then_inc(self.exp_done, 1)

    def vector_norm(self, eng, k, w, steps):
        nc = self.st.nc
        e = self.E[w % self.RING][:].rearrange("p (n q) -> p n q", q=self.size)
        r = self.r[:, w % 2, :]
        eng.wait_ge(self.exp_done, k + 1)
        steps.link(nc.vector.tensor_reduce(r, e, AX.X, ALU.add))
        steps.link(nc.vector.reciprocal(r, r))
        nc.vector.tensor_tensor(e, e, r.unsqueeze(2).to_broadcast([128, self.ng, self.size]), ALU.mult)\
            .then_inc(self.probs_ready, 1)

    UNIT_STEPS = 3


NQ = NE_L0 // 512
UG = GB * NQ


def bias_parts(nc, v, steps, raw, bias3, part, order):
    pick = (lambda ap: ap) if order is None else order
    for row in range(3):
        steps.link(nc.vector.tensor_copy(part[0:96, :], raw[0:96, :]))
        src = part[32 * row:32 * row + 1, :]
        nc.vector.tensor_copy(bias3[32 * row:32 * row + 1, :], src)
        if row < 2:
            steps.link(nc.vector.tensor_tensor(raw[0:96, :], raw[0:96, :], part[0:96, :], ALU.subtract))


def stage_b1(nc, p, d, XtT):
    with Stage(nc, "B1") as st:
        front = Front(st, p)
        soft = SoftUnit(st, NP)
        acc = [st.bank(f"acc{q}") for q in range(NQ)]
        phiT = st.sb("phiT", [128, NE_L0])
        raw, part = st.sb("raw", [96, NE_L0]), st.sb("part", [96, NE_L0], BF16)
        zero = st.sb("zero", [128, 512], BF16)
        phi_in, raw_in, raw_zero, consts = st.sem("phi_in"), st.sem("raw_in"), st.sem("raw_zero"), st.sem("consts")
        bias_ready, v_step, acc_done, acc_out = st.sem("bias_ready"), st.sem("v_step"), st.sem("acc_done"), st.sem("acc_out")
        block = st.block()

        @block.sync
        def _(sp):
            sp.dma_start(phiT[:], d["phiT"]).then_inc(phi_in, 16)
            sp.wait_ge(raw_zero, 1)
            for row in range(3):
                sp.dma_start(raw[32 * row:32 * row + 1, :], d["phi_b"]).then_inc(raw_in, 16)

        @block.gpsimd
        def _(g):
            nc.gpsimd.memset(raw[:], 0.0).then_inc(raw_zero, 1)
            nc.gpsimd.memset(zero[:], 0.0).then_inc(consts, 1)
            nc.gpsimd.memset(p.ones16[:], 1.0).then_inc(consts, 1)
            nc.gpsimd.memset(p.bias3[:], 0.0).then_inc(consts, 1)

        @block.vector
        def _(v):
            steps = Steps(v, v_step)
            credit(v, (soft.diff_done, 2))
            front.vector(v, 0, 0)
            v.wait_ge(raw_in, 48)
            v.wait_ge(consts, 3)
            bias_parts(nc, v, steps, raw, p.bias3, part, None)
            steps.link(nc.vector.tensor_copy(part[0:1, 0:8], part[0:1, 8:16]))
            v.sem_inc(bias_ready, 1)

            def group(n, u, more):
                for w in range(UG):
                    soft.vector_diff(v, n * UG + w, w, steps)
                    if w > 0:
                        soft.vector_norm(v, n * UG + w - 1, w - 1, steps)
                    if w == UG // 2 and more:
                        front.vector(v, n + 1, 1 - u)
                soft.vector_norm(v, n * UG + UG - 1, UG - 1, steps)

            over_groups(v, group, steps, 2 * UG * soft.UNIT_STEPS)
            v.wait_ge(acc_done, 1)
            for q in range(NQ):
                ins = nc.vector.tensor_copy(XtT[:, q * 512:(q + 1) * 512], acc[q][:])
            steps.link(ins)

        @block.scalar
        def _(a):
            credit(a, (front.xnT_ready, 1))
            front.scalar(a, 0, 0)

            def group(n, u, more):
                for w in range(UG):
                    soft.scalar_exp(a, n * UG + w, w)
                    if w == UG // 2 and more:
                        front.scalar(a, n + 1, 1 - u)

            over_groups(a, group)

        @block.tensor
        def _(t):
            credit(t, (front.xn_used, 2), (front.xnT_used, 2), (soft.probs_used, soft.RING))
            front.tensor(t, 0, 0)
            t.wait_ge(phi_in, 16)
            t.wait_ge(consts, 3)
            t.wait_ge(bias_ready, 1)
            for q in range(NQ):
                nc.tensor.matmul(acc[q][:], zero[:, 0:128], zero[:], start=True, stop=False, skip_group_check=True)

            def dispatch(k, w, u):
                t.wait_ge(soft.probs_ready, k + 1)
                nc.tensor.matmul(acc[w % NQ][:], front.xn[u][:, w // NQ, :], soft.E[w % soft.RING][:],
                                 start=False, stop=False, skip_group_check=True).then_inc(soft.probs_used, 1)

            def group(n, u, more):
                t.wait_ge(front.xnT_ready, n + 2)
                for w in range(UG):
                    j = w // NQ
                    soft.tensor_logits(t, n * UG + w, w, front.xnT[u][:, j * 128:(j + 1) * 128], phiT, w % NQ, p)
                    if w >= 2:
                        dispatch(n * UG + w - 2, w - 2, u)
                    if w == UG // 2 and more:
                        front.tensor(t, n + 1, 1 - u)
                t.wait_ge(soft.logits_ready, (n + 1) * UG)
                t.sem_inc(front.xnT_used, 1)
                for w in range(UG - 2, UG):
                    dispatch(n * UG + w, w, u)
                t.wait_ge(soft.probs_used, (n + 1) * UG + soft.RING)
                t.sem_inc(front.xn_used, 1)

            over_groups(t, group)
            for q in range(NQ):
                ins = nc.tensor.matmul(acc[q][:], zero[:, 0:128], zero[:], start=False, stop=True, skip_group_check=True)
            ins.then_inc(acc_done, 1)


def stage_mid(nc, p, d, XtT, Yt):
    NC = NE_L0 // 128
    with Stage(nc, "M") as st:
        ew = st.sb("ew", [128, NL, 128])
        eb = st.sb("eb", [NL, 128])
        sel = st.sb("sel", [NL, NE_L0])
        xt = st.sb("xt", [128, NC, D])
        xtn = st.sb("xtn", [128, NC, D])
        yn = st.sb("yn", [128, NC, D])
        stats, mv, rs = st.sb("stats", [128, NC, 6]), st.sb("mv", [128, NC, 2]), st.sb("rs", [128, NC])
        banks = [st.bank(f"b{q}") for q in range(4)]
        ybanks = [st.bank(f"y{q}") for q in range(4)]
        scratch = nc.dram_tensor("slots_scratch", (NP, NL, 128), F32, kind="Internal").ap()
        ew_in, tr, v_step, var_ready, rs_ready = st.sem("ew_in"), st.sem("tr"), st.sem("v_step"), st.sem("var"), st.sem("rs")
        norm, th, tr2, back, y_ps, y_sb = st.sem("norm"), st.sem("th"), st.sem("tr2"), st.sem("back"), st.sem("y_ps"), st.sem("y_sb")
        put, got = st.sem("put"), st.sem("got")
        block = st.block()

        @block.sync
        def _(sp):
            sp.dma_start(ew[:], d["expert_w"]).then_inc(ew_in, 16)
            sp.dma_start(eb[:], d["expert_b"]).then_inc(ew_in, 16)
            sp.dma_start(sel[:], d["sel_expert"]).then_inc(ew_in, 16)
            sp.wait_ge(y_sb, 4)
            for a4 in range(4):
                sp.dma_start(scratch.rearrange("s (c a) h -> a s c h", a=4)[a4], yn[32 * a4:32 * a4 + 32, :, :])\
                    .then_inc(put, 16)
            sp.wait_ge(put, 64)
            sp.dma_start(Yt[:], scratch.rearrange("(c s) n h -> (s n) c h", s=2)).then_inc(got, 16)
            sp.wait_ge(got, 16)

        @block.gpsimd
        def _(g):
            g.wait_ge(var_ready, 1)
            nc.gpsimd.tensor_tensor(rs[:], mv[:, :, 1], p.mhalf[:, 0:NC], ALU.pow).then_inc(rs_ready, 1)

        @block.vector
        def _(v):
            steps = Steps(v, v_step)
            for q in range(4):
                v.wait_ge(tr, q + 1)
                steps.link(nc.vector.tensor_scalar(xt[:, 4 * q:4 * q + 4, :], banks[q][:].rearrange("p (c d) -> p c d", c=4),
                                                   -33000.0, 65000.0, ALU.max, ALU.min))
            for c in range(NC):
                ins = nc.vector.bn_stats(stats[:, c, :], xt[:, c, :])
            steps.link(ins)
            for c in range(NC):
                ins = nc.vector.bn_aggr(mv[:, c, :], stats[:, c, :])
            steps.link(ins)
            nc.vector.tensor_scalar(mv[:, :, 1], mv[:, :, 1], EPS, None, ALU.add).then_inc(var_ready, 1)
            v.wait_ge(rs_ready, 1)
            for c in range(NC):
                nc.vector.tensor_scalar(xtn[:, c, :], xt[:, c, :], mv[:, c, 0:1], rs[:, c:c + 1],
                                        ALU.subtract, ALU.mult).then_inc(norm, 1)
            for q in range(4):
                v.wait_ge(tr2, q + 1)
                nc.vector.tensor_copy(XtT[:, q * 512:(q + 1) * 512], banks[q][:]).then_inc(back, 1)

        @block.scalar
        def _(a):
            for q in range(4):
                a.wait_ge(norm, 4 * q + 4)
                x4 = xtn[:, 4 * q:4 * q + 4, :]
                nc.scalar.activation(x4, x4, ACT.Tanh).then_inc(th, 1)
            for q in range(4):
                a.wait_ge(y_ps, q + 1)
                nc.scalar.activation(yn[:, 4 * q:4 * q + 4, :], ybanks[q][:].rearrange("p (c d) -> p c d", c=4),
                                     ACT.Copy).then_inc(y_sb, 1)

        @block.tensor
        def _(t):
            for q in range(4):
                for c in range(4 * q, 4 * q + 4):
                    ins = nc.tensor.transpose(banks[q][:, (c % 4) * 128:(c % 4 + 1) * 128], XtT[:, c * 128:(c + 1) * 128],
                                              p.ident[:])
                ins.then_inc(tr, 1)
            for q in range(4):
                t.wait_ge(th, q + 1)
                for c in range(4 * q, 4 * q + 4):
                    ins = nc.tensor.transpose(banks[q][:, (c % 4) * 128:(c % 4 + 1) * 128], xtn[:, c, :], p.ident[:])
                ins.then_inc(tr2, 1)
            t.wait_ge(ew_in, 48)
            for q in range(4):
                t.wait_ge(back, q + 1)
                for c in range(4 * q, 4 * q + 4):
                    cols = slice((c % 4) * 128, (c % 4 + 1) * 128)
                    nc.tensor.matmul(ybanks[q][:, cols], sel[:, c * 128:(c + 1) * 128], eb[:], start=True, stop=False,
                                     skip_group_check=True)
                    for a4 in range(4):
                        e = 4 * c + a4
                        ins = nc.tensor.matmul(ybanks[q][32 * a4:32 * a4 + 32, cols], XtT[:, e * NP:(e + 1) * NP],
                                               ew[:, e, :], start=False, stop=True, skip_group_check=True)
                ins.then_inc(y_ps, 1)


def stage_b2(nc, p, d, Yt):
    with Stage(nc, "B2") as st:
        front, tail = Front(st, p), Tail(st, p)
        soft = SoftUnit(st, NL)
        phiT = st.sb("phiT", [128, NE_L0])
        raw, part = st.sb("raw", [96, NE_L0]), st.sb("part", [96, NE_L0], BF16)
        ct_ps = [st.bank(f"ct{i}") for i in range(2)]
        y_ps = st.bank("y")
        CT = [st.sb(f"CT{i}", [128, 512]) for i in range(2)]
        phi_in, raw_in, raw_zero = st.sem("phi_in"), st.sem("raw_in"), st.sem("raw_zero")
        bias_ready, v_step = st.sem("bias_ready"), st.sem("v_step")
        ct_moved, ct_ready, ct_used = st.sem("ct_moved"), st.sem("ct_ready"), st.sem("ct_used")
        y_ready = st.sem("y_ready")
        block = st.block()

        @block.sync
        def _(sp):
            sp.dma_start(phiT[:], d["phiT_slots"]).then_inc(phi_in, 16)
            sp.wait_ge(raw_zero, 1)
            for row in range(3):
                sp.dma_start(raw[32 * row:32 * row + 1, :], d["phi_b_slots"]).then_inc(raw_in, 16)

        @block.gpsimd
        def _(g):
            nc.gpsimd.memset(raw[:], 0.0).then_inc(raw_zero, 1)
            credit(g, (tail.rstd_done, 2))
            over_groups(g, lambda n, u, more: tail.gpsimd(g, n, u))

        @block.vector
        def _(v):
            steps = Steps(v, v_step)
            credit(v, (soft.diff_done, 2), (tail.var_ready, 1))
            front.vector(v, 0, 0)
            v.wait_ge(raw_in, 48)
            bias_parts(nc, v, steps, raw, p.bias3, part, None)
            steps.link(nc.vector.tensor_copy(part[0:1, 0:8], part[0:1, 8:16]))
            v.sem_inc(bias_ready, 1)

            def group(n, u, more):
                for w in range(UG):
                    soft.vector_diff(v, n * UG + w, w, steps)
                    if w > 0:
                        soft.vector_norm(v, n * UG + w - 1, w - 1, steps)
                    if w == UG // 2 and more:
                        front.vector(v, n + 1, 1 - u)
                soft.vector_norm(v, n * UG + UG - 1, UG - 1, steps)
                v.wait_ge(y_ready, n + 1)
                tail.vector(v, n, u, steps, nc.vector.scalar_tensor_tensor(
                    xgroup(p, n), y_ps[:].rearrange("p (a d) -> p a d", a=GB), p.gate[:, 4:5], xgroup(p, n),
                    ALU.mult, ALU.add))

            over_groups(v, group, steps, 2 * (UG * soft.UNIT_STEPS + tail.STEPS))

        @block.scalar
        def _(a):
            credit(a, (front.xnT_ready, 1), (ct_moved, 2))
            front.scalar(a, 0, 0)

            def move(k, w):
                a.wait_ge(ct_ready, k + 1)
                a.wait_ge(ct_used, k + 1)
                nc.scalar.activation(CT[w % 2][:], ct_ps[w % 2][:], ACT.Copy).then_inc(ct_moved, 1)

            def group(n, u, more):
                for w in range(UG):
                    soft.scalar_exp(a, n * UG + w, w)
                    if w >= 2:
                        move(n * UG + w - 2, w - 2)
                    if w == UG // 2 and more:
                        front.scalar(a, n + 1, 1 - u)
                move(n * UG + UG - 2, UG - 2)
                move(n * UG + UG - 1, UG - 1)

            over_groups(a, group)

        @block.tensor
        def _(t):
            credit(t, (front.xn_used, 2), (front.xnT_used, 2), (soft.probs_used, soft.RING), (ct_used, 2))
            front.tensor(t, 0, 0)
            t.wait_ge(phi_in, 16)
            t.wait_ge(bias_ready, 1)

            def turn(k, w):
                t.wait_ge(soft.probs_ready, k + 1)
                t.wait_ge(ct_moved, k + 1)
                for c in range(4):
                    ins = nc.tensor.transpose(ct_ps[w % 2][:, c * 128:(c + 1) * 128],
                                              soft.E[w % soft.RING][:, c * 128:(c + 1) * 128], p.ident[:])
                ins.then_inc(ct_ready, 1)

            def combine(k, w):
                t.wait_ge(ct_moved, k + 3)
                j, q = w // NQ, w % NQ
                for c in range(4):
                    ins = nc.tensor.matmul(y_ps[:, j * 128:(j + 1) * 128], CT[w % 2][:, c * 128:(c + 1) * 128],
                                           Yt[:, 4 * q + c, :], start=(q == 0 and c == 0), stop=(q == 3 and c == 3))
                ins.then_inc(ct_used, 1)

            def group(n, u, more):
                t.wait_ge(front.xnT_ready, n + 2)
                for w in range(UG + 3):
                    if w < UG:
                        j = w // NQ
                        soft.tensor_logits(t, n * UG + w, w, front.xnT[u][:, j * 128:(j + 1) * 128], phiT, w % NQ, p)
                    if w == UG:
                        t.wait_ge(soft.logits_ready, (n + 1) * UG)
                        t.sem_inc(front.xnT_used, 1)
                    if 2 <= w < UG + 2:
                        turn(n * UG + w - 2, w - 2)
                        t.wait_ge(ct_ready, n * UG + w - 1)
                        t.sem_inc(soft.probs_used, 1)
                    if w == 3:
                        t.wait_ge(tail.var_ready, n + 1)
                    if w >= 3:
                        combine(n * UG + w - 3, w - 3)
                    if w == UG // 2 and more:
                        front.tensor(t, n + 1, 1 - u)
                t.wait_ge(ct_used, (n + 1) * UG + 2)
                t.sem_inc(y_ready, 1)
                t.sem_inc(front.xn_used, 1)

            over_groups(t, group)


NHG = 4
HW = NHG * HD


def stage_attn(nc, p, d, name, gate, rope, first):
    PRJ = 6 if rope else 4
    AUX = PRJ + 2
    with Stage(nc, name) as st:
        xn = [st.sb(f"xn{u}", [128, GB, D]) for u in range(2)]
        xnT = st.sb("xnT", [128, GD])
        cT = [st.sb(f"cT{u}", [128, GD]) for u in range(2)]
        wn = ["WqT", "WkT", "WvT", "WoT"] + (["WqrT", "WkrT"] if rope else [])
        W = {k: st.sb(k, [128, 128]) for k in wn}
        bn = ["bq", "bk", "bv"] + (["bqr", "bkr"] if rope else [])
        bias = {k: st.sb(k, [128, 1]) for k in bn}
        if rope:
            tab = {k: st.sb(k, [128, S]) for k in ("cosq", "sinq", "cosk", "sink")}
        bo, gcb, bvb = st.sb("bo", [128, 128]), st.sb("gcb", [128, 128]), st.sb("bvb", [128, 128])
        mi, mneg = st.sb("mi", [128, 128], I32), st.sb("mneg", [128, 128], BF16)
        t1, t2 = st.sb("t1", [128, GD]), st.sb("t2", [128, GD])
        hi = {k: st.sb(f"{k}hi", [128, GD], F32R) for k in "qk"}
        lo = {k: st.sb(f"{k}lo", [128, GD], F32R) for k in "qk"}
        QS = [st.sb(f"QS{u}", [3 * HW, NHG, GD], F32R) for u in range(2)]
        negm = st.sb("negm", [128, 2, NHG])
        sums = st.sb("sums", [128, 2, GB * H])
        E = [st.sb(f"E{i}", [128, 512]) for i in range(4)]
        PT = [st.sb(f"PT{i}", [128, 512]) for i in range(2)]
        R = st.sb("R", [128, GD])
        rT, OT = st.sb("rT", [128, GD]), st.sb("OT", [128, GD])
        tail = Tail(st, p)
        aux = [st.bank(f"aux{i}") for i in range(2)]
        sc = [st.bank(f"sc{i}") for i in range(2)]
        pt = [st.bank(f"pt{i}") for i in range(2)]
        po = [st.bank(f"po{i}") for i in range(2)]
        s = {k: st.sem(k) for k in (
            "w_in", "c_in0", "c_in1", "v_step", "xn_ready", "xnT_ready", "aux_full", "aux_free",
            "q_split", "k_split", "q_put", "k_put", "sc_ready", "max_ready", "exp_done",
            "pt_ready", "pt_moved", "av_done", "v_ready", "const_ready", "zeroed", "R_ready", "OT_ready", "exp_one")}
        s_qin = [st.sem(f"q_in{u}") for u in range(2)]
        s_kin = [st.sem(f"k_in{u}") for u in range(2)]
        NW = len(wn) + len(bn) + 2 + (4 if rope else 0)
        split_d = {k: [nc.dram_tensor(f"{name}_{k}split{u}", (2, 128, GD), F32, kind="Internal").ap() for u in range(2)]
                   for k in "qk"}

        def qcount(n, u):
            return (n - u) * (8 * 3) + 16 * 3

        def kcount(n, u):
            return (n - u) * (8 * 3 * NHG) + 16 * 3 * NHG

        block = st.block()

        @block.sync
        def _(sp):
            for k in wn:
                sp.dma_start(W[k][:], d[f"{name}_{k}"]).then_inc(s["w_in"], 16)
            for k in bn:
                sp.dma_start(bias[k][:], d[f"{name}_{k}"]).then_inc(s["w_in"], 16)
            if rope:
                for k in tab:
                    sp.dma_start(tab[k][:], d[k]).then_inc(s["w_in"], 16)
            sp.dma_start(bo[:], d[f"{name}_bo"].to_broadcast([128, 128])).then_inc(s["w_in"], 16)
            sp.dma_start(mi[:], d[f"{name}_mask"]).then_inc(s["w_in"], 16)

            def load_ctx(n, u):
                sp.dma_start(cT[u][:].rearrange("p (a d) -> p a d", a=GB), d["ctxT"][:, bass.ds(n * GB, GB), :])\
                    .then_inc(s["c_in0"] if u == 0 else s["c_in1"], 16)

            def spread(n, u):
                for k in "qk":
                    sp.wait_ge(s[k + "_split"], n + 1)
                    for i, part in enumerate((hi[k], lo[k])):
                        sp.dma_start(split_d[k][u][i], part[:].bitcast(F32)).then_inc(s[k + "_put"], 16)
                sp.wait_ge(s["q_put"], (n + 1) * 32)
                for r, i in enumerate((0, 0, 1)):
                    sp.dma_start(QS[u][r * HW:(r + 1) * HW, :, :].bitcast(F32),
                                 split_d["q"][u][i].rearrange("(g p) k -> p g k", g=NHG)).then_inc(s_qin[u], 16)
                sp.wait_ge(s["k_put"], (n + 1) * 32)
                for r, i in enumerate((0, 1, 0)):
                    for h4 in range(NHG):
                        sp.dma_start(p.KS[u][r * HW + h4 * HD:r * HW + (h4 + 1) * HD, :, h4, :].bitcast(F32),
                                     split_d["k"][u][i].rearrange("(g h p) k -> h p g k", g=NHG, h=NHG)[h4])\
                            .then_inc(s_kin[u], 16)

            load_ctx(0, 0)
            load_ctx(1, 1)
            sp.wait_ge(s["zeroed"], 2)
            spread(0, 0)

            with sp.Fori(0, NG // 2 - 1) as i:
                for u in range(2):
                    n = i * 2 + u
                    sp.wait_ge(s["aux_full"], (n + 1) * AUX)
                    load_ctx(n + 2, u)
                    sp.wait_ge(s["av_done"], n * UG + 2)
                    spread(n + 1, 1 - u)
            sp.wait_ge(s["av_done"], (NG - 2) * UG + 2)
            spread(NG - 1, 1)

        @block.gpsimd
        def _(g):
            if first:
                nc.gpsimd.memset(p.KS[0][:].bitcast(F32), 0.0)
                nc.gpsimd.memset(p.VZ[0][:], 0.0).then_inc(s["zeroed"], 1)
            else:
                g.sem_inc(s["zeroed"], 1)
            credit(g, (tail.rstd_done, 2))
            over_groups(g, lambda n, u, more: tail.gpsimd(g, n, u))

        @block.vector
        def _(v):
            steps = Steps(v, s["v_step"])
            credit(v, (s["aux_free"], 2), (tail.var_ready, 1), (s["pt_moved"], 2), (s["OT_ready"], 2))
            if first:
                nc.vector.memset(p.KS[1][:].bitcast(F32), 0.0)
                nc.vector.memset(p.VZ[1][:], 0.0).then_inc(s["zeroed"], 1)
            else:
                v.sem_inc(s["zeroed"], 1)
            v.wait_ge(s["zeroed"], 2)
            v.wait_ge(s["w_in"], 16 * NW)
            nc.vector.tensor_scalar(mneg[:], mi[:], 0.0, NEG, ALU.is_equal, ALU.mult)
            steps.link(nc.vector.tensor_copy(bvb[:], bias["bv"][:].to_broadcast([128, 128])))
            v.sem_inc(s["const_ready"], 1)

            def normalise(n, u):
                for j in range(GB):
                    b = n * GB + j
                    ins = nc.vector.tensor_scalar(xn[u][:, j, :], p.X[:, bass.ds(b, 1), :].rearrange("p a d -> p (a d)"),
                                                  p.mean[:, bass.ds(b, 1)], p.rstd[:, bass.ds(b, 1)],
                                                  ALU.subtract, ALU.mult)
                ins.then_inc(s["xn_ready"], 1)

            def split(k, src, n, u):
                steps.link(nc.vector.tensor_copy(hi[k][:], src[:]))
                nc.vector.tensor_tensor(lo[k][:], src[:], hi[k][:].bitcast(F32), ALU.subtract)\
                    .then_inc(s[k + "_split"], 1)
                v.wait_ge(s[k + "_split"], n + 1)

            def project(n, u, a0):
                v.wait_ge(s["aux_full"], a0 + 1)
                steps.link(nc.vector.tensor_copy(xnT[:], aux[0][:]))
                v.sem_inc(s["xnT_ready"], 1)
                v.sem_inc(s["aux_free"], 1)
                i = 1
                first_group = isinstance(n, int) and n == 0
                if not first_group:
                    v.wait_ge(s["q_put"], n * 32)
                    v.wait_ge(s["k_put"], n * 32)
                for k in "qk":
                    if rope:
                        v.wait_ge(s["aux_full"], a0 + i + 1)
                        nc.vector.scalar_tensor_tensor(
                            t1[:].rearrange("p (a s) -> p a s", a=GB), aux[i % 2][:].rearrange("p (a s) -> p a s", a=GB),
                            bias["b" + k][:, 0:1], tab["cos" + k][:].unsqueeze(1).to_broadcast([128, GB, S]),
                            ALU.add, ALU.mult).then_inc(s["aux_free"], 1)
                        v.wait_ge(s["aux_full"], a0 + i + 2)
                        nc.vector.scalar_tensor_tensor(
                            t2[:].rearrange("p (a s) -> p a s", a=GB), aux[(i + 1) % 2][:].rearrange("p (a s) -> p a s", a=GB),
                            bias["b" + k + "r"][:, 0:1], tab["sin" + k][:].unsqueeze(1).to_broadcast([128, GB, S]),
                            ALU.add, ALU.mult).then_inc(s["aux_free"], 1)
                        v.wait_ge(s["aux_free"], a0 + i + 4)
                        steps.link(nc.vector.tensor_tensor(t1[:], t1[:], t2[:], ALU.add))
                        i += 2
                    else:
                        v.wait_ge(s["aux_full"], a0 + i + 1)
                        steps.link(nc.vector.tensor_scalar(t1[:], aux[i % 2][:], bias["b" + k][:, 0:1],
                                                           HD ** -0.5 if k == "q" else 1.0, ALU.add, ALU.mult))
                        v.sem_inc(s["aux_free"], 1)
                        i += 1
                    split(k, t1, n, u)
                v.wait_ge(s["aux_full"], a0 + i + 1)
                if not first_group:
                    v.wait_ge(s["av_done"], (n - 1) * UG + 2)
                for j in range(GB):
                    vz = p.VZ[u][:, j, :]
                    diag = bass.AP(vz.tensor, vz.offset, [vz.ap[0], [NHG * HW, NHG], [HW + HD, NHG], [1, HD]])
                    ins = nc.vector.tensor_copy(diag, aux[i % 2][:, j * 128:(j + 1) * 128]
                                                .rearrange("p (g h d) -> p g h d", g=NHG, h=NHG))
                steps.link(ins)
                v.sem_inc(s["v_ready"], 1)
                v.sem_inc(s["aux_free"], 1)
                return i + 1

            def maximum(k, w, u):
                v.wait_ge(s["sc_ready"], k + 1)
                v.wait_ge(s["exp_done"], k + 1)
                steps.link(nc.vector.tensor_reduce(negm[:, w % 2, :], sc[w % 2][:].rearrange("p (h k) -> p h k", h=NHG),
                                                   AX.X, ALU.max, negate=True))
                v.sem_inc(s["max_ready"], 1)

            def move(k, w):
                v.wait_ge(s["pt_ready"], k + 5)
                v.wait_ge(s["av_done"], k + 1)
                nc.vector.tensor_copy(PT[w % 2][:], pt[w % 2][:]).then_inc(s["pt_moved"], 1)

            def finish(n, u, a0):
                v.wait_ge(s["exp_done"], (n + 1) * UG + 2)
                su = sums[:, u, :]
                steps.link(nc.vector.reciprocal(su, su))
                nc.vector.tensor_copy(R[:].rearrange("p (h d) -> p h d", d=HD),
                                      su.unsqueeze(2).to_broadcast([128, GB * H, HD])).then_inc(s["R_ready"], 1)
                v.wait_ge(s["aux_full"], a0 + 1)
                steps.link(nc.vector.tensor_copy(rT[:], aux[0][:]))
                v.sem_inc(s["aux_free"], 1)
                v.wait_ge(s["av_done"], (n + 1) * UG + 2)
                nc.vector.tensor_tensor(OT[:], po[u][:], rT[:], ALU.mult).then_inc(s["OT_ready"], 1)
                v.wait_ge(s["aux_full"], a0 + 2)
                xg = xgroup(p, n)
                steps.link(nc.vector.scalar_tensor_tensor(xg, aux[1][:].rearrange("p (a d) -> p a d", a=GB),
                                                          p.gate[:, gate:gate + 1], xg, ALU.mult, ALU.add))
                v.sem_inc(s["aux_free"], 1)
                tail.vector(v, n, u, steps, nc.vector.tensor_tensor(
                    xg, xg, gcb[:].unsqueeze(1).to_broadcast([128, GB, D]), ALU.add))


            normalise(0, 0)
            v.wait_ge(s["aux_full"], 1)
            steps.link(nc.vector.tensor_tensor(gcb[:], aux[0][:, 0:128], bo[:], ALU.add))
            v.sem_inc(s["aux_free"], 1)
            steps.link(nc.vector.tensor_scalar(gcb[:], gcb[:], p.gate[:, gate:gate + 1], None, ALU.mult))
            v.wait_ge(s["aux_full"], 2)
            v.sem_inc(s["aux_free"], 1)
            pro = project(0, 0, 2)
            assert pro == PRJ

            def group(n, u, more):
                for w in range(UG + 3):
                    if w < UG:
                        maximum(n * UG + w, w, u)
                    if w >= 3:
                        move(n * UG + w - 3, w - 3)
                    if w == 2 and more:
                        normalise(n + 1, 1 - u)
                    if w == 6 and more:
                        project(n + 1, 1 - u, (n + 1) * AUX)
                finish(n, u, (n + 1) * AUX + (PRJ if more else 0))

            over_groups(v, group, steps, 2 * (UG + 6 + 3 + tail.STEPS))

        @block.scalar
        def _(a):
            credit(a, (s["exp_done"], 2))

            def group(n, u, more):
                for w in range(UG):
                    k = n * UG + w
                    j, hg = w // NHG, w % NHG
                    a.wait_ge(s["max_ready"], k + 1)
                    a.wait_ge(s["pt_ready"], k + 1)
                    for h in range(NHG):
                        col = j * H + hg * NHG + h
                        nc.scalar.activation(E[w % 4][:, h * 128:(h + 1) * 128], sc[w % 2][:, h * 128:(h + 1) * 128],
                                             ACT.Exp, bias=negm[:, w % 2, h:h + 1],
                                             accum_out=sums[:, u, col:col + 1]).then_inc(s["exp_one"], 1)
                    a.wait_ge(s["exp_one"], (k + 1) * NHG)
                    a.sem_inc(s["exp_done"], 1)

            over_groups(a, group)

        @block.tensor
        def _(t):
            credit(t, (s["av_done"], 2), (s["pt_ready"], 4))
            t.wait_ge(s["w_in"], 16 * NW)
            t.wait_ge(s["const_ready"], 1)
            t.wait_ge(s["aux_free"], 1)
            nc.tensor.matmul(aux[0][:, 0:128], bvb[:], W["WoT"][:], start=True, stop=True).then_inc(s["aux_full"], 1)
            t.wait_ge(s["aux_free"], 2)
            nc.tensor.matmul(aux[1][:, 0:128], bvb[:], W["WoT"][:], start=True, stop=True).then_inc(s["aux_full"], 1)

            def project(n, u, a0):
                i = 0

                def free():
                    t.wait_ge(s["aux_free"], a0 + i + 1)
                t.wait_ge(s["xn_ready"], n + 1)
                free()
                for j in range(GB):
                    ins = nc.tensor.transpose(aux[i % 2][:, j * 128:(j + 1) * 128], xn[u][:, j, :], p.ident[:])
                ins.then_inc(s["aux_full"], 1)
                i += 1
                t.wait_ge(s["c_in0"] if u == 0 else s["c_in1"], (n - u) * 8 + 16)
                t.wait_ge(s["xnT_ready"], n + 1)
                for w, src in (("WqT", xnT), ("WqrT", xnT), ("WkT", cT[u]), ("WkrT", cT[u])):
                    if w in W:
                        free()
                        nc.tensor.matmul(aux[i % 2][:], W[w][:], src[:], start=True, stop=True).then_inc(s["aux_full"], 1)
                        i += 1
                free()
                for j in range(GB):
                    ins = nc.tensor.matmul(aux[i % 2][:, j * 128:(j + 1) * 128], cT[u][:, j * 128:(j + 1) * 128],
                                           W["WvT"][:], start=True, stop=True)
                ins.then_inc(s["aux_full"], 1)

            def finish(n, u, a0):
                t.wait_ge(s["R_ready"], n + 1)
                t.wait_ge(s["aux_free"], a0 + 1)
                for j in range(GB):
                    ins = nc.tensor.transpose(aux[0][:, j * 128:(j + 1) * 128], R[:, j * 128:(j + 1) * 128], p.ident[:])
                ins.then_inc(s["aux_full"], 1)
                t.wait_ge(s["OT_ready"], n + 3)
                t.wait_ge(s["aux_free"], a0 + 2)
                for j in range(GB):
                    ins = nc.tensor.matmul(aux[1][:, j * 128:(j + 1) * 128], OT[:, j * 128:(j + 1) * 128], W["WoT"][:],
                                           start=True, stop=True)
                ins.then_inc(s["aux_full"], 1)

            def scores(k, w, u):
                j, hg = w // NHG, w % NHG
                t.wait_ge(s["exp_done"], k + 1)
                nc.tensor.matmul(sc[w % 2][:], QS[u][:, hg, j * 128:(j + 1) * 128],
                                 p.KS[u][:, hg, :, j * 128:(j + 1) * 128], start=True, stop=False)
                nc.tensor.matmul(sc[w % 2][:], p.ident16[:], mneg[:].unsqueeze(1).to_broadcast([128, NHG, 128]),
                                 start=False, stop=True).then_inc(s["sc_ready"], 1)

            def turn(k, w):
                t.wait_ge(s["exp_done"], k + 3)
                t.wait_ge(s["pt_moved"], k + 1)
                for c in range(NHG):
                    ins = nc.tensor.transpose(pt[w % 2][:, c * 128:(c + 1) * 128], E[w % 4][:, c * 128:(c + 1) * 128],
                                              p.ident[:])
                ins.then_inc(s["pt_ready"], 1)

            def attend(k, w, u):
                j, hg = w // NHG, w % NHG
                t.wait_ge(s["pt_moved"], k + 3)
                for c in range(NHG):
                    h = hg * NHG + c
                    ins = nc.tensor.matmul(po[u][hg * HW:(hg + 1) * HW, j * 128:(j + 1) * 128],
                                           p.VZ[u][:, j, h * HW:(h + 1) * HW],
                                           PT[w % 2][:, c * 128:(c + 1) * 128], start=(c == 0), stop=(c == NHG - 1))
                ins.then_inc(s["av_done"], 1)

            project(0, 0, 2)

            def group(n, u, more):
                t.wait_ge(s_qin[u], qcount(n, u))
                t.wait_ge(s_kin[u], kcount(n, u))
                t.wait_ge(s["v_ready"], n + 1)
                t.wait_ge(s["OT_ready"], n + 1)
                for w in range(UG + 3):
                    k = n * UG + w
                    if w < UG:
                        scores(k, w, u)
                    if 2 <= w < UG + 2:
                        turn(k - 2, w - 2)
                    if w >= 3:
                        attend(k - 3, w - 3, u)
                    if w == 6 and more:
                        project(n + 1, 1 - u, (n + 1) * AUX)
                finish(n, u, (n + 1) * AUX + (PRJ if more else 0))

            over_groups(t, group)


LOW, TAKEN = -3.0e38, -3.3e38


class Router:
    STEPS = 9

    def __init__(self, st, p, name, ne, over_chosen):
        self.st, self.p, self.name, self.ne, self.over_chosen = st, p, name, ne, over_chosen
        self.W = st.sb("rW", [128, ne])
        self.b = st.sb("rb", [128, ne])
        self.L = st.sb("rL", [128, GB, ne + 8])
        self.mr = st.sb("rmr", [128, GB, ne + 8])
        self.top, self.rv = st.sb("rtop", [128, GB, 8]), st.sb("rrv", [128, GB, 8])
        self.E, self.r = st.sb("rE", [128, GB, ne]), st.sb("rr", [128, GB])
        self.G = [st.sb(f"G{u}", [128, GB, ne]) for u in range(2)]
        self.GT = [st.sb(f"GT{u}", [128, 128]) for u in range(2)]
        self.ps = st.bank("route")
        s = lambda k: st.sem("route_" + k)
        self.in_, self.logits, self.diff, self.exp = s("in"), s("logits"), s("diff"), s("exp")
        self.waited, self.turn_waited = s("waited"), s("turn_waited")
        self.G_ready, self.GT_ps, self.GT_ready, self.G_used = s("G_ready"), s("GT_ps"), s("GT_ready"), s("G_used")

    def load(self, eng, d):
        eng.dma_start(self.W[:], d[self.name + "_rW"]).then_inc(self.in_, 16)
        eng.dma_start(self.b[:], d[self.name + "_rb"].to_broadcast([128, self.ne])).then_inc(self.in_, 16)

    def start(self, eng, steps):
        nc = self.st.nc
        nc.vector.memset(self.L[:], LOW)
        steps.link(nc.vector.memset(self.rv[:], LOW))
        eng.wait_ge(self.in_, 32)

    def tensor(self, eng, n, xT):
        nc = self.st.nc
        eng.wait_ge(self.GT_ready, n + 1)
        for j in range(GB):
            ins = nc.tensor.matmul(self.ps[:, j * self.ne:(j + 1) * self.ne], xT[:, j * 128:(j + 1) * 128], self.W[:],
                                   start=True, stop=True)
        ins.then_inc(self.logits, 1)

    def vector(self, eng, n, u, steps):
        nc, ne = self.st.nc, self.ne
        L = self.L[:, :, 0:ne]
        eng.wait_ge(self.logits, n + 1)
        steps.link(nc.vector.tensor_tensor(L, self.ps[:, 0:GB * ne].rearrange("p (a e) -> p a e", a=GB),
                                           self.b[:].unsqueeze(1).to_broadcast([128, GB, ne]), ALU.add))
        stand(eng, self.waited)
        for j in range(GB):
            ins = nc.vector.max(self.top[:, j, :], self.L[:, j, 0:ne])
        steps.link(ins)
        nc.vector.tensor_tensor(self.E[:], L, self.top[:, :, 0:1].to_broadcast([128, GB, ne]), ALU.subtract)\
            .then_inc(self.diff, 1)
        steps.link(nc.vector.tensor_copy(self.rv[:, :, 0:TOPK], self.top[:, :, 0:TOPK]))
        stand(eng, self.waited)
        for j in range(GB):
            ins = nc.vector.match_replace(out=self.mr[:, j, :], in_to_replace=self.rv[:, j, :],
                                          in_values=self.L[:, j, :], imm_value=TAKEN)
        steps.link(ins)
        eng.wait_ge(self.exp, n + 1)
        if not self.over_chosen:
            steps.link(nc.vector.tensor_reduce(self.r[:], self.E[:], AX.X, ALU.add))
        steps.link(nc.vector.scalar_tensor_tensor(self.E[:], self.mr[:, :, 0:ne], TAKEN, self.E[:],
                                                  ALU.is_equal, ALU.mult))
        if self.over_chosen:
            steps.link(nc.vector.tensor_reduce(self.r[:], self.E[:], AX.X, ALU.add))
        steps.link(nc.vector.reciprocal(self.r[:], self.r[:]))
        nc.vector.tensor_tensor(self.G[u][:], self.E[:], self.r[:].unsqueeze(2).to_broadcast([128, GB, ne]), ALU.mult)\
            .then_inc(self.G_ready, 1)
        eng.wait_ge(self.G_ready, n + 1)

    VSTEPS = 7

    def scalar_exp(self, eng, n):
        eng.wait_ge(self.diff, n + 1)
        self.st.nc.scalar.activation(self.E[:], self.E[:], ACT.Exp).then_inc(self.exp, 1)

    def tensor_turn(self, eng, n, u):
        eng.wait_ge(self.G_ready, n + 1)
        stand(eng, self.turn_waited)
        self.st.nc.tensor.transpose(self.ps[0:GB * self.ne, 128:256], self.G[u][:].rearrange("p a e -> p (a e)"),
                                    self.p.ident[:]).then_inc(self.GT_ps, 1)

    def scalar_turn(self, eng, n, u):
        eng.wait_ge(self.GT_ps, n + 1)
        k = GB * self.ne
        self.st.nc.scalar.activation(self.GT[u][0:k, :], self.ps[0:k, 128:256], ACT.Copy).then_inc(self.GT_ready, 1)


def stage_l1_ffn(nc, p, d):
    with Stage(nc, "F1") as st:
        front, tail = Front(st, p), Tail(st, p)
        rt = Router(st, p, "L1F", NR, False)
        WrT = st.sb("WrT", [128, NR, 128])
        Ws = st.sb("Ws", [128, 2, 128])
        blk = st.sb("blk", [GB * NR + 1, GD])
        bs = st.sb("bs", [65, 2, 128])
        acc = st.sb("acc", [128, GB, D])
        EB = 4
        eb, sh = [st.bank(f"e{i}") for i in range(EB)], st.bank("shared")
        s = {k: st.sem(k) for k in ("w_in", "blk_in", "zeroed", "v_step", "ws_ready", "e_ready", "e_used", "xn_done")}
        block = st.block()

        @block.sync
        def _(sp):
            sp.dma_start(Ws[:], d["L1F_WsT"]).then_inc(s["w_in"], 16)
            sp.dma_start(bs[64:65, :, :], d["L1F_bs"]).then_inc(s["w_in"], 16)
            rt.load(sp, d)
            sp.dma_start(WrT[:], d["L1F_WrT"]).then_inc(s["w_in"], 16)
            sp.wait_ge(s["zeroed"], 1)
            for j in range(GB):
                sp.dma_start(blk[j * NR:(j + 1) * NR, j * D:(j + 1) * D], d["L1F_br"]).then_inc(s["blk_in"], 16)

        @block.gpsimd
        def _(g):
            nc.gpsimd.memset(blk[:], 0.0).then_inc(s["zeroed"], 1)
            credit(g, (tail.rstd_done, 2))
            over_groups(g, lambda n, u, more: tail.gpsimd(g, n, u))

        @block.vector
        def _(v):
            steps = Steps(v, s["v_step"])
            credit(v, (tail.var_ready, 1), (s["e_used"], EB + 1))
            rt.start(v, steps)
            front.vector(v, 0, 0)
            nc.vector.memset(rt.GT[0][64:65, :], 1.0)
            nc.vector.memset(rt.GT[1][64:65, :], 1.0)
            v.wait_ge(s["w_in"], 48)
            v.wait_ge(s["zeroed"], 1)
            steps.link(nc.vector.tensor_tensor(Ws[:, 0, :], Ws[:, 0, :], Ws[:, 1, :], ALU.add))
            steps.link(nc.vector.tensor_scalar(Ws[:, 0, :], Ws[:, 0, :], 0.5, None, ALU.mult))
            steps.link(nc.vector.tensor_tensor(bs[64:65, 0, :], bs[64:65, 0, :], bs[64:65, 1, :], ALU.add))
            steps.link(nc.vector.tensor_scalar(blk[64:65, :].rearrange("p (a o) -> p a o", a=GB),
                                               bs[64:65, 0:1, :].to_broadcast([1, GB, D]), 0.5, None, ALU.mult))
            v.sem_inc(s["ws_ready"], 1)
            rt.vector(v, 0, 0, steps)

            def group(n, u, more):
                xg = xgroup(p, n)
                k = n * (NR + 1)
                v.wait_ge(s["e_ready"], k + 1)
                steps.link(nc.vector.tensor_tensor(acc[:], sh[:].rearrange("p (a o) -> p a o", a=GB), front.xn[u][:], ALU.add))
                v.sem_inc(s["e_used"], 1)
                for e in range(NR):
                    v.wait_ge(s["e_ready"], k + e + 2)
                    for j in range(GB):
                        ins = nc.vector.scalar_tensor_tensor(acc[:, j, :], eb[e % EB][:, j * 128:(j + 1) * 128],
                                                             rt.G[u][:, j, e:e + 1], acc[:, j, :], ALU.mult, ALU.add)
                    ins.then_inc(s["e_used"], 1)
                    v.wait_ge(s["e_used"], EB + 1 + k + e + 2)
                    if e == 4 and more:
                        front.vector(v, n + 1, 1 - u)
                    if e == 9 and more:
                        rt.vector(v, n + 1, 1 - u, steps)
                tail.vector(v, n, u, steps, nc.vector.scalar_tensor_tensor(xg, acc[:], p.gate[:, 5:6], xg, ALU.mult, ALU.add))

            over_groups(v, group, steps, 2 * (1 + rt.VSTEPS + tail.STEPS))

        @block.scalar
        def _(a):
            credit(a, (front.xnT_ready, 1), (rt.GT_ready, 1))
            front.scalar(a, 0, 0)
            rt.scalar_exp(a, 0)
            rt.scalar_turn(a, 0, 0)

            def group(n, u, more):
                if more:
                    front.scalar(a, n + 1, 1 - u)
                    rt.scalar_exp(a, n + 1)
                    rt.scalar_turn(a, n + 1, 1 - u)

            over_groups(a, group)

        @block.tensor
        def _(t):
            credit(t, (front.xn_used, 2), (front.xnT_used, 2))
            front.tensor(t, 0, 0)
            t.wait_ge(s["w_in"], 48)
            t.wait_ge(s["blk_in"], 64)
            t.wait_ge(s["ws_ready"], 1)
            t.wait_ge(front.xnT_ready, 2)
            rt.tensor(t, 0, front.xnT[0])
            rt.tensor_turn(t, 0, 0)

            def group(n, u, more):
                k = n * (NR + 1)
                t.wait_ge(rt.GT_ready, n + 2)
                t.wait_ge(s["e_used"], k + 2)
                for j in range(GB):
                    nc.tensor.matmul(sh[:, j * 128:(j + 1) * 128], front.xnT[u][:, j * 128:(j + 1) * 128], Ws[:, 0, :],
                                     start=(j == 0), stop=False, skip_group_check=True)
                nc.tensor.matmul(sh[:], rt.GT[u][0:65, :], blk[:], start=False, stop=True, skip_group_check=True)\
                    .then_inc(s["e_ready"], 1)
                for e in range(NR):
                    t.wait_ge(s["e_used"], k + e + 3)
                    for j in range(GB):
                        ins = nc.tensor.matmul(eb[e % EB][:, j * 128:(j + 1) * 128],
                                               front.xnT[u][:, j * 128:(j + 1) * 128], WrT[:, e, :], start=True, stop=True)
                    ins.then_inc(s["e_ready"], 1)
                    if e == 6 and more:
                        front.tensor(t, n + 1, 1 - u)
                    if e == 8 and more:
                        t.wait_ge(front.xnT_ready, n + 3)
                        rt.tensor(t, n + 1, front.xnT[1 - u])
                    if e == 13 and more:
                        rt.tensor_turn(t, n + 1, 1 - u)
                t.wait_ge(s["e_ready"], k + NR + 1)
                t.sem_inc(front.xnT_used, 1)
                t.sem_inc(front.xn_used, 1)

            over_groups(t, group)


def stage_l2_attn(nc, p, d):
    SCALE = float(np.sqrt(D // 16))
    with Stage(nc, "A2") as st:
        front, tail = Front(st, p), Tail(st, p)
        cT, cN = st.sb("cT", [128, B, S]), st.sb("cN", [128, B, D])
        negm, sums = st.sb("negm", [128, GB]), st.sb("sums", [128, GB])
        E, PT = st.sb("E", [128, GD]), st.sb("PT", [128, GD])
        sc, pt, po = st.bank("sc"), st.bank("pt"), st.bank("po")
        s = {k: st.sem(k) for k in ("c_in", "v_step", "sc_ready", "max_ready", "exp_done", "pt_ready", "pt_moved", "po_ready")}
        block = st.block()

        @block.sync
        def _(sp):
            sp.dma_start(cT[:], d["ctxT"]).then_inc(s["c_in"], 16)
            sp.dma_start(cN[:], d["ctx"]).then_inc(s["c_in"], 16)

        @block.gpsimd
        def _(g):
            credit(g, (tail.rstd_done, 2))
            over_groups(g, lambda n, u, more: tail.gpsimd(g, n, u))

        @block.vector
        def _(v):
            steps = Steps(v, s["v_step"])
            credit(v, (tail.var_ready, 1), (s["pt_moved"], 1))
            front.vector(v, 0, 0)

            def group(n, u, more):
                xg = xgroup(p, n)
                v.wait_ge(s["sc_ready"], n + 1)
                steps.link(nc.vector.tensor_reduce(negm[:], sc[:].rearrange("p (a k) -> p a k", a=GB), AX.X, ALU.max, negate=True))
                steps.link(nc.vector.tensor_scalar(negm[:], negm[:], SCALE, None, ALU.mult))
                v.sem_inc(s["max_ready"], 1)
                if more:
                    front.vector(v, n + 1, 1 - u)
                v.wait_ge(s["pt_ready"], n + 1)
                nc.vector.tensor_copy(PT[:], pt[:]).then_inc(s["pt_moved"], 1)
                steps.link(nc.vector.reciprocal(sums[:], sums[:]))
                steps.link(nc.vector.tensor_scalar(sums[:], sums[:], p.gate[:, 2:3], None, ALU.mult))
                v.wait_ge(s["po_ready"], n + 1)
                for j in range(GB):
                    xj = p.X[:, bass.ds(n * GB + j, 1), :].rearrange("p a d -> p (a d)")
                    ins = nc.vector.scalar_tensor_tensor(xj, po[:, j * 128:(j + 1) * 128], sums[:, j:j + 1], xj, ALU.mult, ALU.add)
                tail.vector(v, n, u, steps, ins)

            over_groups(v, group, steps, 2 * (4 + tail.STEPS))

        @block.scalar
        def _(a):
            credit(a, (front.xnT_ready, 1))
            front.scalar(a, 0, 0)

            def group(n, u, more):
                a.wait_ge(s["max_ready"], n + 1)
                for j in range(GB):
                    ins = nc.scalar.activation(E[:, j * 128:(j + 1) * 128], sc[:, j * 128:(j + 1) * 128], ACT.Exp,
                                               bias=negm[:, j:j + 1], scale=SCALE, accum_out=sums[:, j:j + 1])
                    ins.then_inc(s["exp_done"], 1)
                if more:
                    front.scalar(a, n + 1, 1 - u)

            over_groups(a, group)

        @block.tensor
        def _(t):
            credit(t, (front.xn_used, 2), (front.xnT_used, 2))
            front.tensor(t, 0, 0)
            t.wait_ge(s["c_in"], 32)

            def group(n, u, more):
                t.wait_ge(front.xnT_ready, n + 2)
                for j in range(GB):
                    ins = nc.tensor.matmul(sc[:, j * 128:(j + 1) * 128], front.xnT[u][:, j * 128:(j + 1) * 128],
                                           cT[:, bass.ds(n * GB + j, 1), :].rearrange("p a k -> p (a k)"), start=True, stop=True)
                ins.then_inc(s["sc_ready"], 1)
                if more:
                    front.tensor(t, n + 1, 1 - u)
                t.wait_ge(s["exp_done"], (n + 1) * GB)
                t.sem_inc(front.xn_used, 1)
                t.sem_inc(front.xnT_used, 1)
                t.wait_ge(s["pt_moved"], n + 1)
                for j in range(GB):
                    ins = nc.tensor.transpose(pt[:, j * 128:(j + 1) * 128], E[:, j * 128:(j + 1) * 128], p.ident[:])
                ins.then_inc(s["pt_ready"], 1)
                t.wait_ge(s["pt_moved"], n + 2)
                t.wait_ge(tail.var_ready, n + 1)
                for j in range(GB):
                    ins = nc.tensor.matmul(po[:, j * 128:(j + 1) * 128], PT[:, j * 128:(j + 1) * 128],
                                           cN[:, bass.ds(n * GB + j, 1), :].rearrange("p a k -> p (a k)"), start=True, stop=True)
                ins.then_inc(s["po_ready"], 1)

            over_groups(t, group)


def stage_l2_route(nc, p, d):
    with Stage(nc, "R2") as st:
        front = Front(st, p)
        W = st.sb("W", [128, NX])
        E, m = st.sb("E", [128, GB, NX]), st.sb("m", [128, GB])
        work = [st.sb(f"work{i}", [128, S]) for i in range(2)]
        PT = [st.sb(f"PT{i}", [128, S]) for i in range(2)]
        top = st.sb("top", [128, 2, 8])
        ps, tp = st.bank("ps"), st.bank("tp")
        s = {k: st.sem(k) for k in ("w_in", "v_step", "logits", "diff", "exp", "P_ready", "t1", "t2", "G_ready")}
        block = st.block()

        @block.sync
        def _(sp):
            sp.dma_start(W[:], d["L2_gate_w"]).then_inc(s["w_in"], 16)

        @block.vector
        def _(v):
            steps = Steps(v, s["v_step"])
            credit(v, (s["P_ready"], 1))
            front.vector(v, 0, 0)

            def group(n, u, more):
                if more:
                    front.vector(v, n + 1, 1 - u)
                v.wait_ge(s["logits"], n + 1)
                lg = ps[:, 0:GB * NX].rearrange("p (a e) -> p a e", a=GB)
                steps.link(nc.vector.tensor_reduce(m[:], lg, AX.X, ALU.max))
                nc.vector.tensor_tensor(E[:], lg, m[:].unsqueeze(2).to_broadcast([128, GB, NX]), ALU.subtract)\
                    .then_inc(s["diff"], 1)
                v.wait_ge(s["exp"], n + 1)
                steps.link(nc.vector.tensor_reduce(m[:], E[:], AX.X, ALU.add))
                steps.link(nc.vector.reciprocal(m[:], m[:]))
                nc.vector.tensor_tensor(p.G2[:, bass.ds(n * GB, GB), :], E[:], m[:].unsqueeze(2).to_broadcast([128, GB, NX]),
                                        ALU.mult).then_inc(s["P_ready"], 1)
                v.wait_ge(s["P_ready"], n + 2)

            over_groups(v, group, steps, 2 * 3)
            v.wait_ge(s["t1"], 1)
            for i in range(2):
                nc.vector.tensor_copy(work[i][:], tp[:, i * 128:(i + 1) * 128])
                ins = nc.vector.tensor_copy(PT[i][:], tp[:, i * 128:(i + 1) * 128])
            steps.link(ins)
            for r in range(CAP // 8):
                for i in range(2):
                    ins = nc.vector.max(top[:, i, :], work[i][:])
                steps.link(ins)
                for i in range(2):
                    ins = nc.vector.match_replace(out=work[i][:], in_to_replace=top[:, i, :], in_values=work[i][:],
                                                  imm_value=-1.0)
                steps.link(ins)
            for i in range(2):
                ins = nc.vector.scalar_tensor_tensor(PT[i][:], work[i][:], -1.0, PT[i][:], ALU.is_equal, ALU.mult)
            steps.link(ins)
            v.sem_inc(s["G_ready"], 1)
            v.wait_ge(s["t2"], 1)
            for i in range(2):
                ins = nc.vector.tensor_copy(p.G2[:, i * 16:(i + 1) * 16, :],
                                            tp[:, 256 + i * 128:256 + (i + 1) * 128].rearrange("p (a e) -> p a e", e=NX))
            steps.link(ins)

        @block.scalar
        def _(a):
            credit(a, (front.xnT_ready, 1))
            front.scalar(a, 0, 0)

            def group(n, u, more):
                if more:
                    front.scalar(a, n + 1, 1 - u)
                a.wait_ge(s["diff"], n + 1)
                nc.scalar.activation(E[:], E[:], ACT.Exp).then_inc(s["exp"], 1)

            over_groups(a, group)

        @block.tensor
        def _(t):
            credit(t, (front.xn_used, 2), (front.xnT_used, 2))
            front.tensor(t, 0, 0)
            t.wait_ge(s["w_in"], 16)

            def group(n, u, more):
                t.wait_ge(front.xnT_ready, n + 2)
                if more:
                    front.tensor(t, n + 1, 1 - u)
                t.wait_ge(s["P_ready"], n + 1)
                for j in range(GB):
                    ins = nc.tensor.matmul(ps[:, j * NX:(j + 1) * NX], front.xnT[u][:, j * 128:(j + 1) * 128], W[:],
                                           start=True, stop=True)
                ins.then_inc(s["logits"], 1)
                t.wait_ge(s["logits"], n + 1)
                t.sem_inc(front.xn_used, 1)
                t.sem_inc(front.xnT_used, 1)

            over_groups(t, group)
            t.wait_ge(s["P_ready"], NG + 1)
            for i in range(2):
                ins = nc.tensor.transpose(tp[:, i * 128:(i + 1) * 128],
                                          p.G2[:, i * 16:(i + 1) * 16, :].rearrange("p a e -> p (a e)"), p.ident[:])
            ins.then_inc(s["t1"], 1)
            t.wait_ge(s["G_ready"], 1)
            for i in range(2):
                ins = nc.tensor.transpose(tp[:, 256 + i * 128:256 + (i + 1) * 128], PT[i][:], p.ident[:])
            ins.then_inc(s["t2"], 1)


def stage_ffn(nc, p, d, name, gate, routed):
    with Stage(nc, name) as st:
        front, tail = Front(st, p), Tail(st, p)
        rt = Router(st, p, name, NX, True) if routed else None
        w1, w2 = st.sb("w1", [128, NX, FF]), st.sb("w2", [128, NX, FC, 128])
        b1 = st.sb("b1", [128, NX, FC])
        blk = st.sb("blk", [GB * NX, GD])
        hT = [st.sb(f"hT{i}", [128, GD]) for i in range(2 * FC)]
        acc = st.sb("acc", [128, GB, D])
        hb = [st.bank(f"h{i}") for i in range(2)]
        yb = [st.bank(f"y{i}") for i in range(2)]
        ib = st.bank("init")
        s = {k: st.sem(k) for k in ("w_in", "blk_in", "zeroed", "v_step", "h_ps", "h_ready", "y_ready", "y_used",
                                    "init_ready", "init_used")}
        NH = NX * FC
        block = st.block()

        @block.sync
        def _(sp):
            if routed:
                rt.load(sp, d)
                sp.dma_start(b1[:], d[name + "_b1"]).then_inc(s["w_in"], 16)
                sp.wait_ge(s["zeroed"], 1)
                for j in range(GB):
                    sp.dma_start(blk[j * NX:(j + 1) * NX, j * D:(j + 1) * D], d[name + "_b2"]).then_inc(s["blk_in"], 16)
            sp.dma_start(w1[:], d[name + "_w1"]).then_inc(s["w_in"], 16)
            sp.dma_start(w2[:], d[name + "_w2"]).then_inc(s["w_in"], 16)

        @block.gpsimd
        def _(g):
            nc.gpsimd.memset(blk[:], 0.0).then_inc(s["zeroed"], 1)
            credit(g, (tail.rstd_done, 2))
            over_groups(g, lambda n, u, more: tail.gpsimd(g, n, u))

        @block.vector
        def _(v):
            steps = Steps(v, s["v_step"])
            credit(v, (tail.var_ready, 1), (s["y_used"], 2), (s["init_used"], 1))
            front.vector(v, 0, 0)
            if routed:
                rt.start(v, steps)
                rt.vector(v, 0, 0, steps)

            def group(n, u, more):
                xg = xgroup(p, n)
                if routed:
                    v.wait_ge(s["init_ready"], n + 1)
                    steps.link(nc.vector.tensor_copy(acc[:], ib[:].rearrange("p (a o) -> p a o", a=GB)))
                    v.sem_inc(s["init_used"], 1)
                for e in range(NX):
                    k = n * NX + e
                    v.wait_ge(s["y_ready"], k + 3)
                    for j in range(GB):
                        y = yb[e % 2][:, j * 128:(j + 1) * 128]
                        if routed:
                            g = rt.G[u][:, j, e:e + 1]
                        else:
                            g = p.G2[:, bass.ds(n * GB + j, 1), e:e + 1].rearrange("p a e -> p (a e)")
                        if routed or e:
                            ins = nc.vector.scalar_tensor_tensor(acc[:, j, :], y, g, acc[:, j, :], ALU.mult, ALU.add)
                        else:
                            ins = nc.vector.tensor_scalar(acc[:, j, :], y, g, None, ALU.mult)
                    ins.then_inc(s["y_used"], 1)
                    v.wait_ge(s["y_used"], k + 3)
                    if e == 1 and more:
                        front.vector(v, n + 1, 1 - u)
                    if e == 3 and more and routed:
                        rt.vector(v, n + 1, 1 - u, steps)
                tail.vector(v, n, u, steps, nc.vector.scalar_tensor_tensor(xg, acc[:], p.gate[:, gate:gate + 1], xg,
                                                                           ALU.mult, ALU.add))

            over_groups(v, group, steps, 2 * (tail.STEPS + ((1 + rt.VSTEPS) if routed else 0)))

        @block.scalar
        def _(a):
            credit(a, (front.xnT_ready, 1), (s["h_ready"], 2))
            if routed:
                a.sem_inc(rt.GT_ready, 1)
            front.scalar(a, 0, 0)
            if routed:
                rt.scalar_exp(a, 0)
                rt.scalar_turn(a, 0, 0)
            a.wait_ge(s["w_in"], 48 if routed else 32)

            def group(n, u, more):
                for e in range(NX):
                    for c in range(FC):
                        k = n * NH + e * FC + c
                        if c == 0:
                            a.wait_ge(s["y_ready"], n * NX + e + 1)
                        a.wait_ge(s["h_ps"], k + 1)
                        nc.scalar.activation(hT[(e % 2) * FC + c][:], hb[c % 2][:], ACT.Gelu,
                                             bias=b1[:, e, c:c + 1] if routed else 0.0).then_inc(s["h_ready"], 1)
                    if e == 2 and more:
                        front.scalar(a, n + 1, 1 - u)
                    if e == 4 and more and routed:
                        rt.scalar_exp(a, n + 1)
                    if e == 5 and more and routed:
                        rt.scalar_turn(a, n + 1, 1 - u)

            over_groups(a, group)

        @block.tensor
        def _(t):
            credit(t, (front.xn_used, 2), (front.xnT_used, 2), (s["y_ready"], 2))
            front.tensor(t, 0, 0)
            t.wait_ge(front.xnT_ready, 2)
            if routed:
                rt_in = rt.in_
                t.wait_ge(rt_in, 32)
                rt.tensor(t, 0, front.xnT[0])
                rt.tensor_turn(t, 0, 0)
                t.wait_ge(s["blk_in"], 64)
            t.wait_ge(s["w_in"], 48 if routed else 32)

            def second(n, e):
                k = n * NX + e
                t.wait_ge(s["h_ready"], k * FC + FC + 2)
                t.wait_ge(s["y_used"], k + 1)
                for j in range(GB):
                    for c in range(FC):
                        ins = nc.tensor.matmul(yb[e % 2][:, j * 128:(j + 1) * 128],
                                               hT[(e % 2) * FC + c][:, j * 128:(j + 1) * 128], w2[:, e, c, :],
                                               start=(c == 0), stop=(c == FC - 1))
                ins.then_inc(s["y_ready"], 1)

            def group(n, u, more):
                t.wait_ge(front.xnT_ready, n + 2)
                if routed:
                    t.wait_ge(rt.GT_ready, n + 2)
                    t.wait_ge(s["init_used"], n + 1)
                    nc.tensor.matmul(ib[:], rt.GT[u][0:GB * NX, :], blk[:], start=True, stop=True).then_inc(s["init_ready"], 1)
                for e in range(NX):
                    for c in range(FC):
                        k = n * NH + e * FC + c
                        t.wait_ge(s["h_ready"], k + 1)
                        nc.tensor.matmul(hb[c % 2][:], w1[:, e, c * 128:(c + 1) * 128], front.xnT[u][:],
                                         start=True, stop=True).then_inc(s["h_ps"], 1)
                    if e:
                        second(n, e - 1)
                    if e == 2 and more:
                        front.tensor(t, n + 1, 1 - u)
                    if e == 3 and more and routed:
                        t.wait_ge(front.xnT_ready, n + 3)
                        rt.tensor(t, n + 1, front.xnT[1 - u])
                    if e == 5 and more and routed:
                        rt.tensor_turn(t, n + 1, 1 - u)
                t.wait_ge(s["h_ps"], (n + 1) * NH)
                t.sem_inc(front.xnT_used, 1)
                t.sem_inc(front.xn_used, 1)
                second(n, NX - 1)

            over_groups(t, group)


def stage_out(nc, p, out):
    with Stage(nc, "O") as st:
        stored = st.sem("stored")
        block = st.block()

        @block.sync
        def _(sp):
            sp.dma_start(out, p.X[:]).then_inc(stored, 16)
            sp.wait_ge(stored, 16)


class P:
    pass


def build(nc, d, out, layers=range(1, 9)):
    ctx = ExitStack()
    with ctx:
        p = P()

        def sb(name, shape, dt=F32, at=ctx):
            return at.enter_context(nc.sbuf_tensor(name, shape, dt))

        p.X = sb("X", [128, B, D])
        p.mean, p.rstd, p.mhalf = sb("mean", [128, B]), sb("rstd", [128, B]), sb("mhalf", [128, B])
        p.gate, p.ident = sb("gate", [128, 8]), sb("ident", [128, 128])
        p.ident16 = sb("ident16", [128, 128], BF16)
        stage_a(nc, p, d)
        if 2 in layers:
            with ExitStack() as l0:
                p.ones16, p.bias3 = sb("ones16", [128, 128], BF16, l0), sb("bias3", [128, NE_L0], BF16, l0)
                XtT, Yt = sb("XtT", [128, NE_L0], F32, l0), sb("Yt", [128, NE_L0 // 128, 128], F32, l0)
                stage_b1(nc, p, d, XtT)
                stage_mid(nc, p, d, XtT, Yt)
                stage_b2(nc, p, d, Yt)
        p.KS = [sb(f"KS{u}", [3 * HW, NHG, NHG, GD], F32R) for u in range(2)]
        p.VZ = [sb(f"VZ{u}", [128, GB, H * HW]) for u in range(2)]
        p.G2 = sb("G2", [128, B, NX])
        if 3 in layers:
            stage_attn(nc, p, d, "L1", 1, True, True)
        if 4 in layers:
            stage_l1_ffn(nc, p, d)
        if 5 in layers:
            stage_l2_attn(nc, p, d)
        if 6 in layers:
            stage_l2_route(nc, p, d)
            stage_ffn(nc, p, d, "F2", 6, False)
        if 7 in layers:
            stage_attn(nc, p, d, "L3", 3, False, 3 not in layers)
        if 8 in layers:
            stage_ffn(nc, p, d, "F3", 7, True)
        stage_out(nc, p, out)


def attn_layouts(name, n, c, w, rope):
    out = {}
    rot = np.arange(D).reshape(H, 2, HD // 2)[:, ::-1].reshape(D)
    for k in "qkvo":
        out[f"{name}_W{k}T"] = c(n(w[f"{name}_xattn_W{k}"]).T)
    for k in "qkv":
        out[f"{name}_b{k}"] = c(n(w[f"{name}_xattn_b{k}"]).reshape(D, 1))
    out[f"{name}_bo"] = c(n(w[f"{name}_xattn_bo"]).reshape(1, D))
    if rope:
        for k in "qk":
            out[f"{name}_W{k}rT"] = c(n(w[f"{name}_xattn_W{k}"])[rot].T)
            out[f"{name}_b{k}r"] = c(n(w[f"{name}_xattn_b{k}"])[rot].reshape(D, 1))
    return out


def rope_tables():
    half = HD // 2
    inv = (1.0 / 10000.0 ** (np.arange(half, dtype=np.float32) / half)).astype(np.float32)
    ang = np.arange(S, dtype=np.float32)[None, :] * inv[:, None]
    cos, sin = np.cos(ang).astype(np.float32), np.sin(ang).astype(np.float32)
    cos = np.tile(np.concatenate([cos, cos]), (H, 1))
    sin = np.tile(np.concatenate([-sin, sin]), (H, 1))
    sc = np.float32(HD ** -0.5)
    return {"cosk": cos, "sink": sin, "cosq": cos * sc, "sinq": sin * sc}


def layouts(x, itok_S_0_31, ctx_1024, mask_1x1xSxS2_ik0, g_xattn, g_ffn, **w):
    c = np.ascontiguousarray
    n = lambda a: np.asarray(a)
    return {
        "x": c(n(x).transpose(1, 0, 2)),
        "itok": c(n(itok_S_0_31).reshape(1, S)),
        "ctxT_rows": c(n(ctx_1024).transpose(0, 2, 1)),
        "g_xattn": c(n(g_xattn)), "g_ffn": c(n(g_ffn)),
        "phiT": c(n(w["L0_ffn_phi_w"]).T), "phi_b": c(n(w["L0_ffn_phi_b"]).reshape(1, -1)),
        "phiT_slots": c(n(w["L0_ffn_phi_w"]).reshape(NL, NP, D).transpose(2, 1, 0).reshape(D, -1)),
        "phi_b_slots": c(n(w["L0_ffn_phi_b"]).reshape(NL, NP).T.reshape(1, -1)),
        "expert_w": c(n(w["L0_ffn_expert_w"]).transpose(1, 0, 2)), "expert_b": c(n(w["L0_ffn_expert_b"])),
        "sel_expert": np.repeat(np.eye(NL, dtype=np.float32), NP, axis=1),
        "ident": np.eye(128, dtype=np.float32),
        "ctxT": c(n(ctx_1024).transpose(2, 0, 1)), "ctx": c(n(ctx_1024).transpose(1, 0, 2)),
        "L1_mask": np.tril(np.ones((S, S), np.int32)), "L3_mask": c(n(mask_1x1xSxS2_ik0).reshape(S, S)),
        "L1F_rW": c(n(w["L1_ffn_centroids"]).T), "L1F_rb": c(n(w["L1_ffn_expert_biases"]).reshape(1, NR)),
        "L1F_WrT": c(n(w["L1_ffn_Wr"]).transpose(2, 0, 1)), "L1F_br": c(n(w["L1_ffn_br"])),
        "L1F_WsT": c(n(w["L1_ffn_Ws"]).transpose(2, 0, 1)), "L1F_bs": c(n(w["L1_ffn_bs"]).reshape(1, 2, D)),
        "L2_gate_w": c(n(w["L2_ffn_gate_w"])),
        "F2_w1": c(n(w["L2_ffn_w1"]).transpose(1, 0, 2)),
        "F2_w2": c(n(w["L2_ffn_w2"]).reshape(NX, FC, 128, D).transpose(2, 0, 1, 3)),
        "F3_rW": c(n(w["L3_ffn_gate_w"])), "F3_rb": c(n(w["L3_ffn_gate_b"]).reshape(1, NX)),
        "F3_w1": c(n(w["L3_ffn_w1"]).transpose(1, 0, 2)),
        "F3_w2": c(n(w["L3_ffn_w2"]).reshape(NX, FC, 128, D).transpose(2, 0, 1, 3)),
        "F3_b1": c(n(w["L3_ffn_b1"]).reshape(NX, FC, 128).transpose(2, 0, 1)), "F3_b2": c(n(w["L3_ffn_b2"])),
        **rope_tables(), **attn_layouts("L1", n, c, w, True), **attn_layouts("L3", n, c, w, False),
    }


def kernel(**inputs):
    import concourse.bacc as _bacc
    from concourse.bass_utils import run_bass_kernel_spmd as _run

    nc = _bacc.Bacc("TRN2", target_bir_lowering=False, num_devices=1)
    arrays = layouts(**inputs)
    d = {k: nc.dram_tensor(f"in_{k}", a.shape, mybir.dt.from_np(a.dtype), kind="ExternalInput").ap()
         for k, a in arrays.items()}
    out = nc.dram_tensor("out_x", (S, B, D), F32, kind="ExternalOutput").ap()
    build(nc, d, out)
    r = _run(nc, [{f"in_{k}": a for k, a in arrays.items()}], core_ids=[0])
    return r.results[0]["out_x"].transpose(1, 0, 2)
```

```python
import numpy as np
from contextlib import ExitStack

import concourse.bass as bass
from concourse import mybir

F32 = mybir.dt.float32
F32R = mybir.dt.float32r
BF16 = mybir.dt.bfloat16
I32 = mybir.dt.int32
ALU = mybir.AluOpType
ACT = mybir.ActivationFunctionType
AX = mybir.AxisListType

B, S, D = 32, 128, 128
GB = 4
NG = B // GB
GD = GB * D
EPS = 1e-5
NL, NP = 64, 32
NE_L0 = NL * NP
H, HD = 16, 8
NR = 16
NX, FF = 8, 512
FC = FF // 128
CAP = 32
TOPK = 2
NEG = -(2.0 ** 100)


class Steps:

    def __init__(self, eng, sem):
        self.eng, self.sem, self.base, self.k = eng, sem, 0, 0

    def link(self, ins):
        ins.then_inc(self.sem, 1)
        self.k += 1
        self.eng.wait_ge(self.sem, self.base + self.k)

    def loop(self, n, i, per):
        self.start = self.base + self.k
        self.per, self.n = per, n
        self.base, self.k = i * per + self.start, 0

    def end(self):
        assert self.k == self.per, (self.k, self.per)
        self.base, self.k = self.start + self.n * self.per, 0


class Stage:

    def __init__(self, nc, name):
        self.nc, self.name, self.ctx, self.sems = nc, name, ExitStack(), []

    def __enter__(self):
        return self

    def __exit__(self, *a):
        self.ctx.__exit__(*a)
        if a[0] is None:
            self.nc.clear_and_free_semaphores(self.sems)
            self.nc.all_engine_barrier()

    def sb(self, name, shape, dt=F32):
        return self.ctx.enter_context(self.nc.sbuf_tensor(f"{self.name}_{name}", shape, dt))

    def bank(self, name, dt=F32):
        return self.ctx.enter_context(self.nc.psum_tensor(f"{self.name}_{name}", [128, 512], dt))

    def sem(self, name):
        self.sems.append(self.nc.alloc_semaphore(f"{self.name}_{name}"))
        return self.sems[-1]

    def block(self):
        return self.ctx.enter_context(self.nc.Block())


class Front:

    def __init__(self, st, p):
        self.st, self.p = st, p
        self.xn = [st.sb(f"xn{u}", [128, GB, D]) for u in range(2)]
        self.xnT = [st.sb(f"xnT{u}", [128, GD]) for u in range(2)]
        self.ps = st.bank("frontT")
        self.xn_ready = st.sem("xn_ready")
        self.xn_used = st.sem("xn_used")
        self.xnT_ps = st.sem("xnT_ps")
        self.xnT_ready = st.sem("xnT_ready")
        self.xnT_used = st.sem("xnT_used")

    def vector(self, eng, n, u, counted=True):
        nc, p = self.st.nc, self.p
        if counted:
            eng.wait_ge(self.xn_used, n + 1)
        for j in range(GB):
            b = n * GB + j
            ins = nc.vector.tensor_scalar(self.xn[u][:, j, :], p.X[:, bass.ds(b, 1), :].rearrange("p a d -> p (a d)"),
                                          p.mean[:, bass.ds(b, 1)], p.rstd[:, bass.ds(b, 1)],
                                          ALU.subtract, ALU.mult)
        ins.then_inc(self.xn_ready, 1)

    def tensor(self, eng, n, u):
        nc = self.st.nc
        eng.wait_ge(self.xn_ready, n + 1)
        eng.wait_ge(self.xnT_ready, n + 1)
        for j in range(GB):
            ins = nc.tensor.transpose(self.ps[:, j * D:(j + 1) * D], self.xn[u][:, j, :], self.p.ident[:])
        ins.then_inc(self.xnT_ps, 1)

    def scalar(self, eng, n, u, counted=True):
        nc = self.st.nc
        eng.wait_ge(self.xnT_ps, n + 1)
        if counted:
            eng.wait_ge(self.xnT_used, n + 1)
        nc.scalar.activation(self.xnT[u][:], self.ps[:], ACT.Copy).then_inc(self.xnT_ready, 1)


def stand(eng, waited):
    eng.sem_inc(waited, 1)


def credit(eng, *pairs):
    for sem, n in pairs:
        eng.sem_inc(sem, n)


class Tail:
    STEPS = 3

    def __init__(self, st, p):
        self.st, self.p = st, p
        self.stats = st.sb("bn", [128, GB, 6])
        self.mv = st.sb("mv", [128, 2, GB, 2])
        self.var_ready = st.sem("var_ready")
        self.rstd_done = st.sem("rstd_done")
        self.waited = st.sem("tail_waited")

    def vector(self, eng, n, u, steps, last):
        nc, p = self.st.nc, self.p
        steps.link(last)
        stand(eng, self.waited)
        for j in range(GB):
            ins = nc.vector.bn_stats(self.stats[:, j, :], p.X[:, bass.ds(n * GB + j, 1), :].rearrange("p a d -> p (a d)"))
        steps.link(ins)
        eng.wait_ge(self.rstd_done, n + 1)
        stand(eng, self.waited)
        for j in range(GB):
            ins = nc.vector.bn_aggr(self.mv[:, u, j, :], self.stats[:, j, :])
        steps.link(ins)
        stand(eng, self.waited)
        nc.vector.tensor_copy(p.mean[:, bass.ds(n * GB, GB)], self.mv[:, u, :, 0])
        nc.vector.tensor_scalar(self.mv[:, u, :, 1], self.mv[:, u, :, 1], EPS, None, ALU.add)\
            .then_inc(self.var_ready, 1)

    def gpsimd(self, eng, n, u):
        nc, p = self.st.nc, self.p
        eng.wait_ge(self.var_ready, n + 2)
        nc.gpsimd.tensor_tensor(p.rstd[:, bass.ds(n * GB, GB)], self.mv[:, u, :, 1], p.mhalf[:, 0:GB], ALU.pow)\
            .then_inc(self.rstd_done, 1)


def over_groups(eng, body, steps=None, per=0):
    with eng.Fori(0, NG // 2 - 1) as i:
        if steps:
            steps.loop(NG // 2 - 1, i, per)
        body(i * 2, 0, True)
        body(i * 2 + 1, 1, True)
        if steps:
            steps.end()
    body(NG - 2, 0, True)
    body(NG - 1, 1, False)


def over_groups_skewed(eng, body, steps=None, per=0):
    body(0, 0, True, True)
    body(1, 1, False, True)
    with eng.Fori(0, NG // 2 - 2) as i:
        if steps:
            steps.loop(NG // 2 - 2, i, per)
        body(i * 2 + 2, 0, False, True)
        body(i * 2 + 3, 1, False, True)
        if steps:
            steps.end()
    body(NG - 2, 0, False, True)
    body(NG - 1, 1, False, False)


def xgroup(p, n):
    return p.X[:, bass.ds(n * GB, GB), :]


def stage_a(nc, p, d):
    RING, PB = 8, 16
    with Stage(nc, "A") as st:
        xn = [st.sb(f"xn{u}", [128, GB, D]) for u in range(2)]
        xnT = st.sb("xnT", [128, B, S])
        wring = st.sb("wring", [128, RING, D])
        yT = st.sb("yT", [128, B, S])
        stats = st.sb("stats", [128, B, 6])
        itok = st.sb("itok", [1, S], I32)
        graw = st.sb("graw", [128, 8])
        front = [st.bank(f"front{u}") for u in range(2)]
        pos = [st.bank(f"pos{u}") for u in range(2)]
        x_in = [st.sem(f"x_in{g}") for g in range(NG)]
        g_in, tok_in, const_in = st.sem("g_in"), st.sem("tok_in"), st.sem("const_in")
        mh_ready, var_ready, rstd_ready, v_step = st.sem("mh"), st.sem("var"), st.sem("rstd"), st.sem("v_step")
        xn_ready, xT_ps, xT_ready = st.sem("xn_ready"), st.sem("xT_ps"), st.sem("xT_ready")
        w_in = [st.sem(f"w_in{r}") for r in range(RING)]
        w_used, y_ps, y_out = st.sem("w_used"), st.sem("y_ps"), st.sem("y_out")
        yt_ps, x_new, gate_ready = st.sem("yt_ps"), st.sem("x_new"), st.sem("gate_ready")
        pool_done = st.sem("pool_done")
        block = st.block()

        @block.sync
        def _(sp):
            sp.dma_start(itok[:], d["itok"]).then_inc(tok_in, 16)
            for g in range(NG):
                sp.dma_start(p.X[:, g * GB:(g + 1) * GB, :], d["x"][:, g * GB:(g + 1) * GB, :]).then_inc(x_in[g], 16)
            sp.dma_start(p.ident[:], d["ident"]).then_inc(const_in, 16)
            sp.wait_ge(tok_in, 16)
            credit(sp, (w_used, RING))
            with sp.Fori(0, S // RING) as i:
                for r in range(RING):
                    s0 = i * RING
                    t = nc.values_load(itok[0:1, bass.ds(s0 + r, 1)], engines=[mybir.EngineType.SP],
                                       min_val=0, max_val=B - 1)
                    sp.wait_ge(w_used, s0 + r + 1)
                    sp.dma_start(wring[:, r, :], d["ctxT_rows"][bass.ds(t, 1), :, :].rearrange("a p o -> (a p) o"))\
                        .then_inc(w_in[r], 16)

        @block.gpsimd
        def _(g):
            for dst, src in ((graw[:, 0:4], d["g_xattn"]), (graw[:, 4:8], d["g_ffn"])):
                g.dma_start(dst, src.rearrange("(a n) -> a n", a=1).to_broadcast([128, 4])).then_inc(g_in, 16)
            nc.gpsimd.memset(p.mhalf[:], -0.5).then_inc(mh_ready, 1)
            g.wait_ge(mh_ready, 1)
            g.wait_ge(var_ready, 1)
            nc.gpsimd.tensor_tensor(p.rstd[:], stats[:, :, 1], p.mhalf[:], ALU.pow).then_inc(rstd_ready, 1)
            for n in range(NG):
                g.wait_ge(x_new, n + 1)
                nc.gpsimd.tensor_tensor(p.rstd[:, n * GB:(n + 1) * GB], stats[:, n * GB:(n + 1) * GB, 1],
                                        p.mhalf[:, 0:GB], ALU.pow).then_inc(pool_done, 1)

        @block.vector
        def _(v):
            steps = Steps(v, v_step)
            mv = stats
            for g in range(NG):
                v.wait_ge(x_in[g], 16)
                for b in range(g * GB, (g + 1) * GB):
                    ins = nc.vector.bn_stats(xnT[:, b, 0:6], p.X[:, b, :])
            steps.link(ins)
            for b in range(B):
                ins = nc.vector.bn_aggr(mv[:, b, 0:2], xnT[:, b, 0:6])
            steps.link(ins)
            nc.vector.tensor_copy(p.mean[:], mv[:, :, 0])
            steps.link(nc.vector.tensor_scalar(mv[:, :, 1], mv[:, :, 1], EPS, None, ALU.add))
            v.sem_inc(var_ready, 1)
            v.wait_ge(const_in, 16)
            nc.vector.tensor_copy(p.ident16[:], p.ident[:])
            v.wait_ge(rstd_ready, 1)
            for g in range(NG):
                if g >= 2:
                    v.wait_ge(xT_ps, g - 1)
                for j in range(GB):
                    b = g * GB + j
                    ins = nc.vector.tensor_scalar(xn[g % 2][:, j, :], p.X[:, b, :], p.mean[:, b:b + 1],
                                                  p.rstd[:, b:b + 1], ALU.subtract, ALU.mult)
                ins.then_inc(xn_ready, 1)
            v.wait_ge(gate_ready, 1)
            for g in range(NG):
                v.wait_ge(yt_ps, g + 1)
                xg = p.X[:, g * GB:(g + 1) * GB, :]
                steps.link(nc.vector.scalar_tensor_tensor(xg, front[g % 2][:].rearrange("p (a d) -> p a d", a=GB),
                                                          p.gate[:, 0:1], xg, ALU.mult, ALU.add))
                for j in range(GB):
                    ins = nc.vector.bn_stats(xn[0][:, j, 0:6], p.X[:, g * GB + j, :])
                steps.link(ins)
                for j in range(GB):
                    ins = nc.vector.bn_aggr(mv[:, g * GB + j, 0:2], xn[0][:, j, 0:6])
                steps.link(ins)
                nc.vector.tensor_copy(p.mean[:, g * GB:(g + 1) * GB], mv[:, g * GB:(g + 1) * GB, 0])
                steps.link(nc.vector.tensor_scalar(mv[:, g * GB:(g + 1) * GB, 1], mv[:, g * GB:(g + 1) * GB, 1],
                                                   EPS, None, ALU.add))
                v.sem_inc(x_new, 1)

        @block.scalar
        def _(a):
            a.wait_ge(g_in, 32)
            nc.scalar.activation(p.gate[:], graw[:], ACT.Tanh).then_inc(gate_ready, 1)
            for g in range(NG):
                a.wait_ge(xT_ps, g + 1)
                nc.scalar.activation(xnT[:, g * GB:(g + 1) * GB, :],
                                     front[g % 2][:].rearrange("p (a d) -> p a d", a=GB), ACT.Copy).then_inc(xT_ready, 1)
            with a.Fori(0, S // PB // 2) as i:
                for u in range(2):
                    k = i * 2 + u
                    a.wait_ge(y_ps, k + 1)
                    nc.scalar.activation(yT[:, :, bass.ds(k * PB, PB)],
                                         pos[u][:].rearrange("p (s b) -> p b s", s=PB), ACT.Copy).then_inc(y_out, 1)

        @block.tensor
        def _(t):
            t.wait_ge(const_in, 16)
            for g in range(NG):
                t.wait_ge(xn_ready, g + 1)
                if g >= 2:
                    t.wait_ge(xT_ready, g - 1)
                for j in range(GB):
                    ins = nc.tensor.transpose(front[g % 2][:, j * D:(j + 1) * D], xn[g % 2][:, j, :], p.ident[:])
                ins.then_inc(xT_ps, 1)
            t.wait_ge(xT_ready, NG)
            credit(t, (y_out, 2))
            with t.Fori(0, S // PB // 2) as i:
                for u in range(2):
                    k = i * 2 + u
                    t.wait_ge(y_out, k + 1)
                    for q in range(PB):
                        r = q % RING
                        t.wait_ge(w_in[r], k * (16 * PB // RING) + 16 * (q // RING) + 16)
                        ins = nc.tensor.matmul(pos[u][:, q * B:(q + 1) * B], wring[:, r, :],
                                               xnT[:, :, bass.ds(k * PB + q, 1)].rearrange("p b a -> p (b a)"),
                                               start=True, stop=True)
                        ins.then_inc(w_used, 1)
                    t.wait_ge(w_used, (k * PB) + PB + RING)
                    t.sem_inc(y_ps, 1)
            t.wait_ge(y_out, S // PB + 2)
            for g in range(NG):
                if g >= 2:
                    t.wait_ge(x_new, g - 1)
                for j in range(GB):
                    ins = nc.tensor.transpose(front[g % 2][:, j * D:(j + 1) * D], yT[:, g * GB + j, :], p.ident[:])
                ins.then_inc(yt_ps, 1)


class SoftUnit:
    RING = 4

    def __init__(self, st, size, probs_used):
        self.st, self.size, self.ng = st, size, 512 // size
        self.banks = [st.bank(f"logits{i}") for i in range(2)]
        self.E = [st.sb(f"E{i}", [128, 512]) for i in range(self.RING)]
        self.m = st.sb("m", [128, 2, self.ng])
        self.r = st.sb("r", [128, 2, self.ng])
        self.logits_ready = st.sem("logits_ready")
        self.max_done = st.sem("max_done")
        self.diff_done = st.sem("diff_done")
        self.exp_done = st.sem("exp_done")
        self.sum_done = st.sem("sum_done")
        self.inverse_done = st.sem("inverse_done")
        self.probs_ready = st.sem("probs_ready")
        self.probs_used = probs_used

    def bank(self, w):
        return self.banks[w % 2]

    def grouped(self, w):
        return self.E[w % self.RING][:].rearrange("p (n q) -> p n q", q=self.size)

    def tensor_logits(self, eng, k, w, xT, phiT, q, p):
        nc = self.st.nc
        eng.wait_ge(self.diff_done, k + 1)
        nc.tensor.matmul(self.bank(w)[:], xT, phiT[:, q * 512:(q + 1) * 512], start=True, stop=False)
        nc.tensor.matmul(self.bank(w)[:], p.ones16[:], p.bias3[:, q * 512:(q + 1) * 512], start=False, stop=True)\
            .then_inc(self.logits_ready, 1)

    def vector(self, eng, k, w, prev):
        nc = self.st.nc
        lg = self.bank(w)[:].rearrange("p (n q) -> p n q", q=self.size)
        eng.wait_ge(self.logits_ready, k + 1)
        nc.vector.tensor_reduce(self.m[:, w % 2, :], lg, AX.X, ALU.max).then_inc(self.max_done, 1)
        if prev:
            self.vector_sum(eng, k - 1, w - 1)
        eng.wait_ge(self.max_done, k + 1)
        eng.wait_ge(self.probs_used, k + 1)
        nc.vector.tensor_tensor(self.grouped(w), lg, self.m[:, w % 2, :].unsqueeze(2)
                                .to_broadcast([128, self.ng, self.size]), ALU.subtract).then_inc(self.diff_done, 1)
        if prev:
            self.vector_inverse(eng, k - 1, w - 1)

    def vector_sum(self, eng, k, w):
        eng.wait_ge(self.exp_done, k + 1)
        eng.wait_ge(self.probs_ready, k + 1)
        self.st.nc.vector.tensor_reduce(self.r[:, w % 2, :], self.grouped(w), AX.X, ALU.add).then_inc(self.sum_done, 1)

    def vector_inverse(self, eng, k, w):
        r = self.r[:, w % 2, :]
        eng.wait_ge(self.sum_done, k + 1)
        self.st.nc.vector.reciprocal(r, r).then_inc(self.inverse_done, 1)

    def scalar_exp(self, eng, k, w):
        e = self.E[w % self.RING][:]
        eng.wait_ge(self.diff_done, k + 3)
        self.st.nc.scalar.activation(e, e, ACT.Exp).then_inc(self.exp_done, 1)

    def gpsimd(self, eng, k, w):
        e = self.grouped(w)
        eng.wait_ge(self.inverse_done, k + 1)
        self.st.nc.gpsimd.tensor_tensor(e, e, self.r[:, w % 2, :].unsqueeze(2)
                                        .to_broadcast([128, self.ng, self.size]), ALU.mult).then_inc(self.probs_ready, 1)


NQ = NE_L0 // 512
UG = GB * NQ


def bias_parts(nc, v, steps, raw, bias3, part, order):
    pick = (lambda ap: ap) if order is None else order
    for row in range(3):
        steps.link(nc.vector.tensor_copy(part[0:96, :], raw[0:96, :]))
        src = part[32 * row:32 * row + 1, :]
        nc.vector.tensor_copy(bias3[32 * row:32 * row + 1, :], src)
        if row < 2:
            steps.link(nc.vector.tensor_tensor(raw[0:96, :], raw[0:96, :], part[0:96, :], ALU.subtract))


def stage_b1(nc, p, d, XtT):
    LAG = 3
    with Stage(nc, "B1") as st:
        front = Front(st, p)
        probs_used = st.sem("probs_used")
        soft = SoftUnit(st, NP, probs_used)
        acc = [st.bank(f"acc{q}") for q in range(NQ)]
        phiT = st.sb("phiT", [128, NE_L0])
        raw, part = st.sb("raw", [96, NE_L0]), st.sb("part", [96, NE_L0], BF16)
        zero = st.sb("zero", [128, 512], BF16)
        phi_in, raw_in, raw_zero, consts = st.sem("phi_in"), st.sem("raw_in"), st.sem("raw_zero"), st.sem("consts")
        bias_ready, v_step, acc_done, acc_out = st.sem("bias_ready"), st.sem("v_step"), st.sem("acc_done"), st.sem("acc_out")
        block = st.block()

        @block.sync
        def _(sp):
            sp.dma_start(phiT[:], d["phiT"]).then_inc(phi_in, 16)
            sp.wait_ge(raw_zero, 1)
            for row in range(3):
                sp.dma_start(raw[32 * row:32 * row + 1, :], d["phi_b"]).then_inc(raw_in, 16)

        @block.gpsimd
        def _(g):
            nc.gpsimd.memset(raw[:], 0.0).then_inc(raw_zero, 1)
            nc.gpsimd.memset(zero[:], 0.0).then_inc(consts, 1)
            nc.gpsimd.memset(p.ones16[:], 1.0).then_inc(consts, 1)
            nc.gpsimd.memset(p.bias3[:], 0.0).then_inc(consts, 1)
            credit(g, (soft.probs_ready, 2))
            over_groups_skewed(g, lambda n, u, first, more: [soft.gpsimd(g, n * UG + w, w) for w in range(UG)])

        @block.vector
        def _(v):
            steps = Steps(v, v_step)
            credit(v, (soft.diff_done, 2))
            front.vector(v, 0, 0, False)
            v.wait_ge(raw_in, 48)
            v.wait_ge(consts, 3)
            bias_parts(nc, v, steps, raw, p.bias3, part, None)
            steps.link(nc.vector.tensor_copy(part[0:1, 0:8], part[0:1, 8:16]))
            v.sem_inc(bias_ready, 1)

            def group(n, u, first, more):
                for w in range(UG):
                    soft.vector(v, n * UG + w, w, not (first and w == 0))
                    if w == UG // 2 and more:
                        v.wait_ge(probs_used, n * UG + soft.RING)
                        front.vector(v, n + 1, 1 - u, False)

            over_groups_skewed(v, group)
            soft.vector_sum(v, NG * UG - 1, UG - 1)
            soft.vector_inverse(v, NG * UG - 1, UG - 1)
            v.wait_ge(acc_done, 1)
            for q in range(NQ):
                ins = nc.vector.tensor_copy(XtT[:, q * 512:(q + 1) * 512], acc[q][:])
            steps.link(ins)

        @block.scalar
        def _(a):
            credit(a, (front.xnT_ready, 1))
            front.scalar(a, 0, 0, False)

            def group(n, u, first, more):
                for w in range(UG):
                    soft.scalar_exp(a, n * UG + w, w)
                    if w == UG // 2 and more:
                        if not first:
                            a.wait_ge(soft.logits_ready, n * UG)
                        front.scalar(a, n + 1, 1 - u, False)

            over_groups_skewed(a, group)

        @block.tensor
        def _(t):
            credit(t, (probs_used, soft.RING))
            front.tensor(t, 0, 0)
            t.wait_ge(phi_in, 16)
            t.wait_ge(consts, 3)
            t.wait_ge(bias_ready, 1)
            for q in range(NQ):
                nc.tensor.matmul(acc[q][:], zero[:, 0:128], zero[:], start=True, stop=False, skip_group_check=True)

            def dispatch(k, w, u):
                t.wait_ge(soft.probs_ready, k + 3)
                nc.tensor.matmul(acc[w % NQ][:], front.xn[u][:, w // NQ, :], soft.E[w % soft.RING][:],
                                 start=False, stop=False, skip_group_check=True).then_inc(probs_used, 1)

            def group(n, u, first, more):
                t.wait_ge(front.xnT_ready, n + 2)
                for w in range(UG):
                    j = w // NQ
                    soft.tensor_logits(t, n * UG + w, w, front.xnT[u][:, j * 128:(j + 1) * 128], phiT, w % NQ, p)
                    if w >= LAG:
                        dispatch(n * UG + w - LAG, w - LAG, u)
                    elif not first:
                        dispatch(n * UG + w - LAG, w - LAG + UG, 1 - u)
                    if w == UG // 2 and more:
                        front.tensor(t, n + 1, 1 - u)

            over_groups_skewed(t, group)
            for w in range(UG - LAG, UG):
                dispatch((NG - 1) * UG + w, w, 1)
            for q in range(NQ):
                ins = nc.tensor.matmul(acc[q][:], zero[:, 0:128], zero[:], start=False, stop=True, skip_group_check=True)
            ins.then_inc(acc_done, 1)


def stage_mid(nc, p, d, XtT, Yt):
    NC = NE_L0 // 128
    with Stage(nc, "M") as st:
        ew = st.sb("ew", [128, NL, 128])
        eb = st.sb("eb", [NL, 128])
        sel = st.sb("sel", [NL, NE_L0])
        xt = st.sb("xt", [128, NC, D])
        xtn = st.sb("xtn", [128, NC, D])
        yn = st.sb("yn", [128, NC, D])
        stats, mv, rs = st.sb("stats", [128, NC, 6]), st.sb("mv", [128, NC, 2]), st.sb("rs", [128, NC])
        banks = [st.bank(f"b{q}") for q in range(4)]
        ybanks = [st.bank(f"y{q}") for q in range(4)]
        scratch = nc.dram_tensor("slots_scratch", (NP, NL, 128), F32, kind="Internal").ap()
        ew_in, tr, v_step, var_ready, rs_ready = st.sem("ew_in"), st.sem("tr"), st.sem("v_step"), st.sem("var"), st.sem("rs")
        norm, th, tr2, back, y_ps, y_sb = st.sem("norm"), st.sem("th"), st.sem("tr2"), st.sem("back"), st.sem("y_ps"), st.sem("y_sb")
        put, got = st.sem("put"), st.sem("got")
        block = st.block()

        @block.sync
        def _(sp):
            sp.dma_start(ew[:], d["expert_w"]).then_inc(ew_in, 16)
            sp.dma_start(eb[:], d["expert_b"]).then_inc(ew_in, 16)
            sp.dma_start(sel[:], d["sel_expert"]).then_inc(ew_in, 16)
            sp.wait_ge(y_sb, 4)
            for a4 in range(4):
                sp.dma_start(scratch.rearrange("s (c a) h -> a s c h", a=4)[a4], yn[32 * a4:32 * a4 + 32, :, :])\
                    .then_inc(put, 16)
            sp.wait_ge(put, 64)
            sp.dma_start(Yt[:], scratch.rearrange("(c s) n h -> (s n) c h", s=2)).then_inc(got, 16)
            sp.wait_ge(got, 16)

        @block.gpsimd
        def _(g):
            g.wait_ge(var_ready, 1)
            nc.gpsimd.tensor_tensor(rs[:], mv[:, :, 1], p.mhalf[:, 0:NC], ALU.pow).then_inc(rs_ready, 1)

        @block.vector
        def _(v):
            steps = Steps(v, v_step)
            for q in range(4):
                v.wait_ge(tr, q + 1)
                steps.link(nc.vector.tensor_scalar(xt[:, 4 * q:4 * q + 4, :], banks[q][:].rearrange("p (c d) -> p c d", c=4),
                                                   -33000.0, 65000.0, ALU.max, ALU.min))
            for c in range(NC):
                ins = nc.vector.bn_stats(stats[:, c, :], xt[:, c, :])
            steps.link(ins)
            for c in range(NC):
                ins = nc.vector.bn_aggr(mv[:, c, :], stats[:, c, :])
            steps.link(ins)
            nc.vector.tensor_scalar(mv[:, :, 1], mv[:, :, 1], EPS, None, ALU.add).then_inc(var_ready, 1)
            v.wait_ge(rs_ready, 1)
            for c in range(NC):
                nc.vector.tensor_scalar(xtn[:, c, :], xt[:, c, :], mv[:, c, 0:1], rs[:, c:c + 1],
                                        ALU.subtract, ALU.mult).then_inc(norm, 1)
            for q in range(4):
                v.wait_ge(tr2, q + 1)
                nc.vector.tensor_copy(XtT[:, q * 512:(q + 1) * 512], banks[q][:]).then_inc(back, 1)

        @block.scalar
        def _(a):
            for q in range(4):
                a.wait_ge(norm, 4 * q + 4)
                x4 = xtn[:, 4 * q:4 * q + 4, :]
                nc.scalar.activation(x4, x4, ACT.Tanh).then_inc(th, 1)
            for q in range(4):
                a.wait_ge(y_ps, q + 1)
                nc.scalar.activation(yn[:, 4 * q:4 * q + 4, :], ybanks[q][:].rearrange("p (c d) -> p c d", c=4),
                                     ACT.Copy).then_inc(y_sb, 1)

        @block.tensor
        def _(t):
            for q in range(4):
                for c in range(4 * q, 4 * q + 4):
                    ins = nc.tensor.transpose(banks[q][:, (c % 4) * 128:(c % 4 + 1) * 128], XtT[:, c * 128:(c + 1) * 128],
                                              p.ident[:])
                ins.then_inc(tr, 1)
            for q in range(4):
                t.wait_ge(th, q + 1)
                for c in range(4 * q, 4 * q + 4):
                    ins = nc.tensor.transpose(banks[q][:, (c % 4) * 128:(c % 4 + 1) * 128], xtn[:, c, :], p.ident[:])
                ins.then_inc(tr2, 1)
            t.wait_ge(ew_in, 48)
            for q in range(4):
                t.wait_ge(back, q + 1)
                for c in range(4 * q, 4 * q + 4):
                    cols = slice((c % 4) * 128, (c % 4 + 1) * 128)
                    nc.tensor.matmul(ybanks[q][:, cols], sel[:, c * 128:(c + 1) * 128], eb[:], start=True, stop=False,
                                     skip_group_check=True)
                    for a4 in range(4):
                        e = 4 * c + a4
                        ins = nc.tensor.matmul(ybanks[q][32 * a4:32 * a4 + 32, cols], XtT[:, e * NP:(e + 1) * NP],
                                               ew[:, e, :], start=False, stop=True, skip_group_check=True)
                ins.then_inc(y_ps, 1)


def stage_b2(nc, p, d, Yt):
    LAG = 3
    with Stage(nc, "B2") as st:
        front, tail = Front(st, p), Tail(st, p)
        ct_ready = st.sem("ct_ready")
        soft = SoftUnit(st, NL, ct_ready)
        phiT = st.sb("phiT", [128, NE_L0])
        raw, part = st.sb("raw", [96, NE_L0]), st.sb("part", [96, NE_L0], BF16)
        ct_ps = [st.bank(f"ct{i}") for i in range(2)]
        y_ps = [st.bank(f"y{i}") for i in range(2)]
        CT = [st.sb(f"CT{i}", [128, 512]) for i in range(2)]
        phi_in, raw_in, raw_zero = st.sem("phi_in"), st.sem("raw_in"), st.sem("raw_zero")
        bias_ready, v_step = st.sem("bias_ready"), st.sem("v_step")
        ct_moved, ct_used = st.sem("ct_moved"), st.sem("ct_used")
        block = st.block()

        @block.sync
        def _(sp):
            sp.dma_start(phiT[:], d["phiT_slots"]).then_inc(phi_in, 16)
            sp.wait_ge(raw_zero, 1)
            for row in range(3):
                sp.dma_start(raw[32 * row:32 * row + 1, :], d["phi_b_slots"]).then_inc(raw_in, 16)

        @block.gpsimd
        def _(g):
            nc.gpsimd.memset(raw[:], 0.0).then_inc(raw_zero, 1)
            credit(g, (tail.rstd_done, 2))
            credit(g, (soft.probs_ready, 2))

            def group(n, u, first, more):
                for w in range(UG):
                    soft.gpsimd(g, n * UG + w, w)
                    if w == 10 and not first:
                        tail.gpsimd(g, n - 1, 1 - u)

            over_groups_skewed(g, group)
            tail.gpsimd(g, NG - 1, 1)

        @block.vector
        def _(v):
            steps = Steps(v, v_step)
            credit(v, (soft.diff_done, 2), (tail.var_ready, 1))
            front.vector(v, 0, 0, False)
            v.wait_ge(raw_in, 48)
            bias_parts(nc, v, steps, raw, p.bias3, part, None)
            steps.link(nc.vector.tensor_copy(part[0:1, 0:8], part[0:1, 8:16]))
            v.sem_inc(bias_ready, 1)

            def finish(n, u):
                v.wait_ge(ct_used, (n + 1) * UG + 2)
                tail.vector(v, n, u, steps, nc.vector.scalar_tensor_tensor(
                    xgroup(p, n), y_ps[u][:].rearrange("p (a d) -> p a d", a=GB), p.gate[:, 4:5], xgroup(p, n),
                    ALU.mult, ALU.add))

            def group(n, u, first, more):
                for w in range(UG):
                    soft.vector(v, n * UG + w, w, not (first and w == 0))
                    if w == 4 and more:
                        v.wait_ge(ct_ready, n * UG + soft.RING)
                        front.vector(v, n + 1, 1 - u, False)
                    if w == 8 and not first:
                        finish(n - 1, 1 - u)

            over_groups_skewed(v, group, steps, 2 * tail.STEPS)
            soft.vector_sum(v, NG * UG - 1, UG - 1)
            soft.vector_inverse(v, NG * UG - 1, UG - 1)
            finish(NG - 1, 1)

        @block.scalar
        def _(a):
            credit(a, (front.xnT_ready, 1), (ct_moved, 2))
            front.scalar(a, 0, 0, False)

            def move(k, w):
                a.wait_ge(ct_ready, k + 1 + soft.RING)
                a.wait_ge(ct_used, k + 1)
                nc.scalar.activation(CT[w % 2][:], ct_ps[w % 2][:], ACT.Copy).then_inc(ct_moved, 1)

            def group(n, u, first, more):
                for w in range(UG):
                    soft.scalar_exp(a, n * UG + w, w)
                    if not (first and w < LAG):
                        move(n * UG + w - LAG, w - LAG)
                    if w == UG // 2 and more:
                        if not first:
                            a.wait_ge(soft.logits_ready, n * UG)
                        front.scalar(a, n + 1, 1 - u, False)

            over_groups_skewed(a, group)
            for w in range(UG - LAG, UG):
                move((NG - 1) * UG + w, w)

        @block.tensor
        def _(t):
            credit(t, (ct_ready, soft.RING), (ct_used, 2))
            front.tensor(t, 0, 0)
            t.wait_ge(phi_in, 16)
            t.wait_ge(bias_ready, 1)

            def turn(k, w):
                t.wait_ge(soft.probs_ready, k + 3)
                t.wait_ge(ct_moved, k + 1)
                for c in range(4):
                    ins = nc.tensor.transpose(ct_ps[w % 2][:, c * 128:(c + 1) * 128],
                                              soft.E[w % soft.RING][:, c * 128:(c + 1) * 128], p.ident[:])
                ins.then_inc(ct_ready, 1)

            def combine(k, w, u):
                t.wait_ge(ct_moved, k + 3)
                j, q = w // NQ, w % NQ
                for c in range(4):
                    ins = nc.tensor.matmul(y_ps[u][:, j * 128:(j + 1) * 128], CT[w % 2][:, c * 128:(c + 1) * 128],
                                           Yt[:, 4 * q + c, :], start=(q == 0 and c == 0), stop=(q == 3 and c == 3))
                ins.then_inc(ct_used, 1)

            def group(n, u, first, more):
                t.wait_ge(front.xnT_ready, n + 2)
                for w in range(UG):
                    j, k = w // NQ, n * UG + w
                    soft.tensor_logits(t, k, w, front.xnT[u][:, j * 128:(j + 1) * 128], phiT, w % NQ, p)
                    if not (first and w < LAG):
                        turn(k - LAG, (w - LAG) % UG)
                    if w == LAG + 1 and not first:
                        t.wait_ge(tail.var_ready, n)
                    if w > LAG:
                        combine(k - LAG - 1, w - LAG - 1, u)
                    elif not first:
                        combine(k - LAG - 1, w - LAG - 1 + UG, 1 - u)
                    if w == UG // 2 and more:
                        front.tensor(t, n + 1, 1 - u)

            over_groups_skewed(t, group)
            for w in range(UG, UG + LAG + 1):
                if w < UG + LAG:
                    turn((NG - 1) * UG + w - LAG, w - LAG)
                combine((NG - 1) * UG + w - LAG - 1, w - LAG - 1, 1)


NHG = 4
HW = NHG * HD


def stage_attn(nc, p, d, name, gate, rope, first):
    PRJ = 6 if rope else 4
    AUX = PRJ + 2
    LAST = (NG - 1) * AUX + PRJ + 2
    uses = ["x", "q", "qr", "k", "kr", "v"] if rope else ["x", "q", "k", "v"]
    PUT = {"x": 1, "q": 3, "qr": 4, "k": 5, "kr": 6, "v": 7}
    TAKE = {"x": 2, "q": 4, "qr": 5, "k": 6, "kr": 7, "v": 8}

    def project_base(n, first):
        return 2 + PRJ if first else n * AUX + PRJ

    with Stage(nc, name) as st:
        xn = [st.sb(f"xn{u}", [128, GB, D]) for u in range(2)]
        xnT = st.sb("xnT", [128, GD])
        cT = [st.sb(f"cT{u}", [128, GD]) for u in range(2)]
        wn = ["WqT", "WkT", "WvT", "WoT"] + (["WqrT", "WkrT"] if rope else [])
        W = {k: st.sb(k, [128, 128]) for k in wn}
        bn = ["bq", "bk", "bv"] + (["bqr", "bkr"] if rope else [])
        bias = {k: st.sb(k, [128, 1]) for k in bn}
        if rope:
            tab = {k: st.sb(k, [128, S]) for k in ("cosq", "sinq", "cosk", "sink")}
        bo, gcb, bvb = st.sb("bo", [128, 128]), st.sb("gcb", [128, 128]), st.sb("bvb", [128, 128])
        mi, mneg = st.sb("mi", [128, 128], I32), st.sb("mneg", [128, 128], BF16)
        t1, t2 = st.sb("t1", [128, GD]), st.sb("t2", [128, GD])
        hi = {k: st.sb(f"{k}hi", [128, GD], F32R) for k in "qk"}
        lo = {k: st.sb(f"{k}lo", [128, GD], F32R) for k in "qk"}
        QS = [st.sb(f"QS{u}", [3 * HW, NHG, GD], F32R) for u in range(2)]
        negm = st.sb("negm", [128, 2, NHG])
        sums = st.sb("sums", [128, 2, GB * H])
        E = [st.sb(f"E{i}", [128, 512]) for i in range(4)]
        PT = [st.sb(f"PT{i}", [128, 512]) for i in range(2)]
        R = st.sb("R", [128, GD])
        rT, OT = st.sb("rT", [128, GD]), st.sb("OT", [128, GD])
        tail = Tail(st, p)
        aux = [st.bank(f"aux{i}") for i in range(2)]
        sc = [st.bank(f"sc{i}") for i in range(2)]
        pt = [st.bank(f"pt{i}") for i in range(2)]
        po = [st.bank(f"po{i}") for i in range(2)]
        s = {k: st.sem(k) for k in (
            "w_in", "c_in0", "c_in1", "v_step", "xn_ready", "aux_full", "aux_free",
            "q_split", "k_split", "q_put", "k_put", "sc_ready", "max_ready",
            "pt_ready", "pt_moved", "av_done", "v_ready", "const_ready", "zeroed", "R_ready", "OT_ready", "exp_one")}
        s_qin = [st.sem(f"q_in{u}") for u in range(2)]
        s_kin = [st.sem(f"k_in{u}") for u in range(2)]
        NW = len(wn) + len(bn) + 2 + (4 if rope else 0)
        split_d = {k: [nc.dram_tensor(f"{name}_{k}split{u}", (2, 128, GD), F32, kind="Internal").ap() for u in range(2)]
                   for k in "qk"}

        def qcount(n, u):
            return (n - u) * (8 * 3) + 16 * 3

        def kcount(n, u):
            return (n - u) * (8 * 3 * NHG) + 16 * 3 * NHG

        block = st.block()

        @block.sync
        def _(sp):
            for k in wn:
                sp.dma_start(W[k][:], d[f"{name}_{k}"]).then_inc(s["w_in"], 16)
            for k in bn:
                sp.dma_start(bias[k][:], d[f"{name}_{k}"]).then_inc(s["w_in"], 16)
            if rope:
                for k in tab:
                    sp.dma_start(tab[k][:], d[k]).then_inc(s["w_in"], 16)
            sp.dma_start(bo[:], d[f"{name}_bo"].to_broadcast([128, 128])).then_inc(s["w_in"], 16)
            sp.dma_start(mi[:], d[f"{name}_mask"]).then_inc(s["w_in"], 16)

            def load_ctx(n, u):
                sp.dma_start(cT[u][:].rearrange("p (a d) -> p a d", a=GB), d["ctxT"][:, bass.ds(n * GB, GB), :])\
                    .then_inc(s["c_in0"] if u == 0 else s["c_in1"], 16)

            def spread(n, u):
                for k in "qk":
                    sp.wait_ge(s[k + "_split"], n + 1)
                    for i, part in enumerate((hi[k], lo[k])):
                        sp.dma_start(split_d[k][u][i], part[:].bitcast(F32)).then_inc(s[k + "_put"], 16)
                sp.wait_ge(s["q_put"], (n + 1) * 32)
                for r, i in enumerate((0, 0, 1)):
                    sp.dma_start(QS[u][r * HW:(r + 1) * HW, :, :].bitcast(F32),
                                 split_d["q"][u][i].rearrange("(g p) k -> p g k", g=NHG)).then_inc(s_qin[u], 16)
                sp.wait_ge(s["k_put"], (n + 1) * 32)
                for r, i in enumerate((0, 1, 0)):
                    for h4 in range(NHG):
                        sp.dma_start(p.KS[u][r * HW + h4 * HD:r * HW + (h4 + 1) * HD, :, h4, :].bitcast(F32),
                                     split_d["k"][u][i].rearrange("(g h p) k -> h p g k", g=NHG, h=NHG)[h4])\
                            .then_inc(s_kin[u], 16)

            load_ctx(0, 0)
            load_ctx(1, 1)
            sp.wait_ge(s["zeroed"], 2)
            spread(0, 0)

            with sp.Fori(0, NG // 2 - 1) as i:
                for u in range(2):
                    n = i * 2 + u
                    sp.wait_ge(s["aux_full"], n * AUX + PRJ + 2)
                    load_ctx(n + 2, u)
                    sp.wait_ge(s["av_done"], n * UG + 2)
                    spread(n + 1, 1 - u)
            sp.wait_ge(s["av_done"], (NG - 2) * UG + 2)
            spread(NG - 1, 1)

        @block.gpsimd
        def _(g):
            if first:
                nc.gpsimd.memset(p.KS[0][:].bitcast(F32), 0.0)
                nc.gpsimd.memset(p.VZ[0][:], 0.0).then_inc(s["zeroed"], 1)
            else:
                g.sem_inc(s["zeroed"], 1)
            credit(g, (tail.rstd_done, 2))
            over_groups(g, lambda n, u, more: tail.gpsimd(g, n, u))

        @block.vector
        def _(v):
            steps = Steps(v, s["v_step"])
            credit(v, (s["aux_free"], 2), (tail.var_ready, 1), (s["pt_moved"], 2), (s["OT_ready"], 2))
            if first:
                nc.vector.memset(p.KS[1][:].bitcast(F32), 0.0)
                nc.vector.memset(p.VZ[1][:], 0.0).then_inc(s["zeroed"], 1)
            else:
                v.sem_inc(s["zeroed"], 1)
            v.wait_ge(s["zeroed"], 2)
            v.wait_ge(s["w_in"], 16 * NW)
            nc.vector.tensor_scalar(mneg[:], mi[:], 0.0, NEG, ALU.is_equal, ALU.mult)
            steps.link(nc.vector.tensor_copy(bvb[:], bias["bv"][:].to_broadcast([128, 128])))
            v.sem_inc(s["const_ready"], 1)

            def normalise(n, u):
                for j in range(GB):
                    b = n * GB + j
                    ins = nc.vector.tensor_scalar(xn[u][:, j, :], p.X[:, bass.ds(b, 1), :].rearrange("p a d -> p (a d)"),
                                                  p.mean[:, bass.ds(b, 1)], p.rstd[:, bass.ds(b, 1)],
                                                  ALU.subtract, ALU.mult)
                ins.then_inc(s["xn_ready"], 1)

            def split(k, n):
                if not (isinstance(n, int) and n == 0):
                    v.wait_ge(s[k + "_put"], n * 32)
                steps.link(nc.vector.tensor_copy(hi[k][:], t1[:]))
                nc.vector.tensor_tensor(lo[k][:], t1[:], hi[k][:].bitcast(F32), ALU.subtract)\
                    .then_inc(s[k + "_split"], 1)
                v.wait_ge(s[k + "_split"], n + 1)

            def take(use, i, n, u, a0):
                bank = aux[i % 2]
                v.wait_ge(s["aux_full"], a0 + i + 1)
                if use == "x":
                    nc.vector.tensor_copy(xnT[:], bank[:]).then_inc(s["aux_free"], 1)
                elif use == "v":
                    if not (isinstance(n, int) and n < 2):
                        v.wait_ge(s["av_done"], (n - 1) * UG + 2)
                    for j in range(GB):
                        vz = p.VZ[u][:, j, :]
                        diag = bass.AP(vz.tensor, vz.offset, [vz.ap[0], [NHG * HW, NHG], [HW + HD, NHG], [1, HD]])
                        ins = nc.vector.tensor_copy(diag, bank[:, j * 128:(j + 1) * 128]
                                                    .rearrange("p (g h d) -> p g h d", g=NHG, h=NHG))
                    steps.link(ins)
                    v.sem_inc(s["v_ready"], 1)
                    v.sem_inc(s["aux_free"], 1)
                elif rope:
                    k = use[0]
                    dst, table = (t2, "sin" + k) if use[1:] else (t1, "cos" + k)
                    nc.vector.scalar_tensor_tensor(
                        dst[:].rearrange("p (a s) -> p a s", a=GB), bank[:].rearrange("p (a s) -> p a s", a=GB),
                        bias["b" + use][:, 0:1], tab[table][:].unsqueeze(1).to_broadcast([128, GB, S]),
                        ALU.add, ALU.mult).then_inc(s["aux_free"], 1)
                    if use[1:]:
                        v.wait_ge(s["aux_free"], a0 + i + 3)
                        steps.link(nc.vector.tensor_tensor(t1[:], t1[:], t2[:], ALU.add))
                        split(k, n)
                else:
                    nc.vector.tensor_scalar(t1[:], bank[:], bias["b" + use][:, 0:1],
                                            HD ** -0.5 if use == "q" else 1.0, ALU.add, ALU.mult)\
                        .then_inc(s["aux_free"], 1)
                    v.wait_ge(s["aux_free"], a0 + i + 3)
                    split(use, n)

            def maximum(k, w):
                v.wait_ge(s["sc_ready"], k + 1)
                nc.vector.tensor_reduce(negm[:, w % 2, :], sc[w % 2][:].rearrange("p (h k) -> p h k", h=NHG),
                                        AX.X, ALU.max, negate=True).then_inc(s["max_ready"], 1)

            def move(k, w):
                v.wait_ge(s["pt_ready"], k + 5)
                v.wait_ge(s["av_done"], k + 1)
                nc.vector.tensor_copy(PT[w % 2][:], pt[w % 2][:]).then_inc(s["pt_moved"], 1)

            def invert(n, u):
                v.wait_ge(s["exp_one"], ((n + 1) * UG + 2) * NHG)
                su = sums[:, u, :]
                steps.link(nc.vector.reciprocal(su, su))
                nc.vector.tensor_copy(R[:].rearrange("p (h d) -> p h d", d=HD),
                                      su.unsqueeze(2).to_broadcast([128, GB * H, HD])).then_inc(s["R_ready"], 1)

            def divide(n, u, a0):
                v.wait_ge(s["aux_full"], a0 + 1)
                steps.link(nc.vector.tensor_copy(rT[:], aux[0][:]))
                v.sem_inc(s["aux_free"], 1)
                v.wait_ge(s["av_done"], (n + 1) * UG + 2)
                nc.vector.tensor_tensor(OT[:], po[u][:], rT[:], ALU.mult).then_inc(s["OT_ready"], 1)

            def finish(n, u, a0):
                v.wait_ge(s["aux_full"], a0 + 2)
                xg = xgroup(p, n)
                steps.link(nc.vector.scalar_tensor_tensor(xg, aux[1][:].rearrange("p (a d) -> p a d", a=GB),
                                                          p.gate[:, gate:gate + 1], xg, ALU.mult, ALU.add))
                v.sem_inc(s["aux_free"], 1)
                tail.vector(v, n, u, steps, nc.vector.tensor_tensor(
                    xg, xg, gcb[:].unsqueeze(1).to_broadcast([128, GB, D]), ALU.add))

            normalise(0, 0)
            v.wait_ge(s["aux_full"], 1)
            steps.link(nc.vector.tensor_tensor(gcb[:], aux[0][:, 0:128], bo[:], ALU.add))
            v.sem_inc(s["aux_free"], 1)
            steps.link(nc.vector.tensor_scalar(gcb[:], gcb[:], p.gate[:, gate:gate + 1], None, ALU.mult))
            v.wait_ge(s["aux_full"], 2)
            v.sem_inc(s["aux_free"], 1)
            for i, use in enumerate(uses):
                take(use, i, 0, 0, 2)

            def group(n, u, first, more):
                a0 = project_base(n, first)
                f0 = a0 + PRJ if more else a0
                for w in range(UG):
                    k = n * UG + w
                    if not (first and w < 3):
                        move(k - 3, (w - 3) % UG)
                    if more and w == 0:
                        normalise(n + 1, 1 - u)
                    if more:
                        for i, use in enumerate(uses):
                            if TAKE[use] == w:
                                take(use, i, n + 1, 1 - u, a0)
                    if not first and w == 5:
                        invert(n - 1, 1 - u)
                    if not first and w == 9:
                        divide(n - 1, 1 - u, f0)
                    if not first and w == 12:
                        finish(n - 1, 1 - u, f0)
                    maximum(k, w)

            over_groups_skewed(v, group, steps, 2 * (len(uses) - 1 + 3 + tail.STEPS))
            for w in range(3):
                move(NG * UG + w - 3, UG + w - 3)
            invert(NG - 1, 1)
            divide(NG - 1, 1, LAST)
            finish(NG - 1, 1, LAST)

        @block.scalar
        def _(a):
            def group(n, u, more=True):
                for w in range(UG):
                    k = n * UG + w
                    j, hg = w // NHG, w % NHG
                    a.wait_ge(s["max_ready"], k + 1)
                    a.wait_ge(s["pt_ready"], k + 1)
                    for h in range(NHG):
                        col = j * H + hg * NHG + h
                        nc.scalar.activation(E[w % 4][:, h * 128:(h + 1) * 128], sc[w % 2][:, h * 128:(h + 1) * 128],
                                             ACT.Exp, bias=negm[:, w % 2, h:h + 1],
                                             accum_out=sums[:, u, col:col + 1]).then_inc(s["exp_one"], 1)

            over_groups(a, group)

        @block.tensor
        def _(t):
            credit(t, (s["av_done"], 2), (s["pt_ready"], 4), (s["exp_one"], 2 * NHG))
            t.wait_ge(s["w_in"], 16 * NW)
            t.wait_ge(s["const_ready"], 1)
            t.wait_ge(s["aux_free"], 1)
            nc.tensor.matmul(aux[0][:, 0:128], bvb[:], W["WoT"][:], start=True, stop=True).then_inc(s["aux_full"], 1)
            t.wait_ge(s["aux_free"], 2)
            nc.tensor.matmul(aux[1][:, 0:128], bvb[:], W["WoT"][:], start=True, stop=True).then_inc(s["aux_full"], 1)

            def put(use, i, n, u, a0):
                bank = aux[i % 2]
                if use == "x":
                    t.wait_ge(s["xn_ready"], n + 1)
                t.wait_ge(s["aux_free"], a0 + i + 1)
                if use == "x":
                    for j in range(GB):
                        ins = nc.tensor.transpose(bank[:, j * 128:(j + 1) * 128], xn[u][:, j, :], p.ident[:])
                elif use == "v":
                    for j in range(GB):
                        ins = nc.tensor.matmul(bank[:, j * 128:(j + 1) * 128], cT[u][:, j * 128:(j + 1) * 128],
                                               W["WvT"][:], start=True, stop=True)
                else:
                    if use == "q":
                        t.wait_ge(s["aux_free"], a0 + 3)
                    if use == "k":
                        t.wait_ge(s["c_in0"] if u == 0 else s["c_in1"], (n - u) * 8 + 16)
                    ins = nc.tensor.matmul(bank[:], W[f"W{use}T"][:], (xnT if use[0] == "q" else cT[u])[:],
                                           start=True, stop=True)
                ins.then_inc(s["aux_full"], 1)

            def turn_sums(n, a0):
                t.wait_ge(s["R_ready"], n + 1)
                t.wait_ge(s["aux_free"], a0 + 1)
                for j in range(GB):
                    ins = nc.tensor.transpose(aux[0][:, j * 128:(j + 1) * 128], R[:, j * 128:(j + 1) * 128], p.ident[:])
                ins.then_inc(s["aux_full"], 1)

            def output(n, a0):
                t.wait_ge(s["OT_ready"], n + 3)
                t.wait_ge(s["aux_free"], a0 + 2)
                for j in range(GB):
                    ins = nc.tensor.matmul(aux[1][:, j * 128:(j + 1) * 128], OT[:, j * 128:(j + 1) * 128], W["WoT"][:],
                                           start=True, stop=True)
                ins.then_inc(s["aux_full"], 1)

            def scores(k, w, u):
                j, hg = w // NHG, w % NHG
                t.wait_ge(s["exp_one"], (k + 1) * NHG)
                nc.tensor.matmul(sc[w % 2][:], QS[u][:, hg, j * 128:(j + 1) * 128],
                                 p.KS[u][:, hg, :, j * 128:(j + 1) * 128], start=True, stop=False)
                nc.tensor.matmul(sc[w % 2][:], p.ident16[:], mneg[:].unsqueeze(1).to_broadcast([128, NHG, 128]),
                                 start=False, stop=True).then_inc(s["sc_ready"], 1)

            def turn(k, w):
                t.wait_ge(s["exp_one"], (k + 3) * NHG)
                t.wait_ge(s["pt_moved"], k + 1)
                for c in range(NHG):
                    ins = nc.tensor.transpose(pt[w % 2][:, c * 128:(c + 1) * 128], E[w % 4][:, c * 128:(c + 1) * 128],
                                              p.ident[:])
                ins.then_inc(s["pt_ready"], 1)

            def attend(k, w, u):
                j, hg = w // NHG, w % NHG
                t.wait_ge(s["pt_moved"], k + 3)
                for c in range(NHG):
                    h = hg * NHG + c
                    ins = nc.tensor.matmul(po[u][hg * HW:(hg + 1) * HW, j * 128:(j + 1) * 128],
                                           p.VZ[u][:, j, h * HW:(h + 1) * HW],
                                           PT[w % 2][:, c * 128:(c + 1) * 128], start=(c == 0), stop=(c == NHG - 1))
                ins.then_inc(s["av_done"], 1)

            for i, use in enumerate(uses):
                put(use, i, 0, 0, 2)

            def group(n, u, first, more):
                a0 = project_base(n, first)
                f0 = a0 + PRJ if more else a0
                t.wait_ge(s_qin[u], qcount(n, u))
                t.wait_ge(s_kin[u], kcount(n, u))
                for w in range(UG):
                    k = n * UG + w
                    scores(k, w, u)
                    if not (first and w < 2):
                        turn(k - 2, (w - 2) % UG)
                    if w == 4:
                        t.wait_ge(s["v_ready"], n + 1)
                        t.wait_ge(s["OT_ready"], n + 1)
                    if w >= 4:
                        attend(k - 4, w - 4, u)
                    elif not first:
                        attend(k - 4, w - 4 + UG, 1 - u)
                    if more:
                        for i, use in enumerate(uses):
                            if PUT[use] == w:
                                put(use, i, n + 1, 1 - u, a0)
                    if not first and w == 8:
                        turn_sums(n - 1, f0)
                    if not first and w == 11:
                        output(n - 1, f0)

            over_groups_skewed(t, group)
            for w in range(UG, UG + 4):
                if w < UG + 2:
                    turn((NG - 1) * UG + w - 2, w - 2)
                attend((NG - 1) * UG + w - 4, w - 4, 1)
            turn_sums(NG - 1, LAST)
            output(NG - 1, LAST)


LOW, TAKEN = -3.0e38, -3.3e38


class Router:
    STEPS = 9

    def __init__(self, st, p, name, ne, over_chosen):
        self.st, self.p, self.name, self.ne, self.over_chosen = st, p, name, ne, over_chosen
        self.W = st.sb("rW", [128, ne])
        self.b = st.sb("rb", [128, ne])
        self.L = st.sb("rL", [128, GB, ne + 8])
        self.mr = st.sb("rmr", [128, GB, ne + 8])
        self.top, self.rv = st.sb("rtop", [128, GB, 8]), st.sb("rrv", [128, GB, 8])
        self.E, self.r = st.sb("rE", [128, GB, ne]), st.sb("rr", [128, GB])
        self.G = [st.sb(f"G{u}", [128, GB, ne]) for u in range(2)]
        self.GT = [st.sb(f"GT{u}", [128, 128]) for u in range(2)]
        self.ps = st.bank("route")
        s = lambda k: st.sem("route_" + k)
        self.in_, self.logits, self.diff, self.exp = s("in"), s("logits"), s("diff"), s("exp")
        self.waited, self.turn_waited = s("waited"), s("turn_waited")
        self.G_ready, self.GT_ps, self.GT_ready, self.G_used = s("G_ready"), s("GT_ps"), s("GT_ready"), s("G_used")

    def load(self, eng, d):
        eng.dma_start(self.W[:], d[self.name + "_rW"]).then_inc(self.in_, 16)
        eng.dma_start(self.b[:], d[self.name + "_rb"].to_broadcast([128, self.ne])).then_inc(self.in_, 16)

    def start(self, eng, steps):
        nc = self.st.nc
        nc.vector.memset(self.L[:], LOW)
        steps.link(nc.vector.memset(self.rv[:], LOW))
        eng.wait_ge(self.in_, 32)

    def tensor(self, eng, n, xT):
        nc = self.st.nc
        eng.wait_ge(self.GT_ready, n + 1)
        for j in range(GB):
            ins = nc.tensor.matmul(self.ps[:, j * self.ne:(j + 1) * self.ne], xT[:, j * 128:(j + 1) * 128], self.W[:],
                                   start=True, stop=True)
        ins.then_inc(self.logits, 1)

    def vector(self, eng, n, u, steps):
        nc, ne = self.st.nc, self.ne
        L = self.L[:, :, 0:ne]
        eng.wait_ge(self.logits, n + 1)
        steps.link(nc.vector.tensor_tensor(L, self.ps[:, 0:GB * ne].rearrange("p (a e) -> p a e", a=GB),
                                           self.b[:].unsqueeze(1).to_broadcast([128, GB, ne]), ALU.add))
        stand(eng, self.waited)
        for j in range(GB):
            ins = nc.vector.max(self.top[:, j, :], self.L[:, j, 0:ne])
        steps.link(ins)
        nc.vector.tensor_tensor(self.E[:], L, self.top[:, :, 0:1].to_broadcast([128, GB, ne]), ALU.subtract)\
            .then_inc(self.diff, 1)
        steps.link(nc.vector.tensor_copy(self.rv[:, :, 0:TOPK], self.top[:, :, 0:TOPK]))
        stand(eng, self.waited)
        for j in range(GB):
            ins = nc.vector.match_replace(out=self.mr[:, j, :], in_to_replace=self.rv[:, j, :],
                                          in_values=self.L[:, j, :], imm_value=TAKEN)
        steps.link(ins)
        eng.wait_ge(self.exp, n + 1)
        if not self.over_chosen:
            steps.link(nc.vector.tensor_reduce(self.r[:], self.E[:], AX.X, ALU.add))
        steps.link(nc.vector.scalar_tensor_tensor(self.E[:], self.mr[:, :, 0:ne], TAKEN, self.E[:],
                                                  ALU.is_equal, ALU.mult))
        if self.over_chosen:
            steps.link(nc.vector.tensor_reduce(self.r[:], self.E[:], AX.X, ALU.add))
        steps.link(nc.vector.reciprocal(self.r[:], self.r[:]))
        nc.vector.tensor_tensor(self.G[u][:], self.E[:], self.r[:].unsqueeze(2).to_broadcast([128, GB, ne]), ALU.mult)\
            .then_inc(self.G_ready, 1)
        eng.wait_ge(self.G_ready, n + 1)

    VSTEPS = 7

    def scalar_exp(self, eng, n):
        eng.wait_ge(self.diff, n + 1)
        self.st.nc.scalar.activation(self.E[:], self.E[:], ACT.Exp).then_inc(self.exp, 1)

    def tensor_turn(self, eng, n, u):
        eng.wait_ge(self.G_ready, n + 1)
        stand(eng, self.turn_waited)
        self.st.nc.tensor.transpose(self.ps[0:GB * self.ne, 128:256], self.G[u][:].rearrange("p a e -> p (a e)"),
                                    self.p.ident[:]).then_inc(self.GT_ps, 1)

    def scalar_turn(self, eng, n, u):
        eng.wait_ge(self.GT_ps, n + 1)
        k = GB * self.ne
        self.st.nc.scalar.activation(self.GT[u][0:k, :], self.ps[0:k, 128:256], ACT.Copy).then_inc(self.GT_ready, 1)


def stage_l1_ffn(nc, p, d):
    with Stage(nc, "F1") as st:
        front, tail = Front(st, p), Tail(st, p)
        rt = Router(st, p, "L1F", NR, False)
        WrT = st.sb("WrT", [128, NR, 128])
        Ws = st.sb("Ws", [128, 2, 128])
        blk = st.sb("blk", [GB * NR + 1, GD])
        bs = st.sb("bs", [65, 2, 128])
        acc = st.sb("acc", [128, GB, D])
        EB = 4
        eb, sh = [st.bank(f"e{i}") for i in range(EB)], st.bank("shared")
        s = {k: st.sem(k) for k in ("w_in", "blk_in", "zeroed", "v_step", "ws_ready", "e_ready", "e_used", "xn_done")}
        block = st.block()

        @block.sync
        def _(sp):
            sp.dma_start(Ws[:], d["L1F_WsT"]).then_inc(s["w_in"], 16)
            sp.dma_start(bs[64:65, :, :], d["L1F_bs"]).then_inc(s["w_in"], 16)
            rt.load(sp, d)
            sp.dma_start(WrT[:], d["L1F_WrT"]).then_inc(s["w_in"], 16)
            sp.wait_ge(s["zeroed"], 1)
            for j in range(GB):
                sp.dma_start(blk[j * NR:(j + 1) * NR, j * D:(j + 1) * D], d["L1F_br"]).then_inc(s["blk_in"], 16)

        @block.gpsimd
        def _(g):
            nc.gpsimd.memset(blk[:], 0.0).then_inc(s["zeroed"], 1)
            credit(g, (tail.rstd_done, 2))
            over_groups(g, lambda n, u, more: tail.gpsimd(g, n, u))

        @block.vector
        def _(v):
            steps = Steps(v, s["v_step"])
            credit(v, (tail.var_ready, 1), (s["e_used"], EB + 1))
            rt.start(v, steps)
            front.vector(v, 0, 0)
            nc.vector.memset(rt.GT[0][64:65, :], 1.0)
            nc.vector.memset(rt.GT[1][64:65, :], 1.0)
            v.wait_ge(s["w_in"], 48)
            v.wait_ge(s["zeroed"], 1)
            steps.link(nc.vector.tensor_tensor(Ws[:, 0, :], Ws[:, 0, :], Ws[:, 1, :], ALU.add))
            steps.link(nc.vector.tensor_scalar(Ws[:, 0, :], Ws[:, 0, :], 0.5, None, ALU.mult))
            steps.link(nc.vector.tensor_tensor(bs[64:65, 0, :], bs[64:65, 0, :], bs[64:65, 1, :], ALU.add))
            steps.link(nc.vector.tensor_scalar(blk[64:65, :].rearrange("p (a o) -> p a o", a=GB),
                                               bs[64:65, 0:1, :].to_broadcast([1, GB, D]), 0.5, None, ALU.mult))
            v.sem_inc(s["ws_ready"], 1)
            rt.vector(v, 0, 0, steps)

            def group(n, u, more):
                xg = xgroup(p, n)
                k = n * (NR + 1)
                v.wait_ge(s["e_ready"], k + 1)
                steps.link(nc.vector.tensor_tensor(acc[:], sh[:].rearrange("p (a o) -> p a o", a=GB), front.xn[u][:], ALU.add))
                v.sem_inc(s["e_used"], 1)
                for e in range(NR):
                    v.wait_ge(s["e_ready"], k + e + 2)
                    for j in range(GB):
                        ins = nc.vector.scalar_tensor_tensor(acc[:, j, :], eb[e % EB][:, j * 128:(j + 1) * 128],
                                                             rt.G[u][:, j, e:e + 1], acc[:, j, :], ALU.mult, ALU.add)
                    ins.then_inc(s["e_used"], 1)
                    v.wait_ge(s["e_used"], EB + 1 + k + e + 2)
                    if e == 4 and more:
                        front.vector(v, n + 1, 1 - u)
                    if e == 9 and more:
                        rt.vector(v, n + 1, 1 - u, steps)
                tail.vector(v, n, u, steps, nc.vector.scalar_tensor_tensor(xg, acc[:], p.gate[:, 5:6], xg, ALU.mult, ALU.add))

            over_groups(v, group, steps, 2 * (1 + rt.VSTEPS + tail.STEPS))

        @block.scalar
        def _(a):
            credit(a, (front.xnT_ready, 1), (rt.GT_ready, 1))
            front.scalar(a, 0, 0)
            rt.scalar_exp(a, 0)
            rt.scalar_turn(a, 0, 0)

            def group(n, u, more):
                if more:
                    front.scalar(a, n + 1, 1 - u)
                    rt.scalar_exp(a, n + 1)
                    rt.scalar_turn(a, n + 1, 1 - u)

            over_groups(a, group)

        @block.tensor
        def _(t):
            credit(t, (front.xn_used, 2), (front.xnT_used, 2))
            front.tensor(t, 0, 0)
            t.wait_ge(s["w_in"], 48)
            t.wait_ge(s["blk_in"], 64)
            t.wait_ge(s["ws_ready"], 1)
            t.wait_ge(front.xnT_ready, 2)
            rt.tensor(t, 0, front.xnT[0])
            rt.tensor_turn(t, 0, 0)

            def group(n, u, more):
                k = n * (NR + 1)
                t.wait_ge(rt.GT_ready, n + 2)
                t.wait_ge(s["e_used"], k + 2)
                for j in range(GB):
                    nc.tensor.matmul(sh[:, j * 128:(j + 1) * 128], front.xnT[u][:, j * 128:(j + 1) * 128], Ws[:, 0, :],
                                     start=(j == 0), stop=False, skip_group_check=True)
                nc.tensor.matmul(sh[:], rt.GT[u][0:65, :], blk[:], start=False, stop=True, skip_group_check=True)\
                    .then_inc(s["e_ready"], 1)
                for e in range(NR):
                    t.wait_ge(s["e_used"], k + e + 3)
                    for j in range(GB):
                        ins = nc.tensor.matmul(eb[e % EB][:, j * 128:(j + 1) * 128],
                                               front.xnT[u][:, j * 128:(j + 1) * 128], WrT[:, e, :], start=True, stop=True)
                    ins.then_inc(s["e_ready"], 1)
                    if e == 6 and more:
                        front.tensor(t, n + 1, 1 - u)
                    if e == 8 and more:
                        t.wait_ge(front.xnT_ready, n + 3)
                        rt.tensor(t, n + 1, front.xnT[1 - u])
                    if e == 13 and more:
                        rt.tensor_turn(t, n + 1, 1 - u)
                t.wait_ge(s["e_ready"], k + NR + 1)
                t.sem_inc(front.xnT_used, 1)
                t.sem_inc(front.xn_used, 1)

            over_groups(t, group)


def stage_l2_attn(nc, p, d):
    SCALE = float(np.sqrt(D // 16))
    with Stage(nc, "A2") as st:
        front, tail = Front(st, p), Tail(st, p)
        cT, cN = st.sb("cT", [128, B, S]), st.sb("cN", [128, B, D])
        negm, sums = st.sb("negm", [128, GB]), st.sb("sums", [128, GB])
        E, PT = st.sb("E", [128, GD]), st.sb("PT", [128, GD])
        sc, pt, po = st.bank("sc"), st.bank("pt"), st.bank("po")
        s = {k: st.sem(k) for k in ("c_in", "v_step", "sc_ready", "max_ready", "exp_done", "pt_ready", "pt_moved", "po_ready")}
        block = st.block()

        @block.sync
        def _(sp):
            sp.dma_start(cT[:], d["ctxT"]).then_inc(s["c_in"], 16)
            sp.dma_start(cN[:], d["ctx"]).then_inc(s["c_in"], 16)

        @block.gpsimd
        def _(g):
            credit(g, (tail.rstd_done, 2))
            over_groups(g, lambda n, u, more: tail.gpsimd(g, n, u))

        @block.vector
        def _(v):
            steps = Steps(v, s["v_step"])
            credit(v, (tail.var_ready, 1), (s["pt_moved"], 1))
            front.vector(v, 0, 0)

            def group(n, u, more):
                xg = xgroup(p, n)
                v.wait_ge(s["sc_ready"], n + 1)
                steps.link(nc.vector.tensor_reduce(negm[:], sc[:].rearrange("p (a k) -> p a k", a=GB), AX.X, ALU.max, negate=True))
                steps.link(nc.vector.tensor_scalar(negm[:], negm[:], SCALE, None, ALU.mult))
                v.sem_inc(s["max_ready"], 1)
                if more:
                    front.vector(v, n + 1, 1 - u)
                v.wait_ge(s["pt_ready"], n + 1)
                nc.vector.tensor_copy(PT[:], pt[:]).then_inc(s["pt_moved"], 1)
                steps.link(nc.vector.reciprocal(sums[:], sums[:]))
                steps.link(nc.vector.tensor_scalar(sums[:], sums[:], p.gate[:, 2:3], None, ALU.mult))
                v.wait_ge(s["po_ready"], n + 1)
                for j in range(GB):
                    xj = p.X[:, bass.ds(n * GB + j, 1), :].rearrange("p a d -> p (a d)")
                    ins = nc.vector.scalar_tensor_tensor(xj, po[:, j * 128:(j + 1) * 128], sums[:, j:j + 1], xj, ALU.mult, ALU.add)
                tail.vector(v, n, u, steps, ins)

            over_groups(v, group, steps, 2 * (4 + tail.STEPS))

        @block.scalar
        def _(a):
            credit(a, (front.xnT_ready, 1))
            front.scalar(a, 0, 0)

            def group(n, u, more):
                a.wait_ge(s["max_ready"], n + 1)
                for j in range(GB):
                    ins = nc.scalar.activation(E[:, j * 128:(j + 1) * 128], sc[:, j * 128:(j + 1) * 128], ACT.Exp,
                                               bias=negm[:, j:j + 1], scale=SCALE, accum_out=sums[:, j:j + 1])
                    ins.then_inc(s["exp_done"], 1)
                if more:
                    front.scalar(a, n + 1, 1 - u)

            over_groups(a, group)

        @block.tensor
        def _(t):
            credit(t, (front.xn_used, 2), (front.xnT_used, 2))
            front.tensor(t, 0, 0)
            t.wait_ge(s["c_in"], 32)

            def group(n, u, more):
                t.wait_ge(front.xnT_ready, n + 2)
                for j in range(GB):
                    ins = nc.tensor.matmul(sc[:, j * 128:(j + 1) * 128], front.xnT[u][:, j * 128:(j + 1) * 128],
                                           cT[:, bass.ds(n * GB + j, 1), :].rearrange("p a k -> p (a k)"), start=True, stop=True)
                ins.then_inc(s["sc_ready"], 1)
                if more:
                    front.tensor(t, n + 1, 1 - u)
                t.wait_ge(s["exp_done"], (n + 1) * GB)
                t.sem_inc(front.xn_used, 1)
                t.sem_inc(front.xnT_used, 1)
                t.wait_ge(s["pt_moved"], n + 1)
                for j in range(GB):
                    ins = nc.tensor.transpose(pt[:, j * 128:(j + 1) * 128], E[:, j * 128:(j + 1) * 128], p.ident[:])
                ins.then_inc(s["pt_ready"], 1)
                t.wait_ge(s["pt_moved"], n + 2)
                t.wait_ge(tail.var_ready, n + 1)
                for j in range(GB):
                    ins = nc.tensor.matmul(po[:, j * 128:(j + 1) * 128], PT[:, j * 128:(j + 1) * 128],
                                           cN[:, bass.ds(n * GB + j, 1), :].rearrange("p a k -> p (a k)"), start=True, stop=True)
                ins.then_inc(s["po_ready"], 1)

            over_groups(t, group)


def stage_l2_route(nc, p, d):
    with Stage(nc, "R2") as st:
        front = Front(st, p)
        W = st.sb("W", [128, NX])
        E, m = st.sb("E", [128, GB, NX]), st.sb("m", [128, GB])
        work = [st.sb(f"work{i}", [128, S]) for i in range(2)]
        PT = [st.sb(f"PT{i}", [128, S]) for i in range(2)]
        top = st.sb("top", [128, 2, 8])
        ps, tp = st.bank("ps"), st.bank("tp")
        s = {k: st.sem(k) for k in ("w_in", "v_step", "logits", "diff", "exp", "P_ready", "t1", "t2", "G_ready")}
        block = st.block()

        @block.sync
        def _(sp):
            sp.dma_start(W[:], d["L2_gate_w"]).then_inc(s["w_in"], 16)

        @block.vector
        def _(v):
            steps = Steps(v, s["v_step"])
            credit(v, (s["P_ready"], 1))
            front.vector(v, 0, 0)

            def group(n, u, more):
                if more:
                    front.vector(v, n + 1, 1 - u)
                v.wait_ge(s["logits"], n + 1)
                lg = ps[:, 0:GB * NX].rearrange("p (a e) -> p a e", a=GB)
                steps.link(nc.vector.tensor_reduce(m[:], lg, AX.X, ALU.max))
                nc.vector.tensor_tensor(E[:], lg, m[:].unsqueeze(2).to_broadcast([128, GB, NX]), ALU.subtract)\
                    .then_inc(s["diff"], 1)
                v.wait_ge(s["exp"], n + 1)
                steps.link(nc.vector.tensor_reduce(m[:], E[:], AX.X, ALU.add))
                steps.link(nc.vector.reciprocal(m[:], m[:]))
                nc.vector.tensor_tensor(p.G2[:, bass.ds(n * GB, GB), :], E[:], m[:].unsqueeze(2).to_broadcast([128, GB, NX]),
                                        ALU.mult).then_inc(s["P_ready"], 1)
                v.wait_ge(s["P_ready"], n + 2)

            over_groups(v, group, steps, 2 * 3)
            v.wait_ge(s["t1"], 1)
            for i in range(2):
                nc.vector.tensor_copy(work[i][:], tp[:, i * 128:(i + 1) * 128])
                ins = nc.vector.tensor_copy(PT[i][:], tp[:, i * 128:(i + 1) * 128])
            steps.link(ins)
            for r in range(CAP // 8):
                for i in range(2):
                    ins = nc.vector.max(top[:, i, :], work[i][:])
                steps.link(ins)
                for i in range(2):
                    ins = nc.vector.match_replace(out=work[i][:], in_to_replace=top[:, i, :], in_values=work[i][:],
                                                  imm_value=-1.0)
                steps.link(ins)
            for i in range(2):
                ins = nc.vector.scalar_tensor_tensor(PT[i][:], work[i][:], -1.0, PT[i][:], ALU.is_equal, ALU.mult)
            steps.link(ins)
            v.sem_inc(s["G_ready"], 1)
            v.wait_ge(s["t2"], 1)
            for i in range(2):
                ins = nc.vector.tensor_copy(p.G2[:, i * 16:(i + 1) * 16, :],
                                            tp[:, 256 + i * 128:256 + (i + 1) * 128].rearrange("p (a e) -> p a e", e=NX))
            steps.link(ins)

        @block.scalar
        def _(a):
            credit(a, (front.xnT_ready, 1))
            front.scalar(a, 0, 0)

            def group(n, u, more):
                if more:
                    front.scalar(a, n + 1, 1 - u)
                a.wait_ge(s["diff"], n + 1)
                nc.scalar.activation(E[:], E[:], ACT.Exp).then_inc(s["exp"], 1)

            over_groups(a, group)

        @block.tensor
        def _(t):
            credit(t, (front.xn_used, 2), (front.xnT_used, 2))
            front.tensor(t, 0, 0)
            t.wait_ge(s["w_in"], 16)

            def group(n, u, more):
                t.wait_ge(front.xnT_ready, n + 2)
                if more:
                    front.tensor(t, n + 1, 1 - u)
                t.wait_ge(s["P_ready"], n + 1)
                for j in range(GB):
                    ins = nc.tensor.matmul(ps[:, j * NX:(j + 1) * NX], front.xnT[u][:, j * 128:(j + 1) * 128], W[:],
                                           start=True, stop=True)
                ins.then_inc(s["logits"], 1)
                t.wait_ge(s["logits"], n + 1)
                t.sem_inc(front.xn_used, 1)
                t.sem_inc(front.xnT_used, 1)

            over_groups(t, group)
            t.wait_ge(s["P_ready"], NG + 1)
            for i in range(2):
                ins = nc.tensor.transpose(tp[:, i * 128:(i + 1) * 128],
                                          p.G2[:, i * 16:(i + 1) * 16, :].rearrange("p a e -> p (a e)"), p.ident[:])
            ins.then_inc(s["t1"], 1)
            t.wait_ge(s["G_ready"], 1)
            for i in range(2):
                ins = nc.tensor.transpose(tp[:, 256 + i * 128:256 + (i + 1) * 128], PT[i][:], p.ident[:])
            ins.then_inc(s["t2"], 1)


def stage_ffn(nc, p, d, name, gate, routed):
    with Stage(nc, name) as st:
        front, tail = Front(st, p), Tail(st, p)
        rt = Router(st, p, name, NX, True) if routed else None
        w1, w2 = st.sb("w1", [128, NX, FF]), st.sb("w2", [128, NX, FC, 128])
        b1 = st.sb("b1", [128, NX, FC])
        blk = st.sb("blk", [GB * NX, GD])
        hT = [st.sb(f"hT{i}", [128, GD]) for i in range(2 * FC)]
        acc = st.sb("acc", [128, GB, D])
        hb = [st.bank(f"h{i}") for i in range(2)]
        yb = [st.bank(f"y{i}") for i in range(2)]
        ib = st.bank("init")
        s = {k: st.sem(k) for k in ("w_in", "blk_in", "zeroed", "v_step", "h_ps", "h_ready", "y_ready", "y_used",
                                    "init_ready", "init_used")}
        NH = NX * FC
        block = st.block()

        @block.sync
        def _(sp):
            if routed:
                rt.load(sp, d)
                sp.dma_start(b1[:], d[name + "_b1"]).then_inc(s["w_in"], 16)
                sp.wait_ge(s["zeroed"], 1)
                for j in range(GB):
                    sp.dma_start(blk[j * NX:(j + 1) * NX, j * D:(j + 1) * D], d[name + "_b2"]).then_inc(s["blk_in"], 16)
            sp.dma_start(w1[:], d[name + "_w1"]).then_inc(s["w_in"], 16)
            sp.dma_start(w2[:], d[name + "_w2"]).then_inc(s["w_in"], 16)

        @block.gpsimd
        def _(g):
            nc.gpsimd.memset(blk[:], 0.0).then_inc(s["zeroed"], 1)
            credit(g, (tail.rstd_done, 2))
            over_groups(g, lambda n, u, more: tail.gpsimd(g, n, u))

        @block.vector
        def _(v):
            steps = Steps(v, s["v_step"])
            credit(v, (tail.var_ready, 1), (s["y_used"], 2), (s["init_used"], 1))
            front.vector(v, 0, 0)
            if routed:
                rt.start(v, steps)
                rt.vector(v, 0, 0, steps)

            def group(n, u, more):
                xg = xgroup(p, n)
                if routed:
                    v.wait_ge(s["init_ready"], n + 1)
                    steps.link(nc.vector.tensor_copy(acc[:], ib[:].rearrange("p (a o) -> p a o", a=GB)))
                    v.sem_inc(s["init_used"], 1)
                for e in range(NX):
                    k = n * NX + e
                    v.wait_ge(s["y_ready"], k + 3)
                    for j in range(GB):
                        y = yb[e % 2][:, j * 128:(j + 1) * 128]
                        if routed:
                            g = rt.G[u][:, j, e:e + 1]
                        else:
                            g = p.G2[:, bass.ds(n * GB + j, 1), e:e + 1].rearrange("p a e -> p (a e)")
                        if routed or e:
                            ins = nc.vector.scalar_tensor_tensor(acc[:, j, :], y, g, acc[:, j, :], ALU.mult, ALU.add)
                        else:
                            ins = nc.vector.tensor_scalar(acc[:, j, :], y, g, None, ALU.mult)
                    ins.then_inc(s["y_used"], 1)
                    v.wait_ge(s["y_used"], k + 3)
                    if e == 1 and more:
                        front.vector(v, n + 1, 1 - u)
                    if e == 3 and more and routed:
                        rt.vector(v, n + 1, 1 - u, steps)
                tail.vector(v, n, u, steps, nc.vector.scalar_tensor_tensor(xg, acc[:], p.gate[:, gate:gate + 1], xg,
                                                                           ALU.mult, ALU.add))

            over_groups(v, group, steps, 2 * (tail.STEPS + ((1 + rt.VSTEPS) if routed else 0)))

        @block.scalar
        def _(a):
            credit(a, (front.xnT_ready, 1), (s["h_ready"], 2))
            if routed:
                a.sem_inc(rt.GT_ready, 1)
            front.scalar(a, 0, 0)
            if routed:
                rt.scalar_exp(a, 0)
                rt.scalar_turn(a, 0, 0)
            a.wait_ge(s["w_in"], 48 if routed else 32)

            def group(n, u, more):
                for e in range(NX):
                    for c in range(FC):
                        k = n * NH + e * FC + c
                        if c == 0:
                            a.wait_ge(s["y_ready"], n * NX + e + 1)
                        a.wait_ge(s["h_ps"], k + 1)
                        nc.scalar.activation(hT[(e % 2) * FC + c][:], hb[c % 2][:], ACT.Gelu,
                                             bias=b1[:, e, c:c + 1] if routed else 0.0).then_inc(s["h_ready"], 1)
                    if e == 2 and more:
                        front.scalar(a, n + 1, 1 - u)
                    if e == 4 and more and routed:
                        rt.scalar_exp(a, n + 1)
                    if e == 5 and more and routed:
                        rt.scalar_turn(a, n + 1, 1 - u)

            over_groups(a, group)

        @block.tensor
        def _(t):
            credit(t, (front.xn_used, 2), (front.xnT_used, 2), (s["y_ready"], 2))
            front.tensor(t, 0, 0)
            t.wait_ge(front.xnT_ready, 2)
            if routed:
                rt_in = rt.in_
                t.wait_ge(rt_in, 32)
                rt.tensor(t, 0, front.xnT[0])
                rt.tensor_turn(t, 0, 0)
                t.wait_ge(s["blk_in"], 64)
            t.wait_ge(s["w_in"], 48 if routed else 32)

            def second(n, e):
                k = n * NX + e
                t.wait_ge(s["h_ready"], k * FC + FC + 2)
                t.wait_ge(s["y_used"], k + 1)
                for j in range(GB):
                    for c in range(FC):
                        ins = nc.tensor.matmul(yb[e % 2][:, j * 128:(j + 1) * 128],
                                               hT[(e % 2) * FC + c][:, j * 128:(j + 1) * 128], w2[:, e, c, :],
                                               start=(c == 0), stop=(c == FC - 1))
                ins.then_inc(s["y_ready"], 1)

            def group(n, u, more):
                t.wait_ge(front.xnT_ready, n + 2)
                if routed:
                    t.wait_ge(rt.GT_ready, n + 2)
                    t.wait_ge(s["init_used"], n + 1)
                    nc.tensor.matmul(ib[:], rt.GT[u][0:GB * NX, :], blk[:], start=True, stop=True).then_inc(s["init_ready"], 1)
                for e in range(NX):
                    for c in range(FC):
                        k = n * NH + e * FC + c
                        t.wait_ge(s["h_ready"], k + 1)
                        nc.tensor.matmul(hb[c % 2][:], w1[:, e, c * 128:(c + 1) * 128], front.xnT[u][:],
                                         start=True, stop=True).then_inc(s["h_ps"], 1)
                    if e:
                        second(n, e - 1)
                    if e == 2 and more:
                        front.tensor(t, n + 1, 1 - u)
                    if e == 3 and more and routed:
                        t.wait_ge(front.xnT_ready, n + 3)
                        rt.tensor(t, n + 1, front.xnT[1 - u])
                    if e == 5 and more and routed:
                        rt.tensor_turn(t, n + 1, 1 - u)
                t.wait_ge(s["h_ps"], (n + 1) * NH)
                t.sem_inc(front.xnT_used, 1)
                t.sem_inc(front.xn_used, 1)
                second(n, NX - 1)

            over_groups(t, group)


def stage_out(nc, p, out):
    with Stage(nc, "O") as st:
        stored = st.sem("stored")
        block = st.block()

        @block.sync
        def _(sp):
            sp.dma_start(out, p.X[:]).then_inc(stored, 16)
            sp.wait_ge(stored, 16)


class P:
    pass


def build(nc, d, out, layers=range(1, 9)):
    ctx = ExitStack()
    with ctx:
        p = P()

        def sb(name, shape, dt=F32, at=ctx):
            return at.enter_context(nc.sbuf_tensor(name, shape, dt))

        p.X = sb("X", [128, B, D])
        p.mean, p.rstd, p.mhalf = sb("mean", [128, B]), sb("rstd", [128, B]), sb("mhalf", [128, B])
        p.gate, p.ident = sb("gate", [128, 8]), sb("ident", [128, 128])
        p.ident16 = sb("ident16", [128, 128], BF16)
        stage_a(nc, p, d)
        if 2 in layers:
            with ExitStack() as l0:
                p.ones16, p.bias3 = sb("ones16", [128, 128], BF16, l0), sb("bias3", [128, NE_L0], BF16, l0)
                XtT, Yt = sb("XtT", [128, NE_L0], F32, l0), sb("Yt", [128, NE_L0 // 128, 128], F32, l0)
                stage_b1(nc, p, d, XtT)
                stage_mid(nc, p, d, XtT, Yt)
                stage_b2(nc, p, d, Yt)
        p.KS = [sb(f"KS{u}", [3 * HW, NHG, NHG, GD], F32R) for u in range(2)]
        p.VZ = [sb(f"VZ{u}", [128, GB, H * HW]) for u in range(2)]
        p.G2 = sb("G2", [128, B, NX])
        if 3 in layers:
            stage_attn(nc, p, d, "L1", 1, True, True)
        if 4 in layers:
            stage_l1_ffn(nc, p, d)
        if 5 in layers:
            stage_l2_attn(nc, p, d)
        if 6 in layers:
            stage_l2_route(nc, p, d)
            stage_ffn(nc, p, d, "F2", 6, False)
        if 7 in layers:
            stage_attn(nc, p, d, "L3", 3, False, 3 not in layers)
        if 8 in layers:
            stage_ffn(nc, p, d, "F3", 7, True)
        stage_out(nc, p, out)


def attn_layouts(name, n, c, w, rope):
    out = {}
    rot = np.arange(D).reshape(H, 2, HD // 2)[:, ::-1].reshape(D)
    for k in "qkvo":
        out[f"{name}_W{k}T"] = c(n(w[f"{name}_xattn_W{k}"]).T)
    for k in "qkv":
        out[f"{name}_b{k}"] = c(n(w[f"{name}_xattn_b{k}"]).reshape(D, 1))
    out[f"{name}_bo"] = c(n(w[f"{name}_xattn_bo"]).reshape(1, D))
    if rope:
        for k in "qk":
            out[f"{name}_W{k}rT"] = c(n(w[f"{name}_xattn_W{k}"])[rot].T)
            out[f"{name}_b{k}r"] = c(n(w[f"{name}_xattn_b{k}"])[rot].reshape(D, 1))
    return out


def rope_tables():
    half = HD // 2
    inv = (1.0 / 10000.0 ** (np.arange(half, dtype=np.float32) / half)).astype(np.float32)
    ang = np.arange(S, dtype=np.float32)[None, :] * inv[:, None]
    cos, sin = np.cos(ang).astype(np.float32), np.sin(ang).astype(np.float32)
    cos = np.tile(np.concatenate([cos, cos]), (H, 1))
    sin = np.tile(np.concatenate([-sin, sin]), (H, 1))
    sc = np.float32(HD ** -0.5)
    return {"cosk": cos, "sink": sin, "cosq": cos * sc, "sinq": sin * sc}


def layouts(x, itok_S_0_31, ctx_1024, mask_1x1xSxS2_ik0, g_xattn, g_ffn, **w):
    c = np.ascontiguousarray
    n = lambda a: np.asarray(a)
    return {
        "x": c(n(x).transpose(1, 0, 2)),
        "itok": c(n(itok_S_0_31).reshape(1, S)),
        "ctxT_rows": c(n(ctx_1024).transpose(0, 2, 1)),
        "g_xattn": c(n(g_xattn)), "g_ffn": c(n(g_ffn)),
        "phiT": c(n(w["L0_ffn_phi_w"]).T), "phi_b": c(n(w["L0_ffn_phi_b"]).reshape(1, -1)),
        "phiT_slots": c(n(w["L0_ffn_phi_w"]).reshape(NL, NP, D).transpose(2, 1, 0).reshape(D, -1)),
        "phi_b_slots": c(n(w["L0_ffn_phi_b"]).reshape(NL, NP).T.reshape(1, -1)),
        "expert_w": c(n(w["L0_ffn_expert_w"]).transpose(1, 0, 2)), "expert_b": c(n(w["L0_ffn_expert_b"])),
        "sel_expert": np.repeat(np.eye(NL, dtype=np.float32), NP, axis=1),
        "ident": np.eye(128, dtype=np.float32),
        "ctxT": c(n(ctx_1024).transpose(2, 0, 1)), "ctx": c(n(ctx_1024).transpose(1, 0, 2)),
        "L1_mask": np.tril(np.ones((S, S), np.int32)), "L3_mask": c(n(mask_1x1xSxS2_ik0).reshape(S, S)),
        "L1F_rW": c(n(w["L1_ffn_centroids"]).T), "L1F_rb": c(n(w["L1_ffn_expert_biases"]).reshape(1, NR)),
        "L1F_WrT": c(n(w["L1_ffn_Wr"]).transpose(2, 0, 1)), "L1F_br": c(n(w["L1_ffn_br"])),
        "L1F_WsT": c(n(w["L1_ffn_Ws"]).transpose(2, 0, 1)), "L1F_bs": c(n(w["L1_ffn_bs"]).reshape(1, 2, D)),
        "L2_gate_w": c(n(w["L2_ffn_gate_w"])),
        "F2_w1": c(n(w["L2_ffn_w1"]).transpose(1, 0, 2)),
        "F2_w2": c(n(w["L2_ffn_w2"]).reshape(NX, FC, 128, D).transpose(2, 0, 1, 3)),
        "F3_rW": c(n(w["L3_ffn_gate_w"])), "F3_rb": c(n(w["L3_ffn_gate_b"]).reshape(1, NX)),
        "F3_w1": c(n(w["L3_ffn_w1"]).transpose(1, 0, 2)),
        "F3_w2": c(n(w["L3_ffn_w2"]).reshape(NX, FC, 128, D).transpose(2, 0, 1, 3)),
        "F3_b1": c(n(w["L3_ffn_b1"]).reshape(NX, FC, 128).transpose(2, 0, 1)), "F3_b2": c(n(w["L3_ffn_b2"])),
        **rope_tables(), **attn_layouts("L1", n, c, w, True), **attn_layouts("L3", n, c, w, False),
    }


def kernel(**inputs):
    import concourse.bacc as _bacc
    from concourse.bass_utils import run_bass_kernel_spmd as _run

    nc = _bacc.Bacc("TRN2", target_bir_lowering=False, num_devices=1)
    arrays = layouts(**inputs)
    d = {k: nc.dram_tensor(f"in_{k}", a.shape, mybir.dt.from_np(a.dtype), kind="ExternalInput").ap()
         for k, a in arrays.items()}
    out = nc.dram_tensor("out_x", (S, B, D), F32, kind="ExternalOutput").ap()
    build(nc, d, out)
    r = _run(nc, [{f"in_{k}": a for k, a in arrays.items()}], core_ids=[0])
    return r.results[0]["out_x"].transpose(1, 0, 2)
```

```python
import numpy as np
from contextlib import ExitStack

import concourse.bass as bass
from concourse import mybir

F32 = mybir.dt.float32
F32R = mybir.dt.float32r
BF16 = mybir.dt.bfloat16
I32 = mybir.dt.int32
ALU = mybir.AluOpType
ACT = mybir.ActivationFunctionType
AX = mybir.AxisListType

B, S, D = 32, 128, 128
GB = 4
NG = B // GB
GD = GB * D
EPS = 1e-5
NL, NP = 64, 32
NE_L0 = NL * NP
H, HD = 16, 8
NR = 16
NX, FF = 8, 512
FC = FF // 128
CAP = 32
TOPK = 2
NEG = -(2.0 ** 100)


class Steps:

    def __init__(self, eng, sem):
        self.eng, self.sem, self.base, self.k = eng, sem, 0, 0

    def link(self, ins):
        ins.then_inc(self.sem, 1)
        self.k += 1
        self.eng.wait_ge(self.sem, self.base + self.k)

    def mark(self, ins):
        ins.then_inc(self.sem, 1)
        self.k += 1
        return self.k

    def need(self, k):
        self.eng.wait_ge(self.sem, self.base + k)

    def loop(self, n, i, per):
        self.start = self.base + self.k
        self.per, self.n = per, n
        self.base, self.k = i * per + self.start, 0

    def end(self):
        assert self.k == self.per, (self.k, self.per)
        self.base, self.k = self.start + self.n * self.per, 0


class Stage:

    def __init__(self, nc, name):
        self.nc, self.name, self.ctx, self.sems = nc, name, ExitStack(), []

    def __enter__(self):
        return self

    def __exit__(self, *a):
        self.ctx.__exit__(*a)
        if a[0] is None:
            self.nc.clear_and_free_semaphores(self.sems)
            self.nc.all_engine_barrier()

    def sb(self, name, shape, dt=F32):
        return self.ctx.enter_context(self.nc.sbuf_tensor(f"{self.name}_{name}", shape, dt))

    def bank(self, name, dt=F32):
        return self.ctx.enter_context(self.nc.psum_tensor(f"{self.name}_{name}", [128, 512], dt))

    def sem(self, name):
        self.sems.append(self.nc.alloc_semaphore(f"{self.name}_{name}"))
        return self.sems[-1]

    def block(self):
        return self.ctx.enter_context(self.nc.Block())


class Front:

    def __init__(self, st, p):
        self.st, self.p = st, p
        self.xn = [st.sb(f"xn{u}", [128, GB, D]) for u in range(2)]
        self.xnT = [st.sb(f"xnT{u}", [128, GD]) for u in range(2)]
        self.ps = st.bank("frontT")
        self.xn_ready = st.sem("xn_ready")
        self.xn_used = st.sem("xn_used")
        self.xnT_ps = st.sem("xnT_ps")
        self.xnT_ready = st.sem("xnT_ready")
        self.xnT_used = st.sem("xnT_used")

    def vector(self, eng, n, u, counted=True):
        nc, p = self.st.nc, self.p
        if counted:
            eng.wait_ge(self.xn_used, n + 1)
        for j in range(GB):
            b = n * GB + j
            ins = nc.vector.tensor_scalar(self.xn[u][:, j, :], p.X[:, bass.ds(b, 1), :].rearrange("p a d -> p (a d)"),
                                          p.mean[:, bass.ds(b, 1)], p.rstd[:, bass.ds(b, 1)],
                                          ALU.subtract, ALU.mult)
        ins.then_inc(self.xn_ready, 1)

    def tensor(self, eng, n, u):
        nc = self.st.nc
        eng.wait_ge(self.xn_ready, n + 1)
        eng.wait_ge(self.xnT_ready, n + 1)
        for j in range(GB):
            ins = nc.tensor.transpose(self.ps[:, j * D:(j + 1) * D], self.xn[u][:, j, :], self.p.ident[:])
        ins.then_inc(self.xnT_ps, 1)

    def scalar(self, eng, n, u, counted=True):
        nc = self.st.nc
        eng.wait_ge(self.xnT_ps, n + 1)
        if counted:
            eng.wait_ge(self.xnT_used, n + 1)
        nc.scalar.activation(self.xnT[u][:], self.ps[:], ACT.Copy).then_inc(self.xnT_ready, 1)


def stand(eng, waited):
    eng.sem_inc(waited, 1)


def credit(eng, *pairs):
    for sem, n in pairs:
        eng.sem_inc(sem, n)


class Tail:
    STEPS = 3

    def __init__(self, st, p):
        self.st, self.p = st, p
        self.stats = st.sb("bn", [128, GB, 6])
        self.mv = st.sb("mv", [128, 2, GB, 2])
        self.var_ready = st.sem("var_ready")
        self.rstd_done = st.sem("rstd_done")
        self.waited = st.sem("tail_waited")

    def vector(self, eng, n, u, steps, last):
        if last is not None:
            steps.link(last)
        steps.need(self.row_stats(eng, n, u, steps))
        steps.need(self.combine(eng, n, u, steps))
        self.hand_over(eng, n, u)

    def row_stats(self, eng, n, u, steps):
        nc, p = self.st.nc, self.p
        stand(eng, self.waited)
        for j in range(GB):
            ins = nc.vector.bn_stats(self.stats[:, j, :], p.X[:, bass.ds(n * GB + j, 1), :].rearrange("p a d -> p (a d)"))
        return steps.mark(ins)

    def combine(self, eng, n, u, steps):
        eng.wait_ge(self.rstd_done, n + 1)
        stand(eng, self.waited)
        for j in range(GB):
            ins = self.st.nc.vector.bn_aggr(self.mv[:, u, j, :], self.stats[:, j, :])
        return steps.mark(ins)

    def hand_over(self, eng, n, u):
        nc = self.st.nc
        stand(eng, self.waited)
        nc.vector.tensor_copy(self.p.mean[:, bass.ds(n * GB, GB)], self.mv[:, u, :, 0])
        nc.vector.tensor_scalar(self.mv[:, u, :, 1], self.mv[:, u, :, 1], EPS, None, ALU.add)\
            .then_inc(self.var_ready, 1)

    def gpsimd(self, eng, n, u):
        nc, p = self.st.nc, self.p
        eng.wait_ge(self.var_ready, n + 2)
        nc.gpsimd.tensor_tensor(p.rstd[:, bass.ds(n * GB, GB)], self.mv[:, u, :, 1], p.mhalf[:, 0:GB], ALU.pow)\
            .then_inc(self.rstd_done, 1)


def over_groups(eng, body, steps=None, per=0):
    with eng.Fori(0, NG // 2 - 1) as i:
        if steps:
            steps.loop(NG // 2 - 1, i, per)
        body(i * 2, 0, True)
        body(i * 2 + 1, 1, True)
        if steps:
            steps.end()
    body(NG - 2, 0, True)
    body(NG - 1, 1, False)


def over_groups_skewed(eng, body, steps=None, per=0):
    body(0, 0, True, True)
    body(1, 1, False, True)
    with eng.Fori(0, NG // 2 - 2) as i:
        if steps:
            steps.loop(NG // 2 - 2, i, per)
        body(i * 2 + 2, 0, False, True)
        body(i * 2 + 3, 1, False, True)
        if steps:
            steps.end()
    body(NG - 2, 0, False, True)
    body(NG - 1, 1, False, False)


def xgroup(p, n):
    return p.X[:, bass.ds(n * GB, GB), :]


def bias_parts(eng, steps, raw, bias3):
    for rows in (96, 64, 32):
        steps.link(eng.tensor_copy(bias3[0:rows, :], raw[0:rows, :]))
        if rows > 32:
            steps.link(eng.tensor_tensor(raw[0:rows - 32, :], raw[0:rows - 32, :], bias3[0:rows - 32, :], ALU.subtract))


def stage_a(nc, p, d):
    PB = 16
    with Stage(nc, "A") as st:
        xn = [st.sb(f"xn{u}", [128, GB, D]) for u in range(2)]
        xnT = st.sb("xnT", [128, B, S])
        wring = [st.sb(f"wring{u}", [128, PB, D]) for u in range(2)]
        yT = st.sb("yT", [128, B, S])
        ctxT = st.sb("ctxT", [128, B, D])
        stats = st.sb("stats", [128, B, 6])
        raw = [st.sb(f"raw{i}", [96, NE_L0]) for i in range(2)]
        itok = st.sb("itok", [1, S], I32)
        graw = st.sb("graw", [128, 8])
        front = [st.bank(f"front{u}") for u in range(2)]
        pos = [st.bank(f"pos{u}") for u in range(2)]
        x_in = [st.sem(f"x_in{g}") for g in range(NG)]
        g_in, tok_in, const_in = st.sem("g_in"), st.sem("tok_in"), st.sem("const_in")
        mh_ready, var_ready, rstd_ready, v_step = st.sem("mh"), st.sem("var"), st.sem("rstd"), st.sem("v_step")
        xn_ready, xT_ps, xT_ready = st.sem("xn_ready"), st.sem("xT_ps"), st.sem("xT_ready")
        ctx_in, w_ready = st.sem("ctx_in"), [st.sem(f"w_ready{u}") for u in range(2)]
        w_waited = [st.sem(f"w_waited{u}") for u in range(2)]
        w_used, y_ps, y_out = st.sem("w_used"), st.sem("y_ps"), st.sem("y_out")
        yt_ps, x_new, gate_ready = st.sem("yt_ps"), st.sem("x_new"), st.sem("gate_ready")
        pool_done, g_step = st.sem("pool_done"), st.sem("g_step")
        l0_in, raw_zero, raw_in = st.sem("l0_in"), st.sem("raw_zero"), [st.sem(f"raw_in{i}") for i in range(2)]
        block = st.block()

        def pick(eng, i, u, engine, copy):
            s0 = (i * 2 + u) * PB
            _, toks = nc.values_load_multi_w_load_instructions(itok[0:1, bass.ds(s0, PB)], engines=[engine],
                                                               min_val=0, max_val=B - 1)
            for q, tok in enumerate(toks):
                eng.wait_ge(w_used, s0 + q + 1)
                stand(eng, w_waited[u])
                copy(wring[u][:, q, :], ctxT[:, bass.ds(tok, 1), :].rearrange("p a o -> p (a o)")).then_inc(w_ready[u], 1)

        @block.sync
        def _(sp):
            sp.dma_start(itok[:], d["itok"]).then_inc(tok_in, 16)
            for g in range(NG):
                sp.dma_start(p.X[:, g * GB:(g + 1) * GB, :], d["x"][:, g * GB:(g + 1) * GB, :]).then_inc(x_in[g], 16)
            sp.dma_start(p.ident[:], d["ident"]).then_inc(const_in, 16)
            sp.dma_start(ctxT[:], d["ctxT"]).then_inc(ctx_in, 16)
            sp.wait_ge(raw_zero, 1)
            for i, name in enumerate(("phi_b", "phi_b_slots")):
                for row in range(3):
                    sp.dma_start(raw[i][32 * row:32 * row + 1, :], d[name]).then_inc(raw_in[i], 16)
            for i, name in enumerate(("phiT", "phiT_slots")):
                sp.dma_start(p.phiT[i][:], d[name]).then_inc(l0_in, 16)
            sp.dma_start(p.ew[:], d["expert_w"]).then_inc(l0_in, 16)
            sp.wait_ge(l0_in, 48)

        @block.gpsimd
        def _(g):
            for dst, src in ((graw[:, 0:4], d["g_xattn"]), (graw[:, 4:8], d["g_ffn"])):
                g.dma_start(dst, src.rearrange("(a n) -> a n", a=1).to_broadcast([128, 4])).then_inc(g_in, 16)
            nc.gpsimd.memset(p.mhalf[:], -0.5).then_inc(mh_ready, 1)
            g.wait_ge(mh_ready, 1)
            g.wait_ge(var_ready, 1)
            nc.gpsimd.tensor_tensor(p.rstd[:], stats[:, :, 1], p.mhalf[:], ALU.pow).then_inc(rstd_ready, 1)
            steps = Steps(g, g_step)
            nc.gpsimd.memset(raw[0][:], 0.0)
            nc.gpsimd.memset(raw[1][:], 0.0).then_inc(raw_zero, 1)
            nc.gpsimd.memset(p.ones16[:], 1.0)
            for i in range(2):
                steps.link(nc.gpsimd.memset(p.bias3[i][:], 0.0))
                g.wait_ge(raw_in[i], 48)
                bias_parts(nc.gpsimd, steps, raw[i], p.bias3[i])
            for n in range(NG):
                g.wait_ge(x_new, n + 1)
                nc.gpsimd.tensor_tensor(p.rstd[:, n * GB:(n + 1) * GB], stats[:, n * GB:(n + 1) * GB, 1],
                                        p.mhalf[:, 0:GB], ALU.pow).then_inc(pool_done, 1)

        @block.vector
        def _(v):
            steps = Steps(v, v_step)
            mv = stats
            for g in range(NG):
                v.wait_ge(x_in[g], 16)
                for b in range(g * GB, (g + 1) * GB):
                    ins = nc.vector.bn_stats(xnT[:, b, 0:6], p.X[:, b, :])
            steps.link(ins)
            for b in range(B):
                ins = nc.vector.bn_aggr(mv[:, b, 0:2], xnT[:, b, 0:6])
            steps.link(ins)
            nc.vector.tensor_copy(p.mean[:], mv[:, :, 0])
            steps.link(nc.vector.tensor_scalar(mv[:, :, 1], mv[:, :, 1], EPS, None, ALU.add))
            v.sem_inc(var_ready, 1)
            v.wait_ge(const_in, 16)
            nc.vector.tensor_copy(p.ident16[:], p.ident[:])
            v.wait_ge(rstd_ready, 1)
            for g in range(NG):
                if g >= 2:
                    v.wait_ge(xT_ps, g - 1)
                for j in range(GB):
                    b = g * GB + j
                    ins = nc.vector.tensor_scalar(xn[g % 2][:, j, :], p.X[:, b, :], p.mean[:, b:b + 1],
                                                  p.rstd[:, b:b + 1], ALU.subtract, ALU.mult)
                ins.then_inc(xn_ready, 1)
            v.wait_ge(tok_in, 16)
            v.wait_ge(ctx_in, 16)
            with v.Fori(0, S // PB // 2) as i:
                pick(v, i, 0, mybir.EngineType.DVE, nc.vector.tensor_copy)
            v.wait_ge(gate_ready, 1)
            for g in range(NG):
                v.wait_ge(yt_ps, g + 1)
                xg = p.X[:, g * GB:(g + 1) * GB, :]
                steps.link(nc.vector.scalar_tensor_tensor(xg, front[g % 2][:].rearrange("p (a d) -> p a d", a=GB),
                                                          p.gate[:, 0:1], xg, ALU.mult, ALU.add))
                for j in range(GB):
                    ins = nc.vector.bn_stats(xn[0][:, j, 0:6], p.X[:, g * GB + j, :])
                steps.link(ins)
                for j in range(GB):
                    ins = nc.vector.bn_aggr(mv[:, g * GB + j, 0:2], xn[0][:, j, 0:6])
                steps.link(ins)
                nc.vector.tensor_copy(p.mean[:, g * GB:(g + 1) * GB], mv[:, g * GB:(g + 1) * GB, 0])
                steps.link(nc.vector.tensor_scalar(mv[:, g * GB:(g + 1) * GB, 1], mv[:, g * GB:(g + 1) * GB, 1],
                                                   EPS, None, ALU.add))
                v.sem_inc(x_new, 1)

        @block.scalar
        def _(a):
            a.wait_ge(g_in, 32)
            nc.scalar.activation(p.gate[:], graw[:], ACT.Tanh).then_inc(gate_ready, 1)
            for g in range(NG):
                a.wait_ge(xT_ps, g + 1)
                nc.scalar.activation(xnT[:, g * GB:(g + 1) * GB, :],
                                     front[g % 2][:].rearrange("p (a d) -> p a d", a=GB), ACT.Copy).then_inc(xT_ready, 1)
            a.wait_ge(tok_in, 16)
            a.wait_ge(ctx_in, 16)
            with a.Fori(0, S // PB // 2) as i:
                pick(a, i, 1, mybir.EngineType.Activation,
                     lambda dst, x: nc.scalar.activation(dst, x, ACT.Copy))
                for u in range(2):
                    k = i * 2 + u
                    a.wait_ge(y_ps, k + 1)
                    nc.scalar.activation(yT[:, :, bass.ds(k * PB, PB)],
                                         pos[u][:].rearrange("p (s b) -> p b s", s=PB), ACT.Copy).then_inc(y_out, 1)

        @block.tensor
        def _(t):
            t.wait_ge(const_in, 16)
            for g in range(NG):
                t.wait_ge(xn_ready, g + 1)
                if g >= 2:
                    t.wait_ge(xT_ready, g - 1)
                for j in range(GB):
                    ins = nc.tensor.transpose(front[g % 2][:, j * D:(j + 1) * D], xn[g % 2][:, j, :], p.ident[:])
                ins.then_inc(xT_ps, 1)
            t.wait_ge(xT_ready, NG)
            credit(t, (y_out, 2), (w_used, 2 * PB))
            with t.Fori(0, S // PB // 2) as i:
                for u in range(2):
                    k = i * 2 + u
                    t.wait_ge(y_out, k + 1)
                    for q in range(PB):
                        t.wait_ge(w_ready[u], i * PB + q + 1)
                        ins = nc.tensor.matmul(pos[u][:, q * B:(q + 1) * B], wring[u][:, q, :],
                                               xnT[:, :, bass.ds(k * PB + q, 1)].rearrange("p b a -> p (b a)"),
                                               start=True, stop=True)
                        ins.then_inc(w_used, 1)
                    t.wait_ge(w_used, (k * PB) + PB + 2 * PB)
                    t.sem_inc(y_ps, 1)
            t.wait_ge(y_out, S // PB + 2)
            for g in range(NG):
                if g >= 2:
                    t.wait_ge(x_new, g - 1)
                for j in range(GB):
                    ins = nc.tensor.transpose(front[g % 2][:, j * D:(j + 1) * D], yT[:, g * GB + j, :], p.ident[:])
                ins.then_inc(yt_ps, 1)


class SoftUnit:
    RING = 4

    def __init__(self, st, size, probs_used, phiT, bias3):
        self.st, self.size, self.ng = st, size, 512 // size
        self.phiT, self.bias3 = phiT, bias3
        self.banks = [st.bank(f"logits{i}") for i in range(2)]
        self.E = [st.sb(f"E{i}", [128, 512]) for i in range(self.RING)]
        self.m = st.sb("m", [128, 2, self.ng])
        self.r = st.sb("r", [128, 2, self.ng])
        self.logits_ready = st.sem("logits_ready")
        self.max_done = st.sem("max_done")
        self.diff_done = st.sem("diff_done")
        self.exp_done = st.sem("exp_done")
        self.sum_done = st.sem("sum_done")
        self.inverse_done = st.sem("inverse_done")
        self.probs_ready = st.sem("probs_ready")
        self.probs_used = probs_used

    def bank(self, w):
        return self.banks[w % 2]

    def grouped(self, w):
        return self.E[w % self.RING][:].rearrange("p (n q) -> p n q", q=self.size)

    def tensor_logits(self, eng, k, w, xT, q, p):
        nc = self.st.nc
        eng.wait_ge(self.diff_done, k + 1)
        nc.tensor.matmul(self.bank(w)[:], xT, self.phiT[:, q * 512:(q + 1) * 512], start=True, stop=False)
        nc.tensor.matmul(self.bank(w)[:], p.ones16[:], self.bias3[:, q * 512:(q + 1) * 512], start=False, stop=True)\
            .then_inc(self.logits_ready, 1)

    def vector(self, eng, k, w, prev):
        nc = self.st.nc
        lg = self.bank(w)[:].rearrange("p (n q) -> p n q", q=self.size)
        eng.wait_ge(self.logits_ready, k + 1)
        nc.vector.tensor_reduce(self.m[:, w % 2, :], lg, AX.X, ALU.max).then_inc(self.max_done, 1)
        if prev:
            self.vector_sum(eng, k - 1, w - 1)
        eng.wait_ge(self.max_done, k + 1)
        eng.wait_ge(self.probs_used, k + 1)
        nc.vector.tensor_tensor(self.grouped(w), lg, self.m[:, w % 2, :].unsqueeze(2)
                                .to_broadcast([128, self.ng, self.size]), ALU.subtract).then_inc(self.diff_done, 1)
        if prev:
            self.vector_inverse(eng, k - 1, w - 1)

    def vector_sum(self, eng, k, w):
        eng.wait_ge(self.exp_done, k + 1)
        eng.wait_ge(self.probs_ready, k + 1)
        self.st.nc.vector.tensor_reduce(self.r[:, w % 2, :], self.grouped(w), AX.X, ALU.add).then_inc(self.sum_done, 1)

    def vector_inverse(self, eng, k, w):
        r = self.r[:, w % 2, :]
        eng.wait_ge(self.sum_done, k + 1)
        self.st.nc.vector.reciprocal(r, r).then_inc(self.inverse_done, 1)

    def scalar_exp(self, eng, k, w):
        e = self.E[w % self.RING][:]
        eng.wait_ge(self.diff_done, k + 3)
        self.st.nc.scalar.activation(e, e, ACT.Exp).then_inc(self.exp_done, 1)

    def gpsimd(self, eng, k, w):
        e = self.grouped(w)
        eng.wait_ge(self.inverse_done, k + 1)
        self.st.nc.gpsimd.tensor_tensor(e, e, self.r[:, w % 2, :].unsqueeze(2)
                                        .to_broadcast([128, self.ng, self.size]), ALU.mult).then_inc(self.probs_ready, 1)


NQ = NE_L0 // 512
UG = GB * NQ


def stage_b1(nc, p, d, XtT):
    LAG = 3
    with Stage(nc, "B1") as st:
        front = Front(st, p)
        probs_used = st.sem("probs_used")
        soft = SoftUnit(st, NP, probs_used, p.phiT[0], p.bias3[0])
        acc = [st.bank(f"acc{q}") for q in range(NQ)]
        zero = st.sb("zero", [128, 512], BF16)
        consts, acc_done = st.sem("consts"), st.sem("acc_done")
        block = st.block()

        @block.gpsimd
        def _(g):
            nc.gpsimd.memset(zero[:], 0.0).then_inc(consts, 1)
            credit(g, (soft.probs_ready, 2))
            over_groups_skewed(g, lambda n, u, first, more: [soft.gpsimd(g, n * UG + w, w) for w in range(UG)])

        @block.vector
        def _(v):
            credit(v, (soft.diff_done, 2))
            front.vector(v, 0, 0, False)

            def group(n, u, first, more):
                for w in range(UG):
                    soft.vector(v, n * UG + w, w, not (first and w == 0))
                    if w == UG // 2 and more:
                        v.wait_ge(probs_used, n * UG + soft.RING)
                        front.vector(v, n + 1, 1 - u, False)

            over_groups_skewed(v, group)
            soft.vector_sum(v, NG * UG - 1, UG - 1)
            soft.vector_inverse(v, NG * UG - 1, UG - 1)
            v.wait_ge(acc_done, 1)
            for q in range(NQ):
                nc.vector.tensor_copy(XtT[:, q * 512:(q + 1) * 512], acc[q][:])

        @block.scalar
        def _(a):
            credit(a, (front.xnT_ready, 1))
            front.scalar(a, 0, 0, False)

            def group(n, u, first, more):
                for w in range(UG):
                    soft.scalar_exp(a, n * UG + w, w)
                    if w == UG // 2 and more:
                        if not first:
                            a.wait_ge(soft.logits_ready, n * UG)
                        front.scalar(a, n + 1, 1 - u, False)

            over_groups_skewed(a, group)

        @block.tensor
        def _(t):
            credit(t, (probs_used, soft.RING))
            front.tensor(t, 0, 0)
            t.wait_ge(consts, 1)
            for q in range(NQ):
                nc.tensor.matmul(acc[q][:], zero[:, 0:128], zero[:], start=True, stop=False, skip_group_check=True)

            def dispatch(k, w, u):
                t.wait_ge(soft.probs_ready, k + 3)
                nc.tensor.matmul(acc[w % NQ][:], front.xn[u][:, w // NQ, :], soft.E[w % soft.RING][:],
                                 start=False, stop=False, skip_group_check=True).then_inc(probs_used, 1)

            def group(n, u, first, more):
                t.wait_ge(front.xnT_ready, n + 2)
                for w in range(UG):
                    j = w // NQ
                    soft.tensor_logits(t, n * UG + w, w, front.xnT[u][:, j * 128:(j + 1) * 128], w % NQ, p)
                    if w >= LAG:
                        dispatch(n * UG + w - LAG, w - LAG, u)
                    elif not first:
                        dispatch(n * UG + w - LAG, w - LAG + UG, 1 - u)
                    if w == UG // 2 and more:
                        front.tensor(t, n + 1, 1 - u)

            over_groups_skewed(t, group)
            for w in range(UG - LAG, UG):
                dispatch((NG - 1) * UG + w, w, 1)
            for q in range(NQ):
                ins = nc.tensor.matmul(acc[q][:], zero[:, 0:128], zero[:], start=False, stop=True, skip_group_check=True)
            ins.then_inc(acc_done, 1)


def stage_mid(nc, p, d, XtT, Yt):
    NC = NE_L0 // 128
    with Stage(nc, "M") as st:
        eb = st.sb("eb", [NL, 128])
        sel = st.sb("sel", [NL, NE_L0])
        xt = st.sb("xt", [128, NC, D])
        xtn = st.sb("xtn", [128, NC, D])
        yn = st.sb("yn", [128, NC, D])
        stats, mv, rs = st.sb("stats", [128, NC, 6]), st.sb("mv", [128, NC, 2]), st.sb("rs", [128, NC])
        banks = [st.bank(f"b{q}") for q in range(4)]
        ybanks = [st.bank(f"y{q}") for q in range(4)]
        scratch = nc.dram_tensor("slots_scratch", (NP, NL, 128), F32, kind="Internal").ap()
        ew_in, tr, v_step, var_ready, rs_ready = st.sem("ew_in"), st.sem("tr"), st.sem("v_step"), st.sem("var"), st.sem("rs")
        norm, th, tr2, back, y_ps, y_sb = st.sem("norm"), st.sem("th"), st.sem("tr2"), st.sem("back"), st.sem("y_ps"), st.sem("y_sb")
        put, got = st.sem("put"), st.sem("got")
        block = st.block()

        @block.sync
        def _(sp):
            sp.dma_start(eb[:], d["expert_b"]).then_inc(ew_in, 16)
            sp.dma_start(sel[:], d["sel_expert"]).then_inc(ew_in, 16)
            sp.wait_ge(y_sb, 4)
            for a4 in range(4):
                sp.dma_start(scratch.rearrange("s (c a) h -> a s c h", a=4)[a4], yn[32 * a4:32 * a4 + 32, :, :])\
                    .then_inc(put, 16)
            sp.wait_ge(put, 64)
            sp.dma_start(Yt[:], scratch.rearrange("(c s) n h -> (s n) c h", s=2)).then_inc(got, 16)
            sp.wait_ge(got, 16)

        @block.gpsimd
        def _(g):
            g.wait_ge(var_ready, 1)
            nc.gpsimd.tensor_tensor(rs[:], mv[:, :, 1], p.mhalf[:, 0:NC], ALU.pow).then_inc(rs_ready, 1)

        @block.vector
        def _(v):
            steps = Steps(v, v_step)
            for q in range(4):
                v.wait_ge(tr, q + 1)
                steps.link(nc.vector.tensor_scalar(xt[:, 4 * q:4 * q + 4, :], banks[q][:].rearrange("p (c d) -> p c d", c=4),
                                                   -33000.0, 65000.0, ALU.max, ALU.min))
            for c in range(NC):
                ins = nc.vector.bn_stats(stats[:, c, :], xt[:, c, :])
            steps.link(ins)
            for c in range(NC):
                ins = nc.vector.bn_aggr(mv[:, c, :], stats[:, c, :])
            steps.link(ins)
            nc.vector.tensor_scalar(mv[:, :, 1], mv[:, :, 1], EPS, None, ALU.add).then_inc(var_ready, 1)
            v.wait_ge(rs_ready, 1)
            for c in range(NC):
                nc.vector.tensor_scalar(xtn[:, c, :], xt[:, c, :], mv[:, c, 0:1], rs[:, c:c + 1],
                                        ALU.subtract, ALU.mult).then_inc(norm, 1)
            for q in range(4):
                v.wait_ge(tr2, q + 1)
                nc.vector.tensor_copy(XtT[:, q * 512:(q + 1) * 512], banks[q][:]).then_inc(back, 1)

        @block.scalar
        def _(a):
            for q in range(4):
                a.wait_ge(norm, 4 * q + 4)
                x4 = xtn[:, 4 * q:4 * q + 4, :]
                nc.scalar.activation(x4, x4, ACT.Tanh).then_inc(th, 1)
            for q in range(4):
                a.wait_ge(y_ps, q + 1)
                nc.scalar.activation(yn[:, 4 * q:4 * q + 4, :], ybanks[q][:].rearrange("p (c d) -> p c d", c=4),
                                     ACT.Copy).then_inc(y_sb, 1)

        @block.tensor
        def _(t):
            for q in range(4):
                for c in range(4 * q, 4 * q + 4):
                    ins = nc.tensor.transpose(banks[q][:, (c % 4) * 128:(c % 4 + 1) * 128], XtT[:, c * 128:(c + 1) * 128],
                                              p.ident[:])
                ins.then_inc(tr, 1)
            for q in range(4):
                t.wait_ge(th, q + 1)
                for c in range(4 * q, 4 * q + 4):
                    ins = nc.tensor.transpose(banks[q][:, (c % 4) * 128:(c % 4 + 1) * 128], xtn[:, c, :], p.ident[:])
                ins.then_inc(tr2, 1)
            t.wait_ge(ew_in, 32)
            for q in range(4):
                t.wait_ge(back, q + 1)
                for c in range(4 * q, 4 * q + 4):
                    cols = slice((c % 4) * 128, (c % 4 + 1) * 128)
                    nc.tensor.matmul(ybanks[q][:, cols], sel[:, c * 128:(c + 1) * 128], eb[:], start=True, stop=False,
                                     skip_group_check=True)
                    for a4 in range(4):
                        e = 4 * c + a4
                        ins = nc.tensor.matmul(ybanks[q][32 * a4:32 * a4 + 32, cols], XtT[:, e * NP:(e + 1) * NP],
                                               p.ew[:, e, :], start=False, stop=True, skip_group_check=True)
                ins.then_inc(y_ps, 1)


def stage_b2(nc, p, d, Yt):
    LAG = 3
    with Stage(nc, "B2") as st:
        front, tail = Front(st, p), Tail(st, p)
        ct_ready = st.sem("ct_ready")
        soft = SoftUnit(st, NL, ct_ready, p.phiT[1], p.bias3[1])
        ct_ps = [st.bank(f"ct{i}") for i in range(2)]
        y_ps = [st.bank(f"y{i}") for i in range(2)]
        CT = [st.sb(f"CT{i}", [128, 512]) for i in range(2)]
        v_step = st.sem("v_step")
        ct_moved, ct_used = st.sem("ct_moved"), st.sem("ct_used")
        block = st.block()

        @block.gpsimd
        def _(g):
            credit(g, (tail.rstd_done, 2))
            credit(g, (soft.probs_ready, 2))

            def group(n, u, first, more):
                for w in range(UG):
                    soft.gpsimd(g, n * UG + w, w)
                    if w == 10 and not first:
                        tail.gpsimd(g, n - 1, 1 - u)

            over_groups_skewed(g, group)
            tail.gpsimd(g, NG - 1, 1)

        @block.vector
        def _(v):
            steps = Steps(v, v_step)
            credit(v, (soft.diff_done, 2), (tail.var_ready, 1))
            front.vector(v, 0, 0, False)

            def finish(n, u):
                v.wait_ge(ct_used, (n + 1) * UG + 2)
                tail.vector(v, n, u, steps, nc.vector.scalar_tensor_tensor(
                    xgroup(p, n), y_ps[u][:].rearrange("p (a d) -> p a d", a=GB), p.gate[:, 4:5], xgroup(p, n),
                    ALU.mult, ALU.add))

            def group(n, u, first, more):
                for w in range(UG):
                    soft.vector(v, n * UG + w, w, not (first and w == 0))
                    if w == 4 and more:
                        v.wait_ge(ct_ready, n * UG + soft.RING)
                        front.vector(v, n + 1, 1 - u, False)
                    if w == 8 and not first:
                        finish(n - 1, 1 - u)

            over_groups_skewed(v, group, steps, 2 * tail.STEPS)
            soft.vector_sum(v, NG * UG - 1, UG - 1)
            soft.vector_inverse(v, NG * UG - 1, UG - 1)
            finish(NG - 1, 1)

        @block.scalar
        def _(a):
            credit(a, (front.xnT_ready, 1), (ct_moved, 2))
            front.scalar(a, 0, 0, False)

            def move(k, w):
                a.wait_ge(ct_ready, k + 1 + soft.RING)
                a.wait_ge(ct_used, k + 1)
                nc.scalar.activation(CT[w % 2][:], ct_ps[w % 2][:], ACT.Copy).then_inc(ct_moved, 1)

            def group(n, u, first, more):
                for w in range(UG):
                    soft.scalar_exp(a, n * UG + w, w)
                    if not (first and w < LAG):
                        move(n * UG + w - LAG, w - LAG)
                    if w == UG // 2 and more:
                        if not first:
                            a.wait_ge(soft.logits_ready, n * UG)
                        front.scalar(a, n + 1, 1 - u, False)

            over_groups_skewed(a, group)
            for w in range(UG - LAG, UG):
                move((NG - 1) * UG + w, w)

        @block.tensor
        def _(t):
            credit(t, (ct_ready, soft.RING), (ct_used, 2))
            front.tensor(t, 0, 0)

            def turn(k, w):
                t.wait_ge(soft.probs_ready, k + 3)
                t.wait_ge(ct_moved, k + 1)
                for c in range(4):
                    ins = nc.tensor.transpose(ct_ps[w % 2][:, c * 128:(c + 1) * 128],
                                              soft.E[w % soft.RING][:, c * 128:(c + 1) * 128], p.ident[:])
                ins.then_inc(ct_ready, 1)

            def combine(k, w, u):
                t.wait_ge(ct_moved, k + 3)
                j, q = w // NQ, w % NQ
                for c in range(4):
                    ins = nc.tensor.matmul(y_ps[u][:, j * 128:(j + 1) * 128], CT[w % 2][:, c * 128:(c + 1) * 128],
                                           Yt[:, 4 * q + c, :], start=(q == 0 and c == 0), stop=(q == 3 and c == 3))
                ins.then_inc(ct_used, 1)

            def group(n, u, first, more):
                t.wait_ge(front.xnT_ready, n + 2)
                for w in range(UG):
                    j, k = w // NQ, n * UG + w
                    soft.tensor_logits(t, k, w, front.xnT[u][:, j * 128:(j + 1) * 128], w % NQ, p)
                    if not (first and w < LAG):
                        turn(k - LAG, (w - LAG) % UG)
                    if w == LAG + 1 and not first:
                        t.wait_ge(tail.var_ready, n)
                    if w > LAG:
                        combine(k - LAG - 1, w - LAG - 1, u)
                    elif not first:
                        combine(k - LAG - 1, w - LAG - 1 + UG, 1 - u)
                    if w == UG // 2 and more:
                        front.tensor(t, n + 1, 1 - u)

            over_groups_skewed(t, group)
            for w in range(UG, UG + LAG + 1):
                if w < UG + LAG:
                    turn((NG - 1) * UG + w - LAG, w - LAG)
                combine((NG - 1) * UG + w - LAG - 1, w - LAG - 1, 1)


NHG = 4
HW = NHG * HD


def stage_attn(nc, p, d, name, gate, rope, first):
    PRJ = 6 if rope else 4
    AUX = PRJ + 2
    LAST = (NG - 1) * AUX + PRJ + 2
    uses = ["x", "q", "qr", "k", "kr", "v"] if rope else ["x", "q", "k", "v"]
    PUT = {"x": 1, "q": 3, "qr": 4, "k": 5, "kr": 6, "v": 7}
    TAKE = {"x": 2, "q": 4, "qr": 5, "k": 6, "kr": 7, "v": 9}

    def project_base(n, first):
        return 2 + PRJ if first else n * AUX + PRJ

    with Stage(nc, name) as st:
        xn = [st.sb(f"xn{u}", [128, GB, D]) for u in range(2)]
        xnT = st.sb("xnT", [128, GD])
        cT = [st.sb(f"cT{u}", [128, GD]) for u in range(2)]
        wn = ["WqT", "WkT", "WvT", "WoT"] + (["WqrT", "WkrT"] if rope else [])
        W_all = st.sb("W", [128, len(wn), 128])
        W = {k: W_all[:, i, :] for i, k in enumerate(wn)}
        bn = ["bq", "bk", "bv"] + (["bqr", "bkr"] if rope else [])
        bias_all = st.sb("bias", [128, len(bn)])
        bias = {k: bias_all[:, i:i + 1] for i, k in enumerate(bn)}
        if rope:
            tab_all = st.sb("tab", [128, 4, S])
            tab = {k: tab_all[:, i, :] for i, k in enumerate(("cosq", "sinq", "cosk", "sink"))}
        bo, gcb, bvb = st.sb("bo", [128, 128]), st.sb("gcb", [128, 128]), st.sb("bvb", [128, 128])
        mi, mneg = st.sb("mi", [128, 128], I32), st.sb("mneg", [128, 128], BF16)
        t1 = {k: st.sb(f"t1{k}", [128, GD]) for k in "qk"}
        t2 = {k: st.sb(f"t2{k}", [128, GD]) for k in "qk"} if rope else None
        hi = {k: st.sb(f"{k}hi", [128, GD], F32R) for k in "qk"}
        lo = {k: st.sb(f"{k}lo", [128, GD], F32R) for k in "qk"}
        QS = [st.sb(f"QS{u}", [3 * HW, NHG, GD], F32R) for u in range(2)]
        VZ = [st.sb(f"VZ{u}", [128, GB, H * HW]) for u in range(2)]
        negm = st.sb("negm", [128, 2, NHG])
        sums = st.sb("sums", [128, 2, GB * H])
        E = [st.sb(f"E{i}", [128, 512]) for i in range(4)]
        PT = [st.sb(f"PT{i}", [128, 512]) for i in range(2)]
        R = st.sb("R", [128, GD])
        rT, OT = st.sb("rT", [128, GD]), st.sb("OT", [128, GD])
        tail = Tail(st, p)
        aux = [st.bank(f"aux{i}") for i in range(2)]
        sc = [st.bank(f"sc{i}") for i in range(2)]
        pt = [st.bank(f"pt{i}") for i in range(2)]
        po = [st.bank(f"po{i}") for i in range(2)]
        s = {k: st.sem(k) for k in (
            "w_in", "c_in0", "c_in1", "v_step", "xn_ready", "aux_full", "aux_free",
            "q_split", "k_split", "q_put", "k_put", "sc_ready", "max_ready",
            "pt_ready", "pt_moved", "av_done", "v_ready", "const_ready", "zeroed", "VZ_zeroed", "R_ready", "OT_ready", "exp_one")}
        s_qin = [st.sem(f"q_in{u}") for u in range(2)]
        s_kin = [st.sem(f"k_in{u}") for u in range(2)]
        NW = 5 if rope else 4
        split_d = {k: [nc.dram_tensor(f"{name}_{k}split{u}", (2, 128, GD), F32, kind="Internal").ap() for u in range(2)]
                   for k in "qk"}

        def qcount(n, u):
            return (n - u) * (8 * 3) + 16 * 3

        def kcount(n, u):
            return (n - u) * (8 * 3 * NHG) + 16 * 3 * NHG

        block = st.block()

        @block.sync
        def _(sp):
            def load_ctx(n, u):
                sp.dma_start(cT[u][:].rearrange("p (a d) -> p a d", a=GB), d["ctxT"][:, bass.ds(n * GB, GB), :])\
                    .then_inc(s["c_in0"] if u == 0 else s["c_in1"], 16)

            load_ctx(0, 0)
            sp.dma_start(W_all[:], d[f"{name}_W"]).then_inc(s["w_in"], 16)
            sp.dma_start(bias_all[:], d[f"{name}_b"]).then_inc(s["w_in"], 16)
            if rope:
                sp.dma_start(tab_all[:], d["rope"]).then_inc(s["w_in"], 16)
            sp.dma_start(bo[:], d[f"{name}_bo"].to_broadcast([128, 128])).then_inc(s["w_in"], 16)
            sp.dma_start(mi[:], d[f"{name}_mask"]).then_inc(s["w_in"], 16)

            def spread(n, u):
                for k in "qk":
                    sp.wait_ge(s[k + "_split"], n + 1)
                    for i, part in enumerate((hi[k], lo[k])):
                        sp.dma_start(split_d[k][u][i], part[:].bitcast(F32)).then_inc(s[k + "_put"], 16)
                sp.wait_ge(s["q_put"], (n + 1) * 32)
                for r, i in enumerate((0, 0, 1)):
                    sp.dma_start(QS[u][r * HW:(r + 1) * HW, :, :].bitcast(F32),
                                 split_d["q"][u][i].rearrange("(g p) k -> p g k", g=NHG)).then_inc(s_qin[u], 16)
                sp.wait_ge(s["k_put"], (n + 1) * 32)
                for r, i in enumerate((0, 1, 0)):
                    for h4 in range(NHG):
                        sp.dma_start(p.KS[u][r * HW + h4 * HD:r * HW + (h4 + 1) * HD, :, h4, :].bitcast(F32),
                                     split_d["k"][u][i].rearrange("(g h p) k -> h p g k", g=NHG, h=NHG)[h4])\
                            .then_inc(s_kin[u], 16)

            load_ctx(1, 1)
            sp.wait_ge(s["zeroed"], 1)
            spread(0, 0)
            sp.wait_ge(s["zeroed"], 2)

            with sp.Fori(0, NG // 2 - 1) as i:
                for u in range(2):
                    n = i * 2 + u
                    sp.wait_ge(s["aux_full"], n * AUX + PRJ + 2)
                    load_ctx(n + 2, u)
                    sp.wait_ge(s["av_done"], n * UG + 2)
                    spread(n + 1, 1 - u)
            sp.wait_ge(s["av_done"], (NG - 2) * UG + 2)
            spread(NG - 1, 1)

        @block.gpsimd
        def _(g):
            if first:
                nc.gpsimd.memset(p.KS[0][:].bitcast(F32), 0.0).then_inc(s["zeroed"], 1)
            else:
                g.sem_inc(s["zeroed"], 1)
            for u in range(2):
                nc.gpsimd.memset(VZ[u][:], 0.0).then_inc(s["VZ_zeroed"], 1)
            if first:
                nc.gpsimd.memset(p.KS[1][:].bitcast(F32), 0.0).then_inc(s["zeroed"], 1)
            else:
                g.sem_inc(s["zeroed"], 1)
            credit(g, (tail.rstd_done, 2))
            over_groups(g, lambda n, u, more: tail.gpsimd(g, n, u))

        @block.vector
        def _(v):
            steps = Steps(v, s["v_step"])
            credit(v, (s["aux_free"], 2), (tail.var_ready, 1), (s["pt_moved"], 2), (s["OT_ready"], 2))

            def normalise(n, u):
                for j in range(GB):
                    b = n * GB + j
                    ins = nc.vector.tensor_scalar(xn[u][:, j, :], p.X[:, bass.ds(b, 1), :].rearrange("p a d -> p (a d)"),
                                                  p.mean[:, bass.ds(b, 1)], p.rstd[:, bass.ds(b, 1)],
                                                  ALU.subtract, ALU.mult)
                ins.then_inc(s["xn_ready"], 1)

            normalise(0, 0)
            v.wait_ge(s["w_in"], 16 * NW)
            nc.vector.tensor_scalar(mneg[:], mi[:], 0.0, NEG, ALU.is_equal, ALU.mult)
            steps.link(nc.vector.tensor_copy(bvb[:], bias["bv"][:].to_broadcast([128, 128])))
            v.sem_inc(s["const_ready"], 1)

            def rotate(k, n, a0):
                v.wait_ge(s["aux_free"], a0 + (5 if k == "k" else 3) + 2)
                return steps.mark(nc.vector.tensor_tensor(t1[k][:], t1[k][:], t2[k][:], ALU.add))

            def upper(k, n, ready):
                if not (isinstance(n, int) and n == 0):
                    v.wait_ge(s[k + "_put"], n * 32)
                ready()
                return steps.mark(nc.vector.tensor_copy(hi[k][:], t1[k][:]))

            def lower(k, mark):
                steps.need(mark)
                nc.vector.tensor_tensor(lo[k][:], t1[k][:], hi[k][:].bitcast(F32), ALU.subtract)\
                    .then_inc(s[k + "_split"], 1)

            def take(use, i, n, u, a0):
                bank = aux[i % 2]
                v.wait_ge(s["aux_full"], a0 + i + 1)
                if use == "x":
                    nc.vector.tensor_copy(xnT[:], bank[:]).then_inc(s["aux_free"], 1)
                elif use == "v":
                    if not (isinstance(n, int) and n < 2):
                        v.wait_ge(s["av_done"], (n - 1) * UG + 2)
                    for j in range(GB):
                        vz = VZ[u][:, j, :]
                        diag = bass.AP(vz.tensor, vz.offset, [vz.ap[0], [NHG * HW, NHG], [HW + HD, NHG], [1, HD]])
                        ins = nc.vector.tensor_copy(diag, bank[:, j * 128:(j + 1) * 128]
                                                    .rearrange("p (g h d) -> p g h d", g=NHG, h=NHG))
                    steps.link(ins)
                    v.sem_inc(s["v_ready"], 1)
                    v.sem_inc(s["aux_free"], 1)
                elif rope:
                    k = use[0]
                    dst, table = (t2[k], "sin" + k) if use[1:] else (t1[k], "cos" + k)
                    nc.vector.scalar_tensor_tensor(
                        dst[:].rearrange("p (a s) -> p a s", a=GB), bank[:].rearrange("p (a s) -> p a s", a=GB),
                        bias["b" + use][:, 0:1], tab[table][:].unsqueeze(1).to_broadcast([128, GB, S]),
                        ALU.add, ALU.mult).then_inc(s["aux_free"], 1)
                else:
                    nc.vector.tensor_scalar(t1[use][:], bank[:], bias["b" + use][:, 0:1],
                                            HD ** -0.5 if use == "q" else 1.0, ALU.add, ALU.mult)\
                        .then_inc(s["aux_free"], 1)

            def maximum(k, w):
                v.wait_ge(s["sc_ready"], k + 1)
                nc.vector.tensor_reduce(negm[:, w % 2, :], sc[w % 2][:].rearrange("p (h k) -> p h k", h=NHG),
                                        AX.X, ALU.max, negate=True).then_inc(s["max_ready"], 1)

            def move(k, w):
                v.wait_ge(s["pt_ready"], k + 5)
                v.wait_ge(s["av_done"], k + 1)
                nc.vector.tensor_copy(PT[w % 2][:], pt[w % 2][:]).then_inc(s["pt_moved"], 1)

            def invert(n, u):
                v.wait_ge(s["exp_one"], ((n + 1) * UG + 2) * NHG)
                return steps.mark(nc.vector.reciprocal(sums[:, u, :], sums[:, u, :]))

            def spread_inverse(u, mark):
                steps.need(mark)
                nc.vector.tensor_copy(R[:].rearrange("p (h d) -> p h d", d=HD),
                                      sums[:, u, :].unsqueeze(2).to_broadcast([128, GB * H, HD]))\
                    .then_inc(s["R_ready"], 1)

            def take_inverse(a0):
                v.wait_ge(s["aux_full"], a0 + 1)
                nc.vector.tensor_copy(rT[:], aux[0][:]).then_inc(s["aux_free"], 1)

            def divide(n, u, a0):
                v.wait_ge(s["aux_free"], a0 + 3)
                v.wait_ge(s["av_done"], (n + 1) * UG + 2)
                nc.vector.tensor_tensor(OT[:], po[u][:], rT[:], ALU.mult).then_inc(s["OT_ready"], 1)

            def add_output(n, a0):
                v.wait_ge(s["aux_full"], a0 + 2)
                xg = xgroup(p, n)
                nc.vector.scalar_tensor_tensor(xg, aux[1][:].rearrange("p (a d) -> p a d", a=GB),
                                               p.gate[:, gate:gate + 1], xg, ALU.mult, ALU.add)\
                    .then_inc(s["aux_free"], 1)

            def add_constant(n, a0):
                v.wait_ge(s["aux_free"], a0 + 4)
                xg = xgroup(p, n)
                return steps.mark(nc.vector.tensor_tensor(xg, xg, gcb[:].unsqueeze(1).to_broadcast([128, GB, D]), ALU.add))

            v.wait_ge(s["aux_full"], 1)
            steps.link(nc.vector.tensor_tensor(gcb[:], aux[0][:, 0:128], bo[:], ALU.add))
            v.sem_inc(s["aux_free"], 1)
            steps.link(nc.vector.tensor_scalar(gcb[:], gcb[:], p.gate[:, gate:gate + 1], None, ALU.mult))
            v.wait_ge(s["aux_full"], 2)
            v.sem_inc(s["aux_free"], 1)
            def t1_ready(k, a0, mark):
                if rope:
                    return lambda: steps.need(mark)
                return lambda: v.wait_ge(s["aux_free"], a0 + uses.index(k) + 3)

            for i, use in enumerate(uses):
                if use == "v":
                    v.wait_ge(s["VZ_zeroed"], 2)
                take(use, i, 0, 0, 2)
                if use in (("qr", "kr") if rope else ("q", "k")):
                    k = use[0]
                    lower(k, upper(k, 0, t1_ready(k, 2, rotate(k, 0, 2) if rope else None)))

            def group(n, u, first, more):
                a0 = project_base(n, first)
                f0 = a0 + PRJ if more else a0
                rot, top = {}, {}
                for w in range(UG):
                    k = n * UG + w
                    if not (first and w < 3):
                        move(k - 3, (w - 3) % UG)
                    if more:
                        if w == 0:
                            normalise(n + 1, 1 - u)
                        for i, use in enumerate(uses):
                            if TAKE[use] == w:
                                take(use, i, n + 1, 1 - u, a0)
                        if rope and w == 6:
                            top["q"] = upper("q", n + 1, t1_ready("q", a0, rot["q"]))
                        if rope and w == 8:
                            top["k"] = upper("k", n + 1, t1_ready("k", a0, rot["k"]))
                        if not rope and w == 5:
                            lower("q", top["q"])
                        if not rope and w == 7:
                            lower("k", top["k"])
                    if not first:
                        if w == 3:
                            inverse = invert(n - 1, 1 - u)
                        if w == 10:
                            take_inverse(f0)
                        if w == 13:
                            add_output(n - 1, f0)
                        if w == 14:
                            steps.need(mark)
                            mark = tail.row_stats(v, n - 1, 1 - u, steps)
                        if w == 15:
                            steps.need(mark)
                            tail.hand_over(v, n - 1, 1 - u)
                    maximum(k, w)
                    if more:
                        if rope and w == 5:
                            rot["q"] = rotate("q", n + 1, a0)
                        if rope and w == 7:
                            rot["k"] = rotate("k", n + 1, a0)
                        if rope and w == 6:
                            lower("q", top["q"])
                        if rope and w == 8:
                            lower("k", top["k"])
                        if not rope and w == 4:
                            top["q"] = upper("q", n + 1, t1_ready("q", a0, None))
                        if not rope and w == 6:
                            top["k"] = upper("k", n + 1, t1_ready("k", a0, None))
                    if not first:
                        if w == 3:
                            spread_inverse(1 - u, inverse)
                        if w == 10:
                            divide(n - 1, 1 - u, f0)
                        if w == 13:
                            mark = add_constant(n - 1, f0)
                        if w == 14:
                            steps.need(mark)
                            mark = tail.combine(v, n - 1, 1 - u, steps)

            over_groups_skewed(v, group, steps, 2 * (len(uses) + 3))
            for w in range(3):
                move(NG * UG + w - 3, UG + w - 3)
            spread_inverse(1, invert(NG - 1, 1))
            take_inverse(LAST)
            divide(NG - 1, 1, LAST)
            add_output(NG - 1, LAST)
            steps.need(add_constant(NG - 1, LAST))
            tail.vector(v, NG - 1, 1, steps, None)

        @block.scalar
        def _(a):
            def group(n, u, more=True):
                for w in range(UG):
                    k = n * UG + w
                    j, hg = w // NHG, w % NHG
                    a.wait_ge(s["max_ready"], k + 1)
                    a.wait_ge(s["pt_ready"], k + 1)
                    for h in range(NHG):
                        col = j * H + hg * NHG + h
                        nc.scalar.activation(E[w % 4][:, h * 128:(h + 1) * 128], sc[w % 2][:, h * 128:(h + 1) * 128],
                                             ACT.Exp, bias=negm[:, w % 2, h:h + 1],
                                             accum_out=sums[:, u, col:col + 1]).then_inc(s["exp_one"], 1)

            over_groups(a, group)

        @block.tensor
        def _(t):
            credit(t, (s["av_done"], 2), (s["pt_ready"], 4), (s["exp_one"], 2 * NHG))
            t.wait_ge(s["w_in"], 16 * NW)
            t.wait_ge(s["const_ready"], 1)
            t.wait_ge(s["aux_free"], 1)
            nc.tensor.matmul(aux[0][:, 0:128], bvb[:], W["WoT"][:], start=True, stop=True).then_inc(s["aux_full"], 1)
            t.wait_ge(s["aux_free"], 2)
            nc.tensor.matmul(aux[1][:, 0:128], bvb[:], W["WoT"][:], start=True, stop=True).then_inc(s["aux_full"], 1)

            def put(use, i, n, u, a0):
                bank = aux[i % 2]
                if use == "x":
                    t.wait_ge(s["xn_ready"], n + 1)
                t.wait_ge(s["aux_free"], a0 + i + 1)
                if use == "x":
                    for j in range(GB):
                        ins = nc.tensor.transpose(bank[:, j * 128:(j + 1) * 128], xn[u][:, j, :], p.ident[:])
                elif use == "v":
                    for j in range(GB):
                        ins = nc.tensor.matmul(bank[:, j * 128:(j + 1) * 128], cT[u][:, j * 128:(j + 1) * 128],
                                               W["WvT"][:], start=True, stop=True)
                else:
                    if use == "q":
                        t.wait_ge(s["aux_free"], a0 + 3)
                    if use == "k":
                        t.wait_ge(s["c_in0"] if u == 0 else s["c_in1"], (n - u) * 8 + 16)
                    ins = nc.tensor.matmul(bank[:], W[f"W{use}T"][:], (xnT if use[0] == "q" else cT[u])[:],
                                           start=True, stop=True)
                ins.then_inc(s["aux_full"], 1)

            def turn_sums(n, a0):
                t.wait_ge(s["R_ready"], n + 1)
                t.wait_ge(s["aux_free"], a0 + 1)
                for j in range(GB):
                    ins = nc.tensor.transpose(aux[0][:, j * 128:(j + 1) * 128], R[:, j * 128:(j + 1) * 128], p.ident[:])
                ins.then_inc(s["aux_full"], 1)

            def output(n, a0):
                t.wait_ge(s["OT_ready"], n + 3)
                t.wait_ge(s["aux_free"], a0 + 2)
                for j in range(GB):
                    ins = nc.tensor.matmul(aux[1][:, j * 128:(j + 1) * 128], OT[:, j * 128:(j + 1) * 128], W["WoT"][:],
                                           start=True, stop=True)
                ins.then_inc(s["aux_full"], 1)

            def scores(k, w, u):
                j, hg = w // NHG, w % NHG
                t.wait_ge(s["exp_one"], (k + 1) * NHG)
                nc.tensor.matmul(sc[w % 2][:], QS[u][:, hg, j * 128:(j + 1) * 128],
                                 p.KS[u][:, hg, :, j * 128:(j + 1) * 128], start=True, stop=False)
                nc.tensor.matmul(sc[w % 2][:], p.ident16[:], mneg[:].unsqueeze(1).to_broadcast([128, NHG, 128]),
                                 start=False, stop=True).then_inc(s["sc_ready"], 1)

            def turn(k, w):
                t.wait_ge(s["exp_one"], (k + 3) * NHG)
                t.wait_ge(s["pt_moved"], k + 1)
                for c in range(NHG):
                    ins = nc.tensor.transpose(pt[w % 2][:, c * 128:(c + 1) * 128], E[w % 4][:, c * 128:(c + 1) * 128],
                                              p.ident[:])
                ins.then_inc(s["pt_ready"], 1)

            def attend(k, w, u):
                j, hg = w // NHG, w % NHG
                t.wait_ge(s["pt_moved"], k + 3)
                for c in range(NHG):
                    h = hg * NHG + c
                    ins = nc.tensor.matmul(po[u][hg * HW:(hg + 1) * HW, j * 128:(j + 1) * 128],
                                           VZ[u][:, j, h * HW:(h + 1) * HW],
                                           PT[w % 2][:, c * 128:(c + 1) * 128], start=(c == 0), stop=(c == NHG - 1))
                ins.then_inc(s["av_done"], 1)

            for i, use in enumerate(uses):
                put(use, i, 0, 0, 2)

            def group(n, u, first, more):
                a0 = project_base(n, first)
                f0 = a0 + PRJ if more else a0
                t.wait_ge(s_qin[u], qcount(n, u))
                t.wait_ge(s_kin[u], kcount(n, u))
                for w in range(UG):
                    k = n * UG + w
                    scores(k, w, u)
                    if not (first and w < 2):
                        turn(k - 2, (w - 2) % UG)
                    if w == 4:
                        t.wait_ge(s["v_ready"], n + 1)
                        t.wait_ge(s["OT_ready"], n + 1)
                    if w >= 4:
                        attend(k - 4, w - 4, u)
                    elif not first:
                        attend(k - 4, w - 4 + UG, 1 - u)
                    if more:
                        for i, use in enumerate(uses):
                            if PUT[use] == w:
                                put(use, i, n + 1, 1 - u, a0)
                    if not first and w == 8:
                        turn_sums(n - 1, f0)
                    if not first and w == 12:
                        output(n - 1, f0)

            over_groups_skewed(t, group)
            for w in range(UG, UG + 4):
                if w < UG + 2:
                    turn((NG - 1) * UG + w - 2, w - 2)
                attend((NG - 1) * UG + w - 4, w - 4, 1)
            turn_sums(NG - 1, LAST)
            output(NG - 1, LAST)


LOW, TAKEN = -3.0e38, -3.3e38


class Router:
    STEPS = 9

    def __init__(self, st, p, name, ne, over_chosen):
        self.st, self.p, self.name, self.ne, self.over_chosen = st, p, name, ne, over_chosen
        self.W = st.sb("rW", [128, ne])
        self.b = st.sb("rb", [128, ne])
        self.L = st.sb("rL", [128, GB, ne + 8])
        self.mr = st.sb("rmr", [128, GB, ne + 8])
        self.top, self.rv = st.sb("rtop", [128, GB, 8]), st.sb("rrv", [128, GB, 8])
        self.E, self.r = st.sb("rE", [128, GB, ne]), st.sb("rr", [128, GB])
        self.G = [st.sb(f"G{u}", [128, GB, ne]) for u in range(2)]
        self.GT = [st.sb(f"GT{u}", [128, 128]) for u in range(2)]
        self.ps = st.bank("route")
        s = lambda k: st.sem("route_" + k)
        self.in_, self.logits, self.diff, self.exp = s("in"), s("logits"), s("diff"), s("exp")
        self.waited, self.turn_waited = s("waited"), s("turn_waited")
        self.G_ready, self.GT_ps, self.GT_ready, self.G_used = s("G_ready"), s("GT_ps"), s("GT_ready"), s("G_used")

    def load(self, eng, d):
        eng.dma_start(self.W[:], d[self.name + "_rW"]).then_inc(self.in_, 16)
        eng.dma_start(self.b[:], d[self.name + "_rb"].to_broadcast([128, self.ne])).then_inc(self.in_, 16)

    def start(self, eng, steps):
        nc = self.st.nc
        nc.vector.memset(self.L[:], LOW)
        steps.link(nc.vector.memset(self.rv[:], LOW))
        eng.wait_ge(self.in_, 32)

    def tensor(self, eng, n, xT):
        nc = self.st.nc
        eng.wait_ge(self.GT_ready, n + 1)
        for j in range(GB):
            ins = nc.tensor.matmul(self.ps[:, j * self.ne:(j + 1) * self.ne], xT[:, j * 128:(j + 1) * 128], self.W[:],
                                   start=True, stop=True)
        ins.then_inc(self.logits, 1)

    def vector(self, eng, n, u, steps):
        self.choose(eng, n, steps)
        self.weigh(eng, n, u, steps)

    def choose(self, eng, n, steps):
        nc, ne = self.st.nc, self.ne
        L = self.L[:, :, 0:ne]
        eng.wait_ge(self.logits, n + 1)
        steps.link(nc.vector.tensor_tensor(L, self.ps[:, 0:GB * ne].rearrange("p (a e) -> p a e", a=GB),
                                           self.b[:].unsqueeze(1).to_broadcast([128, GB, ne]), ALU.add))
        stand(eng, self.waited)
        for j in range(GB):
            ins = nc.vector.max(self.top[:, j, :], self.L[:, j, 0:ne])
        steps.link(ins)
        nc.vector.tensor_tensor(self.E[:], L, self.top[:, :, 0:1].to_broadcast([128, GB, ne]), ALU.subtract)\
            .then_inc(self.diff, 1)
        steps.link(nc.vector.tensor_copy(self.rv[:, :, 0:TOPK], self.top[:, :, 0:TOPK]))
        stand(eng, self.waited)
        for j in range(GB):
            ins = nc.vector.match_replace(out=self.mr[:, j, :], in_to_replace=self.rv[:, j, :],
                                          in_values=self.L[:, j, :], imm_value=TAKEN)
        steps.link(ins)

    def weigh(self, eng, n, u, steps):
        nc, ne = self.st.nc, self.ne
        eng.wait_ge(self.exp, n + 1)
        if not self.over_chosen:
            steps.link(nc.vector.tensor_reduce(self.r[:], self.E[:], AX.X, ALU.add))
        steps.link(nc.vector.scalar_tensor_tensor(self.E[:], self.mr[:, :, 0:ne], TAKEN, self.E[:],
                                                  ALU.is_equal, ALU.mult))
        if self.over_chosen:
            steps.link(nc.vector.tensor_reduce(self.r[:], self.E[:], AX.X, ALU.add))
        steps.link(nc.vector.reciprocal(self.r[:], self.r[:]))
        nc.vector.tensor_tensor(self.G[u][:], self.E[:], self.r[:].unsqueeze(2).to_broadcast([128, GB, ne]), ALU.mult)\
            .then_inc(self.G_ready, 1)
        eng.wait_ge(self.G_ready, n + 1)

    VSTEPS = 7

    def scalar_exp(self, eng, n):
        eng.wait_ge(self.diff, n + 1)
        self.st.nc.scalar.activation(self.E[:], self.E[:], ACT.Exp).then_inc(self.exp, 1)

    def tensor_turn(self, eng, n, u):
        eng.wait_ge(self.G_ready, n + 1)
        stand(eng, self.turn_waited)
        self.st.nc.tensor.transpose(self.ps[0:GB * self.ne, 128:256], self.G[u][:].rearrange("p a e -> p (a e)"),
                                    self.p.ident[:]).then_inc(self.GT_ps, 1)

    def scalar_turn(self, eng, n, u):
        eng.wait_ge(self.GT_ps, n + 1)
        k = GB * self.ne
        self.st.nc.scalar.activation(self.GT[u][0:k, :], self.ps[0:k, 128:256], ACT.Copy).then_inc(self.GT_ready, 1)


def stage_l1_ffn(nc, p, d):
    NO = NR // 2
    with Stage(nc, "F1") as st:
        front, tail = Front(st, p), Tail(st, p)
        rt = Router(st, p, "L1F", NR, False)
        WrT = st.sb("WrT", [128, NR, 128])
        Ws = st.sb("Ws", [128, 2, 128])
        blk = st.sb("blk", [GB * NR + 1, GD])
        bs = st.sb("bs", [65, 2, 128])
        acc = [st.sb(f"acc{u}", [128, GB, D]) for u in range(2)]
        odd = [st.sb(f"odd{u}", [128, GD]) for u in range(2)]
        part = [st.sb(f"part{i}", [128, GD]) for i in range(4)]
        eb = [[st.bank(f"e{k}{i}") for i in range(2)] for k in ("even", "odd")]
        sh = st.bank("shared")
        s = {k: st.sem(k) for k in ("w_in", "blk_in", "zeroed", "v_step", "ws_ready", "e_ready", "even_used", "odd_used",
                                    "odd_added", "odd_taken")}
        block = st.block()

        @block.sync
        def _(sp):
            sp.dma_start(Ws[:], d["L1F_WsT"]).then_inc(s["w_in"], 16)
            sp.dma_start(bs[64:65, :, :], d["L1F_bs"]).then_inc(s["w_in"], 16)
            rt.load(sp, d)
            sp.dma_start(WrT[:], d["L1F_WrT"]).then_inc(s["w_in"], 16)
            sp.wait_ge(s["zeroed"], 1)
            for j in range(GB):
                sp.dma_start(blk[j * NR:(j + 1) * NR, j * D:(j + 1) * D], d["L1F_br"]).then_inc(s["blk_in"], 16)

        @block.gpsimd
        def _(g):
            nc.gpsimd.memset(blk[:], 0.0).then_inc(s["zeroed"], 1)
            credit(g, (tail.rstd_done, 2))
            credit(g, (s["odd_added"], 4))

            def group(n, u, first, more):
                g.wait_ge(s["odd_taken"], n + 1)
                for m in range(1, NO):
                    g.wait_ge(s["odd_used"], n * NO + m + 3)
                    g.wait_ge(s["odd_added"], n * (NO - 1) + m - 1 + 4)
                    nc.gpsimd.tensor_tensor(odd[u][:], part[0][:] if m == 1 else odd[u][:], part[m % 4][:], ALU.add)\
                        .then_inc(s["odd_added"], 1)
                    if m == 4 and not first:
                        tail.gpsimd(g, n - 1, 1 - u)

            over_groups_skewed(g, group)
            tail.gpsimd(g, NG - 1, 1)

        @block.vector
        def _(v):
            steps = Steps(v, s["v_step"])
            credit(v, (tail.var_ready, 1), (s["even_used"], 3), (s["odd_taken"], 2))
            rt.start(v, steps)
            front.vector(v, 0, 0)
            nc.vector.memset(rt.GT[0][64:65, :], 1.0)
            nc.vector.memset(rt.GT[1][64:65, :], 1.0)
            v.wait_ge(s["w_in"], 48)
            v.wait_ge(s["zeroed"], 1)
            steps.link(nc.vector.tensor_tensor(Ws[:, 0, :], Ws[:, 0, :], Ws[:, 1, :], ALU.add))
            steps.link(nc.vector.tensor_scalar(Ws[:, 0, :], Ws[:, 0, :], 0.5, None, ALU.mult))
            steps.link(nc.vector.tensor_tensor(bs[64:65, 0, :], bs[64:65, 0, :], bs[64:65, 1, :], ALU.add))
            steps.link(nc.vector.tensor_scalar(blk[64:65, :].rearrange("p (a o) -> p a o", a=GB),
                                               bs[64:65, 0:1, :].to_broadcast([1, GB, D]), 0.5, None, ALU.mult))
            v.sem_inc(s["ws_ready"], 1)
            rt.vector(v, 0, 0, steps)

            def finish(n, u):
                xg = xgroup(p, n)
                v.wait_ge(s["odd_added"], (n + 1) * (NO - 1) + 4)
                nc.vector.tensor_tensor(acc[u][:], acc[u][:], odd[u][:].rearrange("p (a o) -> p a o", a=GB), ALU.add)\
                    .then_inc(s["odd_taken"], 1)
                v.wait_ge(s["odd_taken"], n + 3)
                tail.vector(v, n, u, steps, nc.vector.scalar_tensor_tensor(xg, acc[u][:], p.gate[:, 5:6], xg,
                                                                           ALU.mult, ALU.add))

            def group(n, u, first, more):
                k = n * (NR + 1)
                v.wait_ge(s["e_ready"], k + 1)
                nc.vector.tensor_tensor(acc[u][:], sh[:].rearrange("p (a o) -> p a o", a=GB), front.xn[u][:], ALU.add)\
                    .then_inc(s["even_used"], 1)
                for i in range(NO):
                    v.wait_ge(s["e_ready"], k + 2 * i + 2)
                    v.wait_ge(s["even_used"], n * (NO + 1) + i + 4)
                    for j in range(GB):
                        ins = nc.vector.scalar_tensor_tensor(acc[u][:, j, :], eb[0][i % 2][:, j * 128:(j + 1) * 128],
                                                             rt.G[u][:, j, 2 * i:2 * i + 1], acc[u][:, j, :],
                                                             ALU.mult, ALU.add)
                    ins.then_inc(s["even_used"], 1)
                    if i == 0 and more:
                        front.vector(v, n + 1, 1 - u)
                    if i == 2 and not first:
                        finish(n - 1, 1 - u)
                    if i == 4 and more:
                        rt.vector(v, n + 1, 1 - u, steps)

            over_groups_skewed(v, group, steps, 2 * (rt.VSTEPS + tail.STEPS))
            v.wait_ge(s["even_used"], NG * (NO + 1) + 3)
            finish(NG - 1, 1)

        @block.scalar
        def _(a):
            credit(a, (front.xnT_ready, 1), (rt.GT_ready, 1))
            front.scalar(a, 0, 0)
            rt.scalar_exp(a, 0)
            rt.scalar_turn(a, 0, 0)

            def group(n, u, more):
                a.wait_ge(rt.G_ready, n + 1)
                for m in range(NO):
                    a.wait_ge(s["e_ready"], n * (NR + 1) + 2 * m + 3)
                    a.wait_ge(s["odd_added"], n * (NO - 1) + (m + 1 if m < 4 else max(m - 4, 1) + 4))
                    for j in range(GB):
                        ins = nc.scalar.activation(part[m % 4][:, j * D:(j + 1) * D], eb[1][m % 2][:, j * D:(j + 1) * D],
                                                   ACT.Copy, scale=rt.G[u][:, j, 2 * m + 1:2 * m + 2])
                    ins.then_inc(s["odd_used"], 1)
                    if m == 2 and more:
                        front.scalar(a, n + 1, 1 - u)
                    if m == 4 and more:
                        rt.scalar_exp(a, n + 1)
                    if m == 6 and more:
                        rt.scalar_turn(a, n + 1, 1 - u)

            over_groups(a, group)

        @block.tensor
        def _(t):
            credit(t, (front.xn_used, 2), (front.xnT_used, 2), (s["odd_used"], 2))
            front.tensor(t, 0, 0)
            t.wait_ge(s["w_in"], 48)
            t.wait_ge(s["blk_in"], 64)
            t.wait_ge(s["ws_ready"], 1)
            t.wait_ge(front.xnT_ready, 2)
            rt.tensor(t, 0, front.xnT[0])
            rt.tensor_turn(t, 0, 0)

            def group(n, u, more):
                k = n * (NR + 1)
                t.wait_ge(rt.GT_ready, n + 2)
                t.wait_ge(s["even_used"], n * (NO + 1) + 1)
                for j in range(GB):
                    nc.tensor.matmul(sh[:, j * 128:(j + 1) * 128], front.xnT[u][:, j * 128:(j + 1) * 128], Ws[:, 0, :],
                                     start=(j == 0), stop=False, skip_group_check=True)
                nc.tensor.matmul(sh[:], rt.GT[u][0:65, :], blk[:], start=False, stop=True, skip_group_check=True)\
                    .then_inc(s["e_ready"], 1)
                for e in range(NR):
                    i = e // 2
                    if e % 2:
                        t.wait_ge(s["odd_used"], n * NO + i + 1)
                    else:
                        t.wait_ge(s["even_used"], n * (NO + 1) + i + 3)
                    for j in range(GB):
                        ins = nc.tensor.matmul(eb[e % 2][i % 2][:, j * 128:(j + 1) * 128],
                                               front.xnT[u][:, j * 128:(j + 1) * 128], WrT[:, e, :], start=True, stop=True)
                    ins.then_inc(s["e_ready"], 1)
                    if e == 4 and more:
                        front.tensor(t, n + 1, 1 - u)
                    if e == 8 and more:
                        t.wait_ge(front.xnT_ready, n + 3)
                        rt.tensor(t, n + 1, front.xnT[1 - u])
                    if e == 13 and more:
                        rt.tensor_turn(t, n + 1, 1 - u)
                t.wait_ge(s["e_ready"], k + NR + 1)
                t.sem_inc(front.xnT_used, 1)
                t.sem_inc(front.xn_used, 1)

            over_groups(t, group)


def stage_l2_attn(nc, p, d):
    SCALE = float(np.sqrt(D // 16))
    with Stage(nc, "A2") as st:
        tail = Tail(st, p)
        cT, cN = st.sb("cT", [128, B, S]), st.sb("cN", [128, B, D])
        negm, sums = st.sb("negm", [128, 2, GB]), st.sb("sums", [128, 4, GB])
        xn, xnT, E, PT = ([st.sb(f"{k}{u}", [128, GD]) for u in range(2)] for k in ("xn", "xnT", "E", "PT"))
        front = st.bank("front")
        sc, pt, po = ([st.bank(f"{k}{u}") for u in range(2)] for k in ("sc", "pt", "po"))
        s = {k: st.sem(k) for k in ("cT_in0", "cT_in1", "cN_in0", "cN_in1", "v_step", "xn_ready", "xnT_ps", "xnT_ready",
                                    "sc_ready", "max_ready", "exp_done", "pt_ready", "pt_moved", "po_ready", "x_new")}
        block = st.block()
        FIRST = 2 * GB

        @block.sync
        def _(sp):
            sp.dma_start(cT[:, 0:FIRST, :], d["ctxT"][:, 0:FIRST, :]).then_inc(s["cT_in0"], 16)
            sp.dma_start(cN[:, 0:FIRST, :], d["ctx"][:, 0:FIRST, :]).then_inc(s["cN_in0"], 16)
            sp.dma_start(cT[:, FIRST:, :], d["ctxT"][:, FIRST:, :]).then_inc(s["cT_in1"], 16)
            sp.dma_start(cN[:, FIRST:, :], d["ctx"][:, FIRST:, :]).then_inc(s["cN_in1"], 16)

        @block.gpsimd
        def _(g):
            credit(g, (tail.rstd_done, 2))
            for n in range(NG):
                tail.gpsimd(g, n, n % 2)

        @block.vector
        def _(v):
            steps = Steps(v, s["v_step"])
            credit(v, (tail.var_ready, 1))

            def normalise(n):
                if n >= 2:
                    v.wait_ge(s["xnT_ps"], n - 1)
                for j in range(GB):
                    b = n * GB + j
                    ins = nc.vector.tensor_scalar(xn[n % 2][:, j * D:(j + 1) * D], p.X[:, b, :], p.mean[:, b:b + 1],
                                                  p.rstd[:, b:b + 1], ALU.subtract, ALU.mult)
                ins.then_inc(s["xn_ready"], 1)

            normalise(0)
            for t in range(NG + 4):
                scored, turned, attended, renewed = (0 <= t - i < NG for i in (1, 2, 3, 4))
                u1, u3, n4 = (t - 1) % 2, (t - 3) % 4, t - 4
                if scored:
                    v.wait_ge(s["sc_ready"], t)
                    top = steps.mark(nc.vector.tensor_reduce(negm[:, u1, :], sc[u1][:].rearrange("p (a k) -> p a k", a=GB),
                                                             AX.X, ALU.max, negate=True))
                if turned:
                    v.wait_ge(s["pt_ready"], t - 1)
                    if t >= 4:
                        v.wait_ge(s["po_ready"], t - 3)
                    nc.vector.tensor_copy(PT[t % 2][:], pt[t % 2][:]).then_inc(s["pt_moved"], 1)
                if scored:
                    steps.need(top)
                    nc.vector.tensor_scalar(negm[:, u1, :], negm[:, u1, :], SCALE, None, ALU.mult).then_inc(s["max_ready"], 1)
                if attended:
                    v.wait_ge(s["exp_done"], (t - 2) * GB)
                    inverse = steps.mark(nc.vector.reciprocal(sums[:, u3, :], sums[:, u3, :]))
                if renewed:
                    v.wait_ge(s["x_new"], n4 + 1)
                    stats = tail.row_stats(v, n4, n4 % 2, steps)
                if attended:
                    steps.need(inverse)
                    factor = steps.mark(nc.vector.tensor_scalar(sums[:, u3, :], sums[:, u3, :], p.gate[:, 2:3], None, ALU.mult))
                if renewed:
                    steps.need(stats)
                    stats = tail.combine(v, n4, n4 % 2, steps)
                if t + 1 < NG:
                    normalise(t + 1)
                if attended:
                    steps.need(factor)
                    v.wait_ge(s["po_ready"], t - 2)
                    for j in range(GB):
                        xj = p.X[:, (t - 3) * GB + j, :]
                        ins = nc.vector.scalar_tensor_tensor(xj, po[(t - 3) % 2][:, j * 128:(j + 1) * 128],
                                                             sums[:, u3, j:j + 1], xj, ALU.mult, ALU.add)
                    ins.then_inc(s["x_new"], 1)
                if renewed:
                    steps.need(stats)
                    tail.hand_over(v, n4, n4 % 2)

        @block.scalar
        def _(a):
            for t in range(NG + 1):
                if t < NG:
                    a.wait_ge(s["xnT_ps"], t + 1)
                    if t >= 2:
                        a.wait_ge(s["sc_ready"], t - 1)
                    nc.scalar.activation(xnT[t % 2][:], front[:], ACT.Copy).then_inc(s["xnT_ready"], 1)
                if t >= 1:
                    n = t - 1
                    a.wait_ge(s["max_ready"], n + 1)
                    if n >= 2:
                        a.wait_ge(s["pt_ready"], n - 1)
                    for j in range(GB):
                        nc.scalar.activation(E[n % 2][:, j * 128:(j + 1) * 128], sc[n % 2][:, j * 128:(j + 1) * 128], ACT.Exp,
                                             bias=negm[:, n % 2, j:j + 1], scale=SCALE,
                                             accum_out=sums[:, n % 4, j:j + 1]).then_inc(s["exp_done"], 1)

        @block.tensor
        def _(t_):
            for t in range(NG + 3):
                n0, n1, n2, n3 = t, t - 1, t - 2, t - 3
                if n0 < NG:
                    t_.wait_ge(s["xn_ready"], n0 + 1)
                    if n0:
                        t_.wait_ge(s["xnT_ready"], n0)
                    for j in range(GB):
                        ins = nc.tensor.transpose(front[:, j * 128:(j + 1) * 128], xn[n0 % 2][:, j * 128:(j + 1) * 128],
                                                  p.ident[:])
                    ins.then_inc(s["xnT_ps"], 1)
                if 0 <= n2 < NG:
                    t_.wait_ge(s["exp_done"], (n2 + 1) * GB)
                    if n2 >= 2:
                        t_.wait_ge(s["pt_moved"], n2 - 1)
                    for j in range(GB):
                        ins = nc.tensor.transpose(pt[n2 % 2][:, j * 128:(j + 1) * 128], E[n2 % 2][:, j * 128:(j + 1) * 128],
                                                  p.ident[:])
                    ins.then_inc(s["pt_ready"], 1)
                if 0 <= n1 < NG:
                    t_.wait_ge(s["xnT_ready"], n1 + 1)
                    t_.wait_ge(s["cT_in0"] if n1 * GB < FIRST else s["cT_in1"], 16)
                    if n1 >= 2:
                        t_.wait_ge(s["exp_done"], (n1 - 1) * GB)
                    for j in range(GB):
                        ins = nc.tensor.matmul(sc[n1 % 2][:, j * 128:(j + 1) * 128], xnT[n1 % 2][:, j * 128:(j + 1) * 128],
                                               cT[:, n1 * GB + j, :], start=True, stop=True)
                    ins.then_inc(s["sc_ready"], 1)
                if 0 <= n3 < NG:
                    t_.wait_ge(s["cN_in0"] if n3 * GB < FIRST else s["cN_in1"], 16)
                    t_.wait_ge(s["pt_moved"], n3 + 1)
                    if n3 >= 2:
                        t_.wait_ge(s["x_new"], n3 - 1)
                    for j in range(GB):
                        ins = nc.tensor.matmul(po[n3 % 2][:, j * 128:(j + 1) * 128], PT[n3 % 2][:, j * 128:(j + 1) * 128],
                                               cN[:, n3 * GB + j, :], start=True, stop=True)
                    ins.then_inc(s["po_ready"], 1)


def stage_l2_ffn(nc, p, d, gate):
    NP2 = B // 2
    SL = NX * CAP
    HB = B // 2
    RW = B * NX // 128
    NQ2 = 2 * NX
    PUT = NX + 1
    HP = NP2 // 2
    with Stage(nc, "F2") as st:
        tail = Tail(st, p)
        xn = st.sb("xn", [128, B, D])
        rot = [st.sb(f"rot{i}", [128, GD]) for i in range(2)]
        xg = st.sb("xg", [128, B, SL])
        w1, w2 = st.sb("w1", [128, NX, FF]), st.sb("w2", [128, NX, FC, 128])
        hT = [st.sb(f"hT{i}", [128, GD]) for i in range(2 * FC)]
        match = [st.sb(f"match{i}", [128, 2 * SL]) for i in range(2)]
        WT = [st.sb(f"WT{i}", [128, 2 * SL]) for i in range(2)]
        iota, upper = st.sb("iota", [128, 2 * SL]), st.sb("upper", [128, 128])
        W = st.sb("W", [128, NX])
        L, m = st.sb("L", [128, B, NX]), st.sb("m", [128, B])
        G, chosen, slot = st.sb("G", [128, B * NX]), st.sb("chosen", [128, B * NX]), st.sb("slot", [128, B * NX])
        work = [st.sb(f"work{i}", [128, S]) for i in range(RW)]
        PT = [st.sb(f"PT{i}", [128, S]) for i in range(RW)]
        MT = [st.sb(f"MT{i}", [128, S]) for i in range(RW)]
        top = st.sb("top", [128, RW, 8])
        gb = [st.bank(f"g{i}") for i in range(2)]
        hb = [st.bank(f"h{i}") for i in range(2)]
        yb = [st.bank(f"y{i}") for i in range(2)]
        ob = [st.bank(f"o{i}") for i in range(2)]
        s = {k: st.sem(k) for k in (
            "w_in", "c_in", "v_step", "xn_ready", "xnT_ps", "xnT_ready", "logits", "diff", "exp", "probs", "probs_T",
            "rows", "mask_T", "chosen_ready", "ranked", "G_ready", "match_ready", "gathered", "xg_ready",
            "h_ps", "h_ready", "y_ready", "y_moved", "weighted", "match_turned", "y_turned", "WT_ready", "yT_ready",
            "put_ready", "x_new")}
        block = st.block()

        @block.sync
        def _(sp):
            for dst, src in ((W[:], d["L2_gate_w"]), (upper[:], d["upper"]), (iota[:], d["iota"].to_broadcast([128, 2 * SL]))):
                sp.dma_start(dst, src).then_inc(s["c_in"], 16)
            sp.dma_start(w1[:], d["F2_w1"]).then_inc(s["w_in"], 16)
            sp.dma_start(w2[:], d["F2_w2"]).then_inc(s["w_in"], 16)

        @block.gpsimd
        def _(g):
            credit(g, (tail.rstd_done, 2))
            g.wait_ge(s["G_ready"], 1)
            for i in range(NP2):
                g.wait_ge(s["match_ready"], NP2 + i + 1)
                mi = match[i % 2][:].rearrange("p (a c) -> p a c", c=CAP)
                nc.gpsimd.tensor_tensor(mi, mi, G[:, i * 2 * NX:(i + 1) * 2 * NX].unsqueeze(2)
                                        .to_broadcast([128, 2 * NX, CAP]), ALU.mult).then_inc(s["weighted"], 1)
                if i >= 2 and i % 2 == 0:
                    tail.gpsimd(g, i // 2 - 1, (i // 2 - 1) % 2)
            tail.gpsimd(g, NG - 1, (NG - 1) % 2)

        @block.vector
        def _(v):
            steps = Steps(v, s["v_step"])
            credit(v, (tail.var_ready, 1))
            for n in range(NG):
                for b in range(n * GB, (n + 1) * GB):
                    ins = nc.vector.tensor_scalar(xn[:, b, :], p.X[:, b, :], p.mean[:, b:b + 1], p.rstd[:, b:b + 1],
                                                  ALU.subtract, ALU.mult)
                ins.then_inc(s["xn_ready"], 1)
            lg = ob[0][:, 0:B * NX].rearrange("p (b e) -> p b e", e=NX)
            v.wait_ge(s["logits"], NG)
            steps.link(nc.vector.tensor_reduce(m[:], lg, AX.X, ALU.max))
            nc.vector.tensor_tensor(L[:], lg, m[:].unsqueeze(2).to_broadcast([128, B, NX]), ALU.subtract)\
                .then_inc(s["diff"], 1)
            v.wait_ge(s["exp"], 1)
            steps.link(nc.vector.tensor_reduce(m[:], L[:], AX.X, ALU.add))
            steps.link(nc.vector.reciprocal(m[:], m[:]))
            nc.vector.tensor_tensor(L[:], L[:], m[:].unsqueeze(2).to_broadcast([128, B, NX]), ALU.mult)\
                .then_inc(s["probs"], 1)
            v.wait_ge(s["probs_T"], 1)
            for i in range(RW):
                ins = nc.vector.tensor_copy(work[i][:], yb[0][:, i * 128:(i + 1) * 128])
            steps.link(ins)
            for r in range(CAP // 8):
                for i in range(RW):
                    ins = nc.vector.max(top[:, i, :], work[i][:])
                steps.link(ins)
                for i in range(RW):
                    ins = nc.vector.match_replace(out=work[i][:], in_to_replace=top[:, i, :], in_values=work[i][:],
                                                  imm_value=-1.0)
                steps.link(ins)
            for i in range(RW):
                nc.vector.tensor_scalar(MT[i][:], work[i][:], -1.0, None, ALU.is_equal)
                ins = nc.vector.scalar_tensor_tensor(PT[i][:], work[i][:], -1.0, yb[0][:, i * 128:(i + 1) * 128],
                                                     ALU.is_equal, ALU.mult)
            ins.then_inc(s["rows"], 1)
            v.wait_ge(s["mask_T"], 1)
            nc.vector.tensor_copy(chosen[:], yb[1][:, 0:B * NX]).then_inc(s["chosen_ready"], 1)
            nc.vector.tensor_copy(G[:], yb[1][:, B * NX:2 * B * NX]).then_inc(s["G_ready"], 1)
            v.wait_ge(s["ranked"], 1)
            v.wait_ge(s["chosen_ready"], 1)
            steps.link(nc.vector.tensor_tensor(slot[:], ob[1][:, 0:B * NX], chosen[:], ALU.mult))
            v.wait_ge(s["c_in"], 48)

            def find(k):
                i = k % NP2
                if k >= NP2 + 2:
                    v.wait_ge(s["match_turned"], k - NP2 - 1)
                elif k >= 2:
                    v.wait_ge(s["gathered"], k - 1)
                nc.vector.tensor_tensor(match[k % 2][:].rearrange("p (a c) -> p a c", c=CAP),
                                        iota[:].rearrange("p (a c) -> p a c", c=CAP),
                                        slot[:, i * 2 * NX:(i + 1) * 2 * NX].unsqueeze(2)
                                        .to_broadcast([128, 2 * NX, CAP]), ALU.is_equal).then_inc(s["match_ready"], 1)

            def move_y(q):
                h, e = q // NX, q % NX
                v.wait_ge(s["y_ready"], q + 1)
                nc.vector.tensor_copy(xg[:, h * HB:(h + 1) * HB, e * CAP:(e + 1) * CAP],
                                      yb[q % 2][:].rearrange("p (b c) -> p b c", c=CAP)).then_inc(s["y_moved"], 1)

            def update(i):
                v.wait_ge(s["put_ready"], i + 1)
                xi = p.X[:, 2 * i:2 * i + 2, :]
                ins = nc.vector.scalar_tensor_tensor(xi, ob[i % 2][:, 0:2 * D].rearrange("p (a d) -> p a d", a=2),
                                                     p.gate[:, gate:gate + 1], xi, ALU.mult, ALU.add)
                ins.then_inc(s["x_new"], 1)
                if i % 2 == 1:
                    v.wait_ge(s["x_new"], i + 1)
                    tail.vector(v, i // 2, (i // 2) % 2, steps, None)

            for k in range(HP):
                find(k)
            for q in range(NQ2 + NP2):
                if q < HP:
                    find(HP + q)
                i = q - PUT
                if 0 <= i < NP2:
                    find(NP2 + i)
                if 1 <= q <= NQ2:
                    move_y(q - 1)
                if 1 <= i <= NP2:
                    update(i - 1)

        @block.scalar
        def _(a):
            for n in range(NG):
                a.wait_ge(s["xnT_ps"], n + 1)
                if n >= 2:
                    a.wait_ge(s["logits"], n - 1)
                nc.scalar.activation(rot[n % 2][:], hb[n % 2][:], ACT.Copy).then_inc(s["xnT_ready"], 1)
            a.wait_ge(s["diff"], 1)
            nc.scalar.activation(L[:], L[:], ACT.Exp).then_inc(s["exp"], 1)

            def take(i):
                a.wait_ge(s["gathered"], i + 1)
                nc.scalar.activation(xg[:, 2 * i:2 * i + 2, :], gb[i % 2][:].rearrange("p (a c) -> p a c", a=2), ACT.Copy)\
                    .then_inc(s["xg_ready"], 1)

            def take_turned(i):
                a.wait_ge(s["match_turned"], i + 1)
                if i >= 2:
                    a.wait_ge(s["put_ready"], i - 1)
                nc.scalar.activation(WT[i % 2][:], gb[0][:], ACT.Copy).then_inc(s["WT_ready"], 1)
                a.wait_ge(s["y_turned"], i + 1)
                nc.scalar.activation(rot[i % 2][:], gb[1][:], ACT.Copy).then_inc(s["yT_ready"], 1)

            for i in range(HP):
                take(i)
            for q in range(NQ2 + NP2):
                if q < NQ2:
                    for c in range(FC):
                        a.wait_ge(s["h_ps"], q * FC + c + 1)
                        if c == 0 and q >= 2:
                            a.wait_ge(s["y_ready"], q - 1)
                        nc.scalar.activation(hT[(q % 2) * FC + c][:], hb[c % 2][:], ACT.Gelu).then_inc(s["h_ready"], 1)
                if q < HP:
                    take(HP + q)
                if 0 <= q - PUT < NP2:
                    take_turned(q - PUT)

        @block.tensor
        def _(t):
            t.wait_ge(s["c_in"], 48)
            for n in range(NG + 1):
                if n < NG:
                    t.wait_ge(s["xn_ready"], n + 1)
                    if n >= 2:
                        t.wait_ge(s["xnT_ready"], n - 1)
                    for j in range(GB):
                        ins = nc.tensor.transpose(hb[n % 2][:, j * 128:(j + 1) * 128], xn[:, n * GB + j, :], p.ident[:])
                    ins.then_inc(s["xnT_ps"], 1)
                if n >= 1:
                    t.wait_ge(s["xnT_ready"], n)
                    for j in range(GB):
                        b = (n - 1) * GB + j
                        ins = nc.tensor.matmul(ob[0][:, b * NX:(b + 1) * NX], rot[(n - 1) % 2][:, j * 128:(j + 1) * 128],
                                               W[:], start=True, stop=True)
                    ins.then_inc(s["logits"], 1)
            t.wait_ge(s["probs"], 1)
            for i in range(RW):
                ins = nc.tensor.transpose(yb[0][:, i * 128:(i + 1) * 128],
                                          L[:, i * 16:(i + 1) * 16, :].rearrange("p b e -> p (b e)"), p.ident[:])
            ins.then_inc(s["probs_T"], 1)
            t.wait_ge(s["rows"], 1)
            for k, rows in enumerate((MT, PT)):
                for i in range(RW):
                    ins = nc.tensor.transpose(yb[1][:, (k * RW + i) * 128:(k * RW + i + 1) * 128], rows[i][:], p.ident[:])
            ins.then_inc(s["mask_T"], 1)
            t.wait_ge(s["chosen_ready"], 1)
            nc.tensor.matmul(ob[1][:, 0:B * NX], upper[:], chosen[:], start=True, stop=True).then_inc(s["ranked"], 1)

            def gather(i):
                t.wait_ge(s["match_ready"], i + 1)
                if i >= 2:
                    t.wait_ge(s["xg_ready"], i - 1)
                for j in range(2):
                    ins = nc.tensor.matmul(gb[i % 2][:, j * SL:(j + 1) * SL], xn[:, 2 * i + j, :],
                                           match[i % 2][:, j * SL:(j + 1) * SL], start=True, stop=True)
                ins.then_inc(s["gathered"], 1)

            def first(q, c):
                h, e = q // NX, q % NX
                if c == 0:
                    t.wait_ge(s["xg_ready"], HP * (h + 1))
                if q * FC + c >= 2:
                    t.wait_ge(s["h_ready"], q * FC + c - 1)
                nc.tensor.matmul(hb[c % 2][:], w1[:, e, c * 128:(c + 1) * 128],
                                 xg[:, h * HB:(h + 1) * HB, e * CAP:(e + 1) * CAP], start=True, stop=True)\
                    .then_inc(s["h_ps"], 1)

            def second(q, c):
                if c == 0 and q >= 2:
                    t.wait_ge(s["y_moved"], q - 1)
                t.wait_ge(s["h_ready"], q * FC + c + 1)
                ins = nc.tensor.matmul(yb[q % 2][:], w2[:, q % NX, c, :], hT[(q % 2) * FC + c][:],
                                       start=(c == 0), stop=(c == FC - 1))
                if c == FC - 1:
                    ins.then_inc(s["y_ready"], 1)

            def turn(i):
                t.wait_ge(s["weighted"], i + 1)
                if i:
                    t.wait_ge(s["WT_ready"], i)
                else:
                    t.wait_ge(s["xg_ready"], NP2)
                for c in range(4):
                    ins = nc.tensor.transpose(gb[0][:, c * 128:(c + 1) * 128], match[i % 2][:, c * 128:(c + 1) * 128],
                                              p.ident[:])
                ins.then_inc(s["match_turned"], 1)
                t.wait_ge(s["y_moved"], NX if i < HP else NQ2)
                if i:
                    t.wait_ge(s["yT_ready"], i)
                for c in range(4):
                    ins = nc.tensor.transpose(gb[1][:, c * 128:(c + 1) * 128],
                                              xg[:, 2 * i + c // 2, (c % 2) * 128:(c % 2 + 1) * 128], p.ident[:])
                ins.then_inc(s["y_turned"], 1)

            def put_back(i):
                t.wait_ge(s["yT_ready"], i + 1)
                if i >= 2:
                    t.wait_ge(s["x_new"], i - 1)
                for j in range(2):
                    for c in range(2):
                        cols = slice((2 * j + c) * 128, (2 * j + c + 1) * 128)
                        ins = nc.tensor.matmul(ob[i % 2][:, j * D:(j + 1) * D], WT[i % 2][:, cols], rot[i % 2][:, cols],
                                               start=(c == 0), stop=(c == 1))
                ins.then_inc(s["put_ready"], 1)

            for i in range(HP):
                gather(i)
            t.wait_ge(s["w_in"], 32)
            for q in range(NQ2 + NP2):
                for c in range(FC):
                    if q < NQ2:
                        first(q, c)
                    if 1 <= q <= NQ2:
                        second(q - 1, c)
                if q < HP:
                    gather(HP + q)
                if 1 <= q - PUT <= NP2:
                    put_back(q - PUT - 1)
                if 0 <= q - PUT < NP2:
                    turn(q - PUT)


def stage_l3_ffn(nc, p, d, name, gate):
    with Stage(nc, name) as st:
        front, tail = Front(st, p), Tail(st, p)
        rt = Router(st, p, name, NX, True)
        w1 = st.sb("w1", [128, NX, FF])
        w1hi, w1lo = (st.sb(f"w1{k}", [128, NX, FF], F32R) for k in ("hi", "lo"))
        w2 = st.sb("w2", [128, NX, FC, 128])
        xhi, xlo = ([st.sb(f"x{k}{u}", [128, GD], F32R) for u in range(2)] for k in ("hi", "lo"))
        b1 = st.sb("b1", [128, NX, FC])
        blk = st.sb("blk", [GB * NX, GD])
        hT = [st.sb(f"hT{i}", [128, GD]) for i in range(2 * FC)]
        acc = st.sb("acc", [128, GB, D])
        hb = [st.bank(f"h{i}") for i in range(2)]
        yb = [st.bank(f"y{i}") for i in range(2)]
        ib = st.bank("init")
        s = {k: st.sem(k) for k in ("w_in", "blk_in", "zeroed", "v_step", "h_ps", "h_ready", "y_ready", "y_used",
                                    "init_ready", "init_used", "w1_in0", "w1_in1", "w2_in1", "w1_split", "x_split")}
        NH = NX * FC
        block = st.block()

        @block.sync
        def _(sp):
            rt.load(sp, d)
            w1d = d[name + "_w1"]
            sp.dma_start(w1[:, 0:2, :], w1d[:, 0:2, :]).then_inc(s["w1_in0"], 16)
            sp.dma_start(b1[:], d[name + "_b1"]).then_inc(s["w_in"], 16)
            sp.wait_ge(s["zeroed"], 1)
            for j in range(GB):
                sp.dma_start(blk[j * NX:(j + 1) * NX, j * D:(j + 1) * D], d[name + "_b2"]).then_inc(s["blk_in"], 16)
            sp.dma_start(w2[:, 0:2], d[name + "_w2"][:, 0:2]).then_inc(s["w_in"], 16)
            sp.dma_start(w1[:, 2:, :], w1d[:, 2:, :]).then_inc(s["w1_in1"], 16)
            sp.dma_start(w2[:, 2:], d[name + "_w2"][:, 2:]).then_inc(s["w2_in1"], 16)

        @block.gpsimd
        def _(g):
            nc.gpsimd.memset(blk[:], 0.0).then_inc(s["zeroed"], 1)
            credit(g, (tail.rstd_done, 2))
            over_groups(g, lambda n, u, more: tail.gpsimd(g, n, u))

        @block.vector
        def _(v):
            steps = Steps(v, s["v_step"])
            credit(v, (tail.var_ready, 1), (s["y_used"], 2), (s["init_used"], 1))
            front.vector(v, 0, 0)

            def split_w1(e):
                steps.link(nc.vector.tensor_copy(w1hi[:, e, :], w1[:, e, :]))
                nc.vector.tensor_tensor(w1lo[:, e, :], w1[:, e, :], w1hi[:, e, :].bitcast(F32),
                                        ALU.subtract).then_inc(s["w1_split"], 1)

            def split_x(n, u):
                v.wait_ge(front.xnT_ready, n + 2)
                steps.link(nc.vector.tensor_copy(xhi[u][:], front.xnT[u][:]))
                nc.vector.tensor_tensor(xlo[u][:], front.xnT[u][:], xhi[u][:].bitcast(F32), ALU.subtract)\
                    .then_inc(s["x_split"], 1)

            rt.start(v, steps)
            split_x(0, 0)
            rt.vector(v, 0, 0, steps)
            for e in range(NX):
                v.wait_ge(s["w1_in0"] if e < 2 else s["w1_in1"], 16)
                split_w1(e)

            def group(n, u, more):
                xg = xgroup(p, n)
                v.wait_ge(s["init_ready"], n + 1)
                steps.link(nc.vector.tensor_copy(acc[:], ib[:].rearrange("p (a o) -> p a o", a=GB)))
                v.sem_inc(s["init_used"], 1)
                for e in range(NX):
                    k = n * NX + e
                    v.wait_ge(s["y_ready"], k + 3)
                    for j in range(GB):
                        y = yb[e % 2][:, j * 128:(j + 1) * 128]
                        ins = nc.vector.scalar_tensor_tensor(acc[:, j, :], y, rt.G[u][:, j, e:e + 1], acc[:, j, :],
                                                             ALU.mult, ALU.add)
                    ins.then_inc(s["y_used"], 1)
                    v.wait_ge(s["y_used"], k + 3)
                    if e == 1 and more:
                        front.vector(v, n + 1, 1 - u)
                    if e == 3 and more:
                        rt.choose(v, n + 1, steps)
                    if e == 4 and more:
                        split_x(n + 1, 1 - u)
                    if e == 5 and more:
                        rt.weigh(v, n + 1, 1 - u, steps)
                tail.vector(v, n, u, steps, nc.vector.scalar_tensor_tensor(xg, acc[:], p.gate[:, gate:gate + 1], xg,
                                                                           ALU.mult, ALU.add))

            over_groups(v, group, steps, 2 * (tail.STEPS + 2 + rt.VSTEPS))

        @block.scalar
        def _(a):
            credit(a, (front.xnT_ready, 1), (s["h_ready"], 2))
            a.sem_inc(rt.GT_ready, 1)
            front.scalar(a, 0, 0)
            rt.scalar_exp(a, 0)
            rt.scalar_turn(a, 0, 0)
            a.wait_ge(s["w_in"], 32)

            def group(n, u, more):
                for e in range(NX):
                    for c in range(FC):
                        k = n * NH + e * FC + c
                        if c == 0:
                            a.wait_ge(s["y_ready"], n * NX + e + 1)
                        a.wait_ge(s["h_ps"], k + 1)
                        nc.scalar.activation(hT[(e % 2) * FC + c][:], hb[c % 2][:], ACT.Gelu,
                                             bias=b1[:, e, c:c + 1]).then_inc(s["h_ready"], 1)
                    if e == 2 and more:
                        front.scalar(a, n + 1, 1 - u)
                    if e == 4 and more:
                        rt.scalar_exp(a, n + 1)
                    if e == NX - 1 and more:
                        rt.scalar_turn(a, n + 1, 1 - u)

            over_groups(a, group)

        @block.tensor
        def _(t):
            credit(t, (front.xn_used, 2), (front.xnT_used, 2), (s["y_ready"], 2))
            front.tensor(t, 0, 0)
            t.wait_ge(front.xnT_ready, 2)
            rt_in = rt.in_
            t.wait_ge(rt_in, 32)
            rt.tensor(t, 0, front.xnT[0])
            rt.tensor_turn(t, 0, 0)
            t.wait_ge(s["blk_in"], 64)
            t.wait_ge(s["w_in"], 32)

            def second(n, e, j):
                k = n * NX + e
                if j == 0:
                    t.wait_ge(s["h_ready"], k * FC + FC + 2)
                    t.wait_ge(s["y_used"], k + 1)
                for c in range(FC):
                    ins = nc.tensor.matmul(yb[e % 2][:, j * 128:(j + 1) * 128],
                                           hT[(e % 2) * FC + c][:, j * 128:(j + 1) * 128], w2[:, e, c, :],
                                           start=(c == 0), stop=(c == FC - 1))
                if j == GB - 1:
                    ins.then_inc(s["y_ready"], 1)

            def group(n, u, first, more):
                t.wait_ge(front.xnT_ready, n + 2)
                t.wait_ge(s["x_split"], n + 1)
                t.wait_ge(rt.GT_ready, n + 2)
                t.wait_ge(s["init_used"], n + 1)
                nc.tensor.matmul(ib[:], rt.GT[u][0:GB * NX, :], blk[:], start=True, stop=True).then_inc(s["init_ready"], 1)
                for e in range(NX):
                    if first:
                        t.wait_ge(s["w1_split"], e + 1)
                    if first and e == 3:
                        t.wait_ge(s["w2_in1"], 16)
                    for c in range(FC):
                        k = n * NH + e * FC + c
                        t.wait_ge(s["h_ready"], k + 1)
                        fs = slice(c * 128, (c + 1) * 128)
                        nc.tensor.matmul(hb[c % 2][:], w1hi[:, e, fs], xhi[u][:], start=True, stop=False)
                        nc.tensor.matmul(hb[c % 2][:], w1hi[:, e, fs], xlo[u][:], start=False, stop=False)
                        nc.tensor.matmul(hb[c % 2][:], w1lo[:, e, fs], xhi[u][:], start=False, stop=True)\
                            .then_inc(s["h_ps"], 1)
                        if e:
                            second(n, e - 1, c)
                        elif not first:
                            second(n - 1, NX - 1, c)
                    if e == 2 and more:
                        front.tensor(t, n + 1, 1 - u)
                    if e == 3 and more:
                        t.wait_ge(front.xnT_ready, n + 3)
                        rt.tensor(t, n + 1, front.xnT[1 - u])
                    if e == NX - 1 and more:
                        rt.tensor_turn(t, n + 1, 1 - u)
                t.wait_ge(s["h_ps"], (n + 1) * NH)
                t.sem_inc(front.xnT_used, 1)
                t.sem_inc(front.xn_used, 1)

            over_groups_skewed(t, group)
            for j in range(GB):
                second(NG - 1, NX - 1, j)


def stage_out(nc, p, out):
    with Stage(nc, "O") as st:
        stored = st.sem("stored")
        block = st.block()

        @block.sync
        def _(sp):
            sp.dma_start(out, p.X[:]).then_inc(stored, 16)
            sp.wait_ge(stored, 16)


class P:
    pass


def build(nc, d, out, layers=range(1, 9)):
    ctx = ExitStack()
    with ctx:
        p = P()

        def sb(name, shape, dt=F32, at=ctx):
            return at.enter_context(nc.sbuf_tensor(name, shape, dt))

        p.X = sb("X", [128, B, D])
        p.mean, p.rstd, p.mhalf = sb("mean", [128, B]), sb("rstd", [128, B]), sb("mhalf", [128, B])
        p.gate, p.ident = sb("gate", [128, 8]), sb("ident", [128, 128])
        p.ident16 = sb("ident16", [128, 128], BF16)
        with ExitStack() as l0:
            p.ones16 = sb("ones16", [128, 128], BF16, l0)
            p.bias3 = [sb(f"bias3_{i}", [128, NE_L0], BF16, l0) for i in range(2)]
            p.phiT = [sb(f"phiT{i}", [128, NE_L0], F32, l0) for i in range(2)]
            p.ew = sb("ew", [128, NL, 128], F32, l0)
            stage_a(nc, p, d)
            if 2 in layers:
                XtT, Yt = sb("XtT", [128, NE_L0], F32, l0), sb("Yt", [128, NE_L0 // 128, 128], F32, l0)
                stage_b1(nc, p, d, XtT)
                stage_mid(nc, p, d, XtT, Yt)
                stage_b2(nc, p, d, Yt)
        p.KS = [sb(f"KS{u}", [3 * HW, NHG, NHG, GD], F32R) for u in range(2)]
        if 3 in layers:
            stage_attn(nc, p, d, "L1", 1, True, True)
        if 4 in layers:
            stage_l1_ffn(nc, p, d)
        if 5 in layers:
            stage_l2_attn(nc, p, d)
        if 6 in layers:
            stage_l2_ffn(nc, p, d, 6)
        if 7 in layers:
            stage_attn(nc, p, d, "L3", 3, False, 3 not in layers)
        if 8 in layers:
            stage_l3_ffn(nc, p, d, "F3", 7)
        stage_out(nc, p, out)


def attn_layouts(name, n, c, w, rope):
    wt = lambda k: n(w[f"{name}_xattn_W{k}"])
    bt = lambda k: n(w[f"{name}_xattn_b{k}"])
    rot = np.arange(D).reshape(H, 2, HD // 2)[:, ::-1].reshape(D)
    return {f"{name}_W": c(np.stack([wt(k).T for k in "qkvo"] + ([wt(k)[rot].T for k in "qk"] if rope else []), axis=1)),
            f"{name}_b": c(np.stack([bt(k) for k in "qkv"] + ([bt(k)[rot] for k in "qk"] if rope else []), axis=1)),
            f"{name}_bo": c(bt("o").reshape(1, D))}


def rope_tables():
    half = HD // 2
    inv = (1.0 / 10000.0 ** (np.arange(half, dtype=np.float32) / half)).astype(np.float32)
    ang = np.arange(S, dtype=np.float32)[None, :] * inv[:, None]
    cos, sin = np.cos(ang).astype(np.float32), np.sin(ang).astype(np.float32)
    cos = np.tile(np.concatenate([cos, cos]), (H, 1))
    sin = np.tile(np.concatenate([-sin, sin]), (H, 1))
    sc = np.float32(HD ** -0.5)
    return {"rope": np.ascontiguousarray(np.stack([cos * sc, sin * sc, cos, sin], axis=1))}


def layouts(x, itok_S_0_31, ctx_1024, mask_1x1xSxS2_ik0, g_xattn, g_ffn, **w):
    c = np.ascontiguousarray
    n = lambda a: np.asarray(a)
    return {
        "x": c(n(x).transpose(1, 0, 2)),
        "itok": c(n(itok_S_0_31).reshape(1, S)),
        "ctxT_rows": c(n(ctx_1024).transpose(0, 2, 1)),
        "g_xattn": c(n(g_xattn)), "g_ffn": c(n(g_ffn)),
        "phiT": c(n(w["L0_ffn_phi_w"]).T), "phi_b": c(n(w["L0_ffn_phi_b"]).reshape(1, -1)),
        "phiT_slots": c(n(w["L0_ffn_phi_w"]).reshape(NL, NP, D).transpose(2, 1, 0).reshape(D, -1)),
        "phi_b_slots": c(n(w["L0_ffn_phi_b"]).reshape(NL, NP).T.reshape(1, -1)),
        "expert_w": c(n(w["L0_ffn_expert_w"]).transpose(1, 0, 2)), "expert_b": c(n(w["L0_ffn_expert_b"])),
        "sel_expert": np.repeat(np.eye(NL, dtype=np.float32), NP, axis=1),
        "ident": np.eye(128, dtype=np.float32),
        "ctxT": c(n(ctx_1024).transpose(2, 0, 1)), "ctx": c(n(ctx_1024).transpose(1, 0, 2)),
        "L1_mask": np.tril(np.ones((S, S), np.int32)), "L3_mask": c(n(mask_1x1xSxS2_ik0).reshape(S, S)),
        "L1F_rW": c(n(w["L1_ffn_centroids"]).T), "L1F_rb": c(n(w["L1_ffn_expert_biases"]).reshape(1, NR)),
        "L1F_WrT": c(n(w["L1_ffn_Wr"]).transpose(2, 0, 1)), "L1F_br": c(n(w["L1_ffn_br"])),
        "L1F_WsT": c(n(w["L1_ffn_Ws"]).transpose(2, 0, 1)), "L1F_bs": c(n(w["L1_ffn_bs"]).reshape(1, 2, D)),
        "L2_gate_w": c(n(w["L2_ffn_gate_w"])),
        "upper": np.triu(np.ones((S, S), np.float32)),
        "iota": np.tile(np.arange(1, CAP + 1, dtype=np.float32), 2 * NX).reshape(1, 2 * NX * CAP),
        "F2_w1": c(n(w["L2_ffn_w1"]).transpose(1, 0, 2)),
        "F2_w2": c(n(w["L2_ffn_w2"]).reshape(NX, FC, 128, D).transpose(2, 0, 1, 3)),
        "F3_rW": c(n(w["L3_ffn_gate_w"])), "F3_rb": c(n(w["L3_ffn_gate_b"]).reshape(1, NX)),
        "F3_w1": c(n(w["L3_ffn_w1"]).transpose(1, 0, 2)),
        "F3_w2": c(n(w["L3_ffn_w2"]).reshape(NX, FC, 128, D).transpose(2, 0, 1, 3)),
        "F3_b1": c(n(w["L3_ffn_b1"]).reshape(NX, FC, 128).transpose(2, 0, 1)), "F3_b2": c(n(w["L3_ffn_b2"])),
        **rope_tables(), **attn_layouts("L1", n, c, w, True), **attn_layouts("L3", n, c, w, False),
    }


def kernel(**inputs):
    import concourse.bacc as _bacc
    from concourse.bass_utils import run_bass_kernel_spmd as _run

    nc = _bacc.Bacc("TRN2", target_bir_lowering=False, num_devices=1)
    arrays = layouts(**inputs)
    d = {k: nc.dram_tensor(f"in_{k}", a.shape, mybir.dt.from_np(a.dtype), kind="ExternalInput").ap()
         for k, a in arrays.items()}
    out = nc.dram_tensor("out_x", (S, B, D), F32, kind="ExternalOutput").ap()
    build(nc, d, out)
    r = _run(nc, [{f"in_{k}": a for k, a in arrays.items()}], core_ids=[0])
    return r.results[0]["out_x"].transpose(1, 0, 2)
```
